# Optimizing a Trainium2 kernel written in Bass

```python
import numpy as np
import jax
import jax.numpy as jnp

def _softmax(x, axis=-1):
    return jax.nn.softmax(x, axis=axis)

def _gelu(x):
    return jax.nn.gelu(x, approximate=True)

def _silu(x):
    return jax.nn.silu(x)

def _sigmoid(x):
    return jax.nn.sigmoid(x)

def _layernorm(x, axis=-1, eps=1e-05):
    m = jnp.mean(x, axis=axis, keepdims=True)
    v = jnp.var(x, axis=axis, keepdims=True)
    return (x - m) / jnp.sqrt(v + eps)

def _scatter_add(tgt, idx, src, axis=0):
    return tgt.at[idx].add(src)

def _segment_sum(src, seg, n):
    return jax.ops.segment_sum(src, seg, n)
kernel_name = 'mk_pixart_seq_d1_seqx_r2_87c654'

def setup_inputs(seed: int=0):
    np.random.seed(seed)
    _w = jnp.asarray

    def _rec_inputs():
        import jax
        import jax.numpy as jnp
        _rk = jax.random.key(seed)
        x = -0.0002928 + 1 * jax.random.normal(jax.random.fold_in(_rk, 1), (16, 224, 512), jnp.float32)
        _lenS = 224 - jax.random.randint(jax.random.fold_in(_rk, 7), (16,), 0, max(1, 224 // 4) + 1, jnp.int32)
        _lenS2 = 750 - jax.random.randint(jax.random.fold_in(_rk, 8), (16,), 0, max(1, 750 // 4) + 1, jnp.int32)
        cond_1024 = 0.0061147 + 1.02565 * jax.random.normal(jax.random.fold_in(_rk, 11), (16, 512), jnp.float32)
        _ctx_1024P = jax.random.normal(jax.random.fold_in(_rk, 12), (16, 16, 512), jnp.float32)
        _ctx_1024c = jax.random.dirichlet(jax.random.fold_in(_rk, 512), 0.3 * jnp.ones((16,), jnp.float32), (16, 750))
        _ctx_1024t = jnp.einsum('bsk,bkd->bsd', _ctx_1024c, _ctx_1024P)
        _ctx_1024t = _ctx_1024t * jax.lax.rsqrt(jnp.mean(jnp.square(_ctx_1024t)) + 1e-12) * 0.953939
        ctx_1024 = -0.00265004 + 0.998804 * (_ctx_1024t + 0.3 * jax.random.normal(jax.random.fold_in(_rk, 612), (16, 750, 512), jnp.float32))
        return (x, cond_1024, ctx_1024)
    x, cond_1024, ctx_1024 = _rec_inputs()

    def _L0_xcond_setup():
        import jax, jax.numpy as jnp
        import numpy as np
        LN_EPS = 1e-06

        def _ln(x):
            mu = jnp.mean(x, axis=-1, keepdims=True)
            var = jnp.var(x, axis=-1, keepdims=True)
            return (x - mu) * jax.lax.rsqrt(var + LN_EPS)
        key = jax.random.key(seed)
        H, NH = (512, 16)
        B, N, S = (4, 512, 77)
        MLP = int(H * 4.0)
        ks = jax.random.split(key, 20)
        s = 1.0 / np.sqrt(H)
        return {'x': jax.random.normal(ks[0], (B, N, H), jnp.float32), 'c': jax.random.normal(ks[1], (B, H), jnp.float32), 'context': jax.random.normal(ks[2], (B, S, H), jnp.float32), 'W_mod': jax.random.normal(ks[3], (H, 6 * H), jnp.float32) * s, 'b_mod': jnp.zeros((6 * H,), jnp.float32), 'W_qkv': jax.random.normal(ks[4], (H, 3 * H), jnp.float32) * s, 'b_qkv': jnp.zeros((3 * H,), jnp.float32), 'W_proj': jax.random.normal(ks[5], (H, H), jnp.float32) * s, 'b_proj': jnp.zeros((H,), jnp.float32), 'W_qc': jax.random.normal(ks[6], (H, H), jnp.float32) * s, 'b_qc': jnp.zeros((H,), jnp.float32), 'W_kvc': jax.random.normal(ks[7], (H, 2 * H), jnp.float32) * s, 'b_kvc': jnp.zeros((2 * H,), jnp.float32), 'W_cproj': jax.random.normal(ks[8], (H, H), jnp.float32) * s, 'b_cproj': jnp.zeros((H,), jnp.float32), 'W_mlp1': jax.random.normal(ks[9], (H, MLP), jnp.float32) * s, 'b_mlp1': jnp.zeros((MLP,), jnp.float32), 'W_mlp2': jax.random.normal(ks[10], (MLP, H), jnp.float32) * (1.0 / np.sqrt(MLP)), 'b_mlp2': jnp.zeros((H,), jnp.float32)}
    _L0_xcond_all = _L0_xcond_setup()
    _L0_xcond_in = {k: v for k, v in _L0_xcond_all.items() if k in ('W_mod', 'b_mod', 'W_qkv', 'b_qkv', 'W_proj', 'b_proj', 'W_qc', 'b_qc', 'W_kvc', 'b_kvc', 'W_cproj', 'b_cproj', 'W_mlp1', 'b_mlp1', 'W_mlp2', 'b_mlp2')}
    del _L0_xcond_all
    return {'x': x, 'cond_1024': cond_1024, 'ctx_1024': ctx_1024, 'L0_xcond_W_mod': _L0_xcond_in['W_mod'], 'L0_xcond_b_mod': _L0_xcond_in['b_mod'], 'L0_xcond_W_qkv': _L0_xcond_in['W_qkv'], 'L0_xcond_b_qkv': _L0_xcond_in['b_qkv'], 'L0_xcond_W_proj': _L0_xcond_in['W_proj'], 'L0_xcond_b_proj': _L0_xcond_in['b_proj'], 'L0_xcond_W_qc': _L0_xcond_in['W_qc'], 'L0_xcond_b_qc': _L0_xcond_in['b_qc'], 'L0_xcond_W_kvc': _L0_xcond_in['W_kvc'], 'L0_xcond_b_kvc': _L0_xcond_in['b_kvc'], 'L0_xcond_W_cproj': _L0_xcond_in['W_cproj'], 'L0_xcond_b_cproj': _L0_xcond_in['b_cproj'], 'L0_xcond_W_mlp1': _L0_xcond_in['W_mlp1'], 'L0_xcond_b_mlp1': _L0_xcond_in['b_mlp1'], 'L0_xcond_W_mlp2': _L0_xcond_in['W_mlp2'], 'L0_xcond_b_mlp2': _L0_xcond_in['b_mlp2']}

def reference(x, cond_1024, ctx_1024, L0_xcond_W_mod, L0_xcond_b_mod, L0_xcond_W_qkv, L0_xcond_b_qkv, L0_xcond_W_proj, L0_xcond_b_proj, L0_xcond_W_qc, L0_xcond_b_qc, L0_xcond_W_kvc, L0_xcond_b_kvc, L0_xcond_W_cproj, L0_xcond_b_cproj, L0_xcond_W_mlp1, L0_xcond_b_mlp1, L0_xcond_W_mlp2, L0_xcond_b_mlp2):
    import jax
    import jax.numpy as jnp

    def _L0_xcond_ref(x, c, context, W_mod, b_mod, W_qkv, b_qkv, W_proj, b_proj, W_qc, b_qc, W_kvc, b_kvc, W_cproj, b_cproj, W_mlp1, b_mlp1, W_mlp2, b_mlp2):
        import jax, jax.numpy as jnp
        import numpy as np
        LN_EPS = 1e-06

        def _ln(x):
            mu = jnp.mean(x, axis=-1, keepdims=True)
            var = jnp.var(x, axis=-1, keepdims=True)
            return (x - mu) * jax.lax.rsqrt(var + LN_EPS)
        B, N, H = x.shape
        NH = 16
        hd = H // NH
        scale = hd ** (-0.5)
        c_proj = jax.nn.silu(c) @ W_mod + b_mod
        shift_a, scale_a, gate_a, shift_m, scale_m, gate_m = jnp.split(c_proj, 6, axis=-1)

        def modulate(t, shift, sc):
            return t * (1 + sc[:, None]) + shift[:, None]
        x_norm = modulate(_ln(x), shift_a, scale_a)
        qkv = x_norm @ W_qkv + b_qkv
        q, k, v = jnp.split(qkv, 3, axis=-1)
        q = q.reshape(B, N, NH, hd).transpose(0, 2, 1, 3)
        k = k.reshape(B, N, NH, hd).transpose(0, 2, 1, 3)
        v = v.reshape(B, N, NH, hd).transpose(0, 2, 1, 3)
        attn_w = jax.nn.softmax(jnp.einsum('bhqd,bhkd->bhqk', q, k) * scale, axis=-1)
        attn_out = jnp.einsum('bhqk,bhkd->bhqd', attn_w, v)
        attn_out = attn_out.transpose(0, 2, 1, 3).reshape(B, N, H)
        attn_out = attn_out @ W_proj + b_proj
        x = x + gate_a[:, None] * attn_out
        S = context.shape[1]
        q_c = _ln(x) @ W_qc + b_qc
        kv_c = _ln(context) @ W_kvc + b_kvc
        k_c, v_c = jnp.split(kv_c, 2, axis=-1)
        q_c = q_c.reshape(B, N, NH, hd).transpose(0, 2, 1, 3)
        k_c = k_c.reshape(B, S, NH, hd).transpose(0, 2, 1, 3)
        v_c = v_c.reshape(B, S, NH, hd).transpose(0, 2, 1, 3)
        c_attn_w = jax.nn.softmax(jnp.einsum('bhqd,bhsd->bhqs', q_c, k_c) * scale, axis=-1)
        c_attn_out = jnp.einsum('bhqs,bhsd->bhqd', c_attn_w, v_c)
        c_attn_out = c_attn_out.transpose(0, 2, 1, 3).reshape(B, N, H)
        c_attn_out = c_attn_out @ W_cproj + b_cproj
        x = x + c_attn_out
        x_norm2 = modulate(_ln(x), shift_m, scale_m)
        h = jax.nn.gelu(x_norm2 @ W_mlp1 + b_mlp1)
        h = h @ W_mlp2 + b_mlp2
        x = x + gate_m[:, None] * h
        return x
    x = _L0_xcond_ref(x, cond_1024, ctx_1024, L0_xcond_W_mod, L0_xcond_b_mod, L0_xcond_W_qkv, L0_xcond_b_qkv, L0_xcond_W_proj, L0_xcond_b_proj, L0_xcond_W_qc, L0_xcond_b_qc, L0_xcond_W_kvc, L0_xcond_b_kvc, L0_xcond_W_cproj, L0_xcond_b_cproj, L0_xcond_W_mlp1, L0_xcond_b_mlp1, L0_xcond_W_mlp2, L0_xcond_b_mlp2)
    return x

_drawn_inputs = setup_inputs


def setup_inputs(seed=0):
    import zlib

    import numpy as np

    out = dict(_drawn_inputs(seed))
    spreads = {'L0_xcond_b_mod': (0.0, 0.1),
     'L0_xcond_b_qkv': (0.0, 0.1),
     'L0_xcond_b_proj': (0.0, 0.1),
     'L0_xcond_b_qc': (0.0, 0.571),
     'L0_xcond_b_kvc': (0.0, 0.1),
     'L0_xcond_b_cproj': (0.0, 0.1),
     'L0_xcond_b_mlp1': (0.0, 0.1),
     'L0_xcond_b_mlp2': (0.0, 0.1)}
    factors = {}
    for name, (base, spread) in spreads.items():
        noise = np.random.default_rng([zlib.crc32(name.encode()), seed]).standard_normal(out[name].shape)
        drawn = base * np.exp(spread * noise) if base else spread * noise
        out[name] = jnp.asarray(drawn.astype(out[name].dtype))
    for name, factor in factors.items():
        out[name] = (out[name] * factor).astype(out[name].dtype)
    return out
```

```python
from contextlib import ExitStack

import concourse.bass as bass
from concourse import mybir

ALU = mybir.AluOpType
ACT = mybir.ActivationFunctionType
F32 = mybir.dt.float32
F32R = mybir.dt.float32r
AX_X = mybir.AxisListType.X

P = 128
B, N, H = 16, 224, 512
S = 750
NH, HD = 16, 32
MLP = 4 * H
KC = H // P
HPG = P // HD
QT, QN = 2, N // 2
ST, SN = 6, S // 6
SHALF = (376, S - 376)
TERMS = 3
SCALE = float(HD) ** -0.5
EPS = 1e-6
SHIFT_A, SCALE_A, GATE_A, SHIFT_M, SCALE_M, GATE_M = range(6)


class Batch:

    def __init__(self, c, i=0):
        self.c, self.i = c, i
        self.par = c % 2

    def plus(self, d):
        return Batch(self.c + d, self.i)

    def index(self):
        return self.i * 2 + self.c

    def n(self, per, k):
        return self.i * (2 * per) + (self.c * per + k)

    def pair(self, per, k=0):
        return self.i * per + ((self.c // 2) * per + k)


def wait(eng, sem, value):
    if not (isinstance(value, int) and value <= 0):
        eng.wait_ge(sem, value)


def product(pe, out, lhs, rhs, first, last):
    pe.matmul(out, lhs[0], rhs[1], start=first, stop=False)
    pe.matmul(out, lhs[1], rhs[0], start=False, stop=False)
    return pe.matmul(out, lhs[0], rhs[0], start=False, stop=last)


def alloc(nc, ctx, phase):
    def sb(name, shape, dt=F32):
        return ctx.enter_context(nc.sbuf_tensor(f"{phase}_{name}", shape, dt))

    def ps(name, shape=(P, 512)):
        return ctx.enter_context(nc.psum_tensor(f"{phase}_{name}", list(shape), F32))

    sems = []

    def sem(name):
        sems.append(nc.alloc_semaphore(f"{phase}_{name}"))
        return sems[-1]

    def clear():
        nc.clear_and_free_semaphores(sems)
        nc.all_engine_barrier()

    ctx.callback(clear)

    return sb, ps, sem


def constants_phase(nc, ident, select, neg_half, eps):
    with ExitStack() as ctx:
        sb, ps, sem = alloc(nc, ctx, "constants")
        filled, shaped = sem("filled"), sem("shaped")
        block = ctx.enter_context(nc.Block())

        @block.gpsimd
        def _(pool):
            pool.memset(ident[:], 0.0)
            pool.memset(select[:], 1.0)
            pool.memset(neg_half[:], -0.5)
            pool.memset(eps[:], EPS).then_inc(filled, 1)
            pool.wait_ge(filled, 1)
            pool.affine_select(out=ident[:], in_=ident[:], compare_op=ALU.not_equal, fill=1.0, base=0,
                               pattern=[[-1, P]], channel_multiplier=1)
            pool.affine_select(out=select[:], in_=select[:], compare_op=ALU.is_ge, fill=0.0, base=0,
                               pattern=[[1, P]], channel_multiplier=-HD).then_inc(shaped, 1)
            pool.wait_ge(shaped, 1)
            pool.affine_select(out=select[:], in_=select[:], compare_op=ALU.is_ge, fill=0.0, base=HD - 1,
                               pattern=[[-1, P]], channel_multiplier=HD).then_inc(shaped, 1)
            pool.wait_ge(shaped, 2)


def condition_phase(nc, cond_t, w_mod, b_mod, gates, mod_t, ident):
    NM = 6 * H
    with ExitStack() as ctx:
        sb, ps, sem = alloc(nc, ctx, "condition")
        c_in = sb("c_in", [P, KC, B])
        c_exp = sb("c_exp", [P, KC, B])
        c_den = sb("c_den", [P, KC, B])
        c_inv = sb("c_inv", [P, KC, B])
        c_silu = sb("c_silu", [P, KC, B])
        wm = sb("wm", [P, 6, KC, H])
        bm = sb("bm", [B, NM])
        rows = sb("rows", [B, NM])
        acc = [ps(f"acc{m}") for m in range(6)]
        cols = ps("cols")
        cond_in, bm_in = sem("cond_in"), sem("bm_in")
        wm_in = [sem(f"wm_in{m}") for m in range(6)]
        exp_done, den_done, inv_done, silu_done = sem("exp_done"), sem("den_done"), sem("inv_done"), sem("silu_done")
        acc_done, rows_done, cols_done, mod_done = sem("acc_done"), sem("rows_done"), sem("cols_done"), sem("mod_done")
        gates_out = sem("gates_out")
        ORDER = [SHIFT_A, SCALE_A, SHIFT_M, SCALE_M, GATE_A, GATE_M]
        block = ctx.enter_context(nc.Block())

        @block.sync
        def _(sp):
            sp.dma_start(c_in[:], cond_t).then_inc(cond_in, 16)
            sp.dma_start(bm[:], b_mod.rearrange("(a n) -> a n", a=1).broadcast_to([B, NM])).then_inc(bm_in, 16)
            for m in ORDER:
                sp.dma_start(wm[:, m], w_mod[:, m * H:(m + 1) * H].rearrange("(k p) n -> p k n", p=P)).then_inc(wm_in[m], 16)
            sp.wait_ge(rows_done, 6)
            for n, m in enumerate((GATE_A, GATE_M)):
                sp.dma_start(gates[n], rows[:, m * H:(m + 1) * H]).then_inc(gates_out, 16)
            sp.wait_ge(gates_out, 32)

        @block.scalar
        def _(act):
            act.wait_ge(cond_in, 16)
            act.activation(c_exp[:], c_in[:], ACT.Exp, scale=-1.0).then_inc(exp_done, 1)

        @block.vector
        def _(dve):
            dve.wait_ge(exp_done, 1)
            dve.tensor_scalar(c_den[:], c_exp[:], 1.0, None, ALU.add).then_inc(den_done, 1)
            dve.wait_ge(den_done, 1)
            dve.reciprocal(c_inv[:], c_den[:]).then_inc(inv_done, 1)
            dve.wait_ge(inv_done, 1)
            dve.tensor_tensor(c_silu[:], c_in[:], c_inv[:], ALU.mult).then_inc(silu_done, 1)
            dve.wait_ge(bm_in, 16)
            for n, m in enumerate(ORDER):
                dve.wait_ge(acc_done, n + 1)
                at = slice(m * H, (m + 1) * H)
                one = 1.0 if m in (SCALE_A, SCALE_M) else 0.0
                dve.scalar_tensor_tensor(out=rows[:, at], in0=acc[m][0:B, :], scalar=one, in1=bm[:, at],
                                         op0=ALU.add, op1=ALU.add).then_inc(rows_done, 1)
            dve.wait_ge(cols_done, 1)
            dve.tensor_copy(mod_t[:], cols[:, 0:4 * KC * B].rearrange("p (m b) -> p m b", b=B)).then_inc(mod_done, 1)
            dve.wait_ge(mod_done, 1)

        @block.tensor
        def _(pe):
            pe.wait_ge(silu_done, 1)
            for m in ORDER:
                pe.wait_ge(wm_in[m], 16)
                for k in range(KC):
                    last = pe.matmul(acc[m][0:B, :], c_silu[:, k], wm[:, m, k], start=k == 0, stop=k == KC - 1)
                last.then_inc(acc_done, 1)
            pe.wait_ge(rows_done, 4)
            for n, m in enumerate((SHIFT_A, SCALE_A, SHIFT_M, SCALE_M)):
                for k in range(KC):
                    at = (n * KC + k) * B
                    last = pe.transpose(cols[:, at:at + B], rows[:, m * H + k * P:m * H + (k + 1) * P], ident[0:B, 0:B])
            last.then_inc(cols_done, 1)


def split_weights(nc, phase, parts):
    RING = 4
    with ExitStack() as ctx:
        sb, ps, sem = alloc(nc, ctx, f"{phase}_split")
        stage = [sb(f"stage{s}", [P, MLP]) for s in range(RING)]
        w_in = [sem(f"w_in{s}") for s in range(RING)]
        high_done, low_done = sem("high_done"), sem("low_done")
        items = [(w, hi, lo, k, c, f) for w, hi, lo, f in parts for k in range(w.shape[0] // P)
                 for c in range(0, w.shape[1], MLP)]
        block = ctx.enter_context(nc.Block())

        def views(item, s):
            w, hi, lo, k, c, f = item
            n = min(MLP, w.shape[1] - c)
            return w[k * P:(k + 1) * P, c:c + n], hi[:, k, c:c + n], lo[:, k, c:c + n], stage[s][:, 0:n], f

        @block.sync
        def _(sp):
            for t, item in enumerate(items):
                src, _, _, st, _ = views(item, t % RING)
                wait(sp, low_done, t - RING + 1)
                sp.dma_start(st, src).then_inc(w_in[t % RING], 16)

        @block.scalar
        def _(act):
            for t, item in enumerate(items):
                _, hi, _, st, f = views(item, t % RING)
                act.wait_ge(w_in[t % RING], 16 * (t // RING + 1))
                act.activation(hi, st, ACT.Identity, scale=f).then_inc(high_done, 1)

        @block.vector
        def _(dve):
            for t, item in enumerate(items):
                _, hi, lo, st, f = views(item, t % RING)
                dve.wait_ge(high_done, t + 1)
                dve.scalar_tensor_tensor(out=lo, in0=st, scalar=f, in1=hi.bitcast(F32), op0=ALU.mult,
                                         op1=ALU.subtract).then_inc(low_done, 1)


def load_columns(nc, phase, pairs):
    with ExitStack() as ctx:
        sb, ps, sem = alloc(nc, ctx, f"{phase}_columns")
        small_in = sem("small_in")
        block = ctx.enter_context(nc.Block())

        @block.sync
        def _(sp):
            for dst, src in pairs:
                sp.dma_start(dst, src).then_inc(small_in, 16)
            sp.wait_ge(small_in, 16 * len(pairs))


def self_phase(nc, x, w_qkv, b_qkv_t, w_proj, b_proj, w_qc, b_qc_t, gates, x1, qc, mod_t, ident, select, neg_half, eps):
    with ExitStack() as ctx:
        sb, ps, sem = alloc(nc, ctx, "self")
        wqkv = [sb(f"wqkv_{s}", [P, KC, 3 * H], F32R) for s in "hl"]
        wproj = [sb(f"wproj_{s}", [P, KC, H], F32R) for s in "hl"]
        wqc = [sb(f"wqc_{s}", [P, KC, H], F32R) for s in "hl"]
        bqkv = sb("bqkv", [P, 3 * KC])
        bqc = sb("bqc", [P, KC])
        bproj = sb("bproj", [QN, H])
        load_columns(nc, "self", [(bqkv[:], b_qkv_t), (bqc[:], b_qc_t), (bproj[:], b_proj.rearrange("(a n) -> a n", a=1).broadcast_to([QN, H]))])
        split_weights(nc, "self", [(w_qkv[:, 0:H], wqkv[0][:, :, 0:H], wqkv[1][:, :, 0:H], SCALE),
                           (w_qkv[:, H:3 * H], wqkv[0][:, :, H:3 * H], wqkv[1][:, :, H:3 * H], 1.0),
                           (w_proj, wproj[0], wproj[1], 1.0), (w_qc, wqc[0], wqc[1], SCALE)])
        x_in = sb("x_in", [QN, QT, H])
        x_res = sb("x_res", [QN, QT, H])
        y = sb("y", [QN, QT, H])
        gate = sb("gate", [QN, H])
        xv = sb("xv", [P, KC, N])
        xT = [sb(f"xT_{s}", [P, KC, N], F32R) for s in "hl"]
        yT = [sb(f"yT_{s}", [P, KC, N], F32R) for s in "hl"]
        nat = [sb(f"nat_{s}", [P, KC, N], F32R) for s in "hl"]
        kst = sb("kst", [TERMS * HD, 2, HPG, KC, N], F32R)
        qst = sb("qst", [TERMS * HD, 2, HPG, KC, N], F32R)
        vt = sb("vt", [QN, 2, QT, H])
        pr = sb("pr", [QN, 2, QT, N])
        prT = sb("prT", [QN, HPG, QT, N])
        ou = sb("ou", [P, KC, N])
        nmax = sb("nmax", [QN, 2, QT])
        rsum = sb("rsum", [QN, 2, HPG, QT])
        rinv = sb("rinv", [QN, HPG, QT])
        rT = sb("rT", [HPG, N])
        rb = sb("rb", [P, N])
        bqs, bqcs = sb("bqs", [P, KC]), sb("bqcs", [P, KC])
        st1, st2 = sb("st1", [QN, QT, 6]), sb("st2", [QN, QT, 6])
        turn = sb("turn", [1, 1])
        mv1, mv2 = sb("mv1", [QN, QT, 2]), sb("mv2", [QN, QT, 2])
        ve1, ve2 = sb("ve1", [QN, QT]), sb("ve2", [QN, QT])
        rs1, rs2 = sb("rs1", [QN, QT]), sb("rs2", [QN, QT])
        nm1, nm2 = sb("nm1", [QN, QT]), sb("nm2", [QN, QT])

        sc_ps = [ps(f"sc_ps{i}") for i in range(2)]
        tr_ps = [ps(f"tr_ps{i}") for i in range(2)]
        pj_ps = [ps(f"pj_ps{i}") for i in range(2)]
        o_ps, r_ps = ps("o_ps"), ps("r_ps")

        x_loaded, res_loaded, gate_loaded = sem("x_loaded"), sem("res_loaded"), sem("gate_loaded")
        stats1, mvs1, vareps1, rstd1, nmr1, xhat1 = (sem(s) for s in ("stats1", "mvs1", "vareps1", "rstd1", "nmr1", "xhat1"))
        stats2, mvs2, vareps2, rstd2, nmr2, xhat2 = (sem(s) for s in ("stats2", "mvs2", "vareps2", "rstd2", "nmr2", "xhat2"))
        xT_ps, xT_v, xT_h, xT_l = sem("xT_ps"), sem("xT_v"), sem("xT_h"), sem("xT_l")
        k_ps, k_h, k_l = sem("k_ps"), sem("k_h"), sem("k_l")
        q_ps, q_h, q_l = sem("q_ps"), sem("q_h"), sem("q_l")
        c_ps, c_h, c_l = sem("c_ps"), sem("c_h"), sem("c_l")
        v_ps, v_done = sem("v_ps"), sem("v_done")
        k_stacked = [sem(f"k_stacked{p}") for p in range(2)]
        q_stacked = [sem(f"q_stacked{p}") for p in range(2)]
        scored, maxed, exped, pT_ps, pT_done = (sem(s) for s in ("scored", "maxed", "exped", "pT_ps", "pT_done"))
        pv_done, inverted, rT_ps, rT_done, rb_ps, rb_done, o_done = (sem(s) for s in ("pv_done", "inverted", "rT_ps", "rT_done", "rb_ps", "rb_done", "o_done"))
        oT_h, oT_l = sem("oT_h"), sem("oT_l")
        proj_ps, proj_done, gated, summed, x1_out = (sem(s) for s in ("proj_ps", "proj_done", "gated", "summed", "x1_out"))
        yT_ps, yT_h, yT_l = sem("yT_ps"), sem("yT_h"), sem("yT_l")
        qc_out = sem("qc_out")
        bias_scaled = sem("bias_scaled")
        STACK = 16 * HPG * TERMS
        block = ctx.enter_context(nc.Block())

        def bodies(eng, body):
            body(Batch(0), True, True, False)
            body(Batch(1), True, True, True)
            with eng.Fori(0, (B - 4) // 2) as i:
                body(Batch(2, i), True, True, True)
                body(Batch(3, i), True, True, True)
            body(Batch(B - 2), True, True, True)
            body(Batch(B - 1), True, False, True)
            body(Batch(B), False, False, True)

        @block.sync
        def _(sp):
            def load_x(b):
                wait(sp, xT_ps, b.n(2, 0))
                sp.dma_start(x_in[:], x[bass.ds(b.index(), 1)].rearrange("a (t p) n -> p (a t) n", p=QN)).then_inc(x_loaded, 16)

            def stack(b, low_done, dst, sems, users):
                sp.wait_ge(low_done, b.n(2, 2))
                for j in range(HPG):
                    for r in range(TERMS):
                        sp.dma_start(dst[HD * r:HD * r + HD, b.par, j].bitcast(F32),
                                     nat[users[r]][HD * j:HD * j + HD].bitcast(F32)).then_inc(sems[b.par], 16)

            def load_res(b):
                wait(sp, yT_ps, b.n(2, 0))
                sp.dma_start(x_res[:], x[bass.ds(b.index(), 1)].rearrange("a (t p) n -> p (a t) n", p=QN)).then_inc(res_loaded, 16)
                wait(sp, gated, b.n(2, 0))
                sp.dma_start(gate[:], gates[0, bass.ds(b.index(), 1)].broadcast_to([QN, H])).then_inc(gate_loaded, 16)

            def store_x1(b):
                for t in range(QT):
                    sp.wait_ge(summed, b.n(2, t + 1))
                    sp.dma_start(x1[bass.ds(b.index(), 1), t * QN:(t + 1) * QN].rearrange("a p n -> p (a n)"), y[:, t]).then_inc(x1_out, 16)

            def store_qc(b):
                sp.wait_ge(c_l, b.n(2, 2))
                for s in range(2):
                    sp.dma_start(qc[bass.ds(b.index(), 1), s].rearrange("a (g p) n -> p (a g) n", p=P), nat[s][:].bitcast(F32)).then_inc(qc_out, 16)

            def body(b, att, nxt, prv):
                a, z = b.plus(1), b.plus(-1)
                if prv:
                    load_res(z)
                if nxt and not (isinstance(b.i, int) and b.c == B - 2):
                    load_x(b.plus(2))
                if nxt:
                    stack(a, k_l, kst, k_stacked, (0, 1, 0))
                if prv:
                    store_x1(z)
                if nxt:
                    stack(a, q_l, qst, q_stacked, (0, 0, 1))
                if prv:
                    store_qc(z)

            load_x(Batch(0))
            load_x(Batch(1))
            stack(Batch(0), k_l, kst, k_stacked, (0, 1, 0))
            stack(Batch(0), q_l, qst, q_stacked, (0, 0, 1))
            bodies(sp, body)
            sp.wait_ge(x1_out, 32 * B)
            sp.wait_ge(qc_out, 32 * B)

        @block.tensor
        def _(pe):
            def trans_x(b):
                pe.wait_ge(xhat1, b.n(1, 1))
                for c in range(2):
                    for k in range(2):
                        for t in range(QT):
                            at = k * N + t * QN
                            last = pe.transpose(pj_ps[c][:, at:at + QN], x_in[:, t, (2 * c + k) * P:(2 * c + k + 1) * P], ident[0:QN, 0:QN])
                    last.then_inc(xT_ps, 1)

            def channels(c, w, first_chunk, src, done):
                for m in range(2):
                    at = (first_chunk + m) * P
                    for k in range(KC):
                        last = product(pe, pj_ps[c][:, m * N:(m + 1) * N], (w[0][:, k, at:at + P], w[1][:, k, at:at + P]),
                                       (src[0][:, k], src[1][:, k]), k == 0, k == KC - 1)
                last.then_inc(done, 1)

            def tokens(c, t, w, at, src, done):
                for k in range(KC):
                    last = product(pe, pj_ps[c][0:QN, :], tuple(s[:, k, t * QN:(t + 1) * QN] for s in src),
                                   (w[0][:, k, at:at + H], w[1][:, k, at:at + H]), k == 0, k == KC - 1)
                last.then_inc(done, 1)

            def score(b, h):
                if h == 0:
                    pe.wait_ge(k_stacked[b.par], b.pair(STACK, STACK))
                    pe.wait_ge(q_stacked[b.par], b.pair(STACK, STACK))
                wait(pe, exped, b.n(NH, h - 1))
                g, j = h // HPG, h % HPG
                for t in range(QT):
                    last = pe.matmul(sc_ps[h % 2][0:QN, t * N:(t + 1) * N], qst[:, b.par, j, g, t * QN:(t + 1) * QN],
                                     kst[:, b.par, j, g, :], start=True, stop=True)
                last.then_inc(scored, 1)

            def trans_p(b, h):
                pe.wait_ge(exped, b.n(NH, h + 1))
                wait(pe, pT_done, b.n(NH, h - 1))
                for kt in range(QT):
                    for t in range(QT):
                        at = kt * N + t * QN
                        last = pe.transpose(tr_ps[h % 2][0:QN, at:at + QN], pr[:, h % 2, t, kt * QN:(kt + 1) * QN], ident[0:QN, 0:QN])
                last.then_inc(pT_ps, 1)

            def pv(b, g):
                pe.wait_ge(pT_done, b.n(NH, HPG * g + HPG))
                if g == 0:
                    pe.wait_ge(v_done, b.n(2, 2))
                wait(pe, o_done, b.n(KC, g))
                for kt in range(QT):
                    for j in range(HPG):
                        ch = g * P + j * HD
                        last = pe.matmul(o_ps[HD * j:HD * j + HD, 0:N], vt[:, b.par, kt, ch:ch + HD], prT[:, j, kt],
                                         start=kt == 0, stop=kt == QT - 1)
                last.then_inc(pv_done, 1)
                pe.wait_ge(inverted, b.n(KC, g + 1))
                wait(pe, rb_done, b.n(KC, g))
                for t in range(QT):
                    last = pe.transpose(r_ps[0:HPG, t * QN:(t + 1) * QN], rinv[:, :, t], ident[0:QN, 0:QN])
                last.then_inc(rT_ps, 1)

            def spread(b, g):
                pe.wait_ge(rT_done, b.n(KC, g + 1))
                pe.matmul(r_ps[:, 0:N], select[:], rT[:], start=True, stop=True).then_inc(rb_ps, 1)

            def trans_y(b):
                pe.wait_ge(xhat2, b.n(1, 1))
                for c in range(2):
                    for k in range(2):
                        for t in range(QT):
                            at = k * N + t * QN
                            last = pe.transpose(pj_ps[c][:, at:at + QN], x_res[:, t, (2 * c + k) * P:(2 * c + k + 1) * P], ident[0:QN, 0:QN])
                    last.then_inc(yT_ps, 1)

            def body(b, att, nxt, prv):
                a, z = b.plus(1), b.plus(-1)
                for h in range(NH):
                    if att:
                        score(b, h)
                    if h > 0 and att:
                        trans_p(b, h - 1)
                    if h == 0 and prv:
                        trans_p(z, NH - 1)
                        pv(z, KC - 1)
                    if h % HPG == 0 and h > 0 and att:
                        pv(b, h // HPG - 1)
                    if h == 1 and prv:
                        spread(z, KC - 1)
                    if h % HPG == 1 and h > 1 and att:
                        spread(b, h // HPG - 1)
                    if nxt and h == 2:
                        pe.wait_ge(v_done, b.n(2, 2))
                        trans_x(a)
                    if nxt and h in (3, 4):
                        if h == 3:
                            pe.wait_ge(xT_l, a.n(1, 1))
                        channels(h - 3, wqkv, KC + 2 * (h - 3), xT, k_ps)
                    if prv and h in (5, 6):
                        if nxt:
                            pe.wait_ge(k_l, a.n(2, h - 4))
                        else:
                            pe.wait_ge(v_done, 2 * B)
                            pe.wait_ge(c_l, z.n(2, 0))
                        if h == 5:
                            pe.wait_ge(oT_l, z.n(KC, KC))
                        tokens(h - 5, h - 5, wproj, 0, yT, proj_ps)
                    if nxt and h in (8, 9):
                        if prv:
                            pe.wait_ge(proj_done, z.n(2, h - 7))
                        else:
                            pe.wait_ge(k_l, a.n(2, h - 7))
                        channels(h - 8, wqkv, 2 * (h - 8), xT, q_ps)
                    if prv and h == 11:
                        if nxt:
                            pe.wait_ge(q_l, a.n(2, 2))
                        pe.wait_ge(proj_done, z.n(2, 2))
                        trans_y(z)
                    if prv and h in (13, 14):
                        pe.wait_ge(yT_l, z.n(2, 2))
                        channels(h - 13, wqc, 2 * (h - 13), yT, c_ps)
                    if nxt and h == 15:
                        for c in range(2):
                            if prv:
                                pe.wait_ge(c_l, z.n(2, c + 1))
                            else:
                                pe.wait_ge(q_l, a.n(2, c + 1))
                            tokens(c, c, wqkv, 2 * H, xT, v_ps)

            a = Batch(0)
            trans_x(a)
            pe.wait_ge(xT_l, 1)
            for c in range(2):
                channels(c, wqkv, KC + 2 * c, xT, k_ps)
            for c in range(2):
                pe.wait_ge(k_l, c + 1)
                channels(c, wqkv, 2 * c, xT, q_ps)
            for c in range(2):
                pe.wait_ge(q_l, c + 1)
                tokens(c, c, wqkv, 2 * H, xT, v_ps)
            bodies(pe, body)

        @block.vector
        def _(dve):
            def stats(b, src, ready, value, st, mv, s_stats, s_mv):
                for t in range(QT):
                    dve.wait_ge(ready, value(t))
                    last = dve.bn_stats(st[:, t], src[:, t])
                last.then_inc(s_stats, 1)
                dve.wait_ge(s_stats, b.n(1, 1))
                dve.memset(turn[:], 0.0)
                for t in range(QT):
                    last = dve.bn_aggr(mv[:, t], st[:, t])
                last.then_inc(s_mv, 1)

            def neg_mean(b, mv, rs, nm, s_rstd, s_nmr):
                dve.wait_ge(s_rstd, b.n(1, 1))
                dve.scalar_tensor_tensor(out=nm[:], in0=mv[:, :, 0], scalar=-1.0, in1=rs[:], op0=ALU.mult, op1=ALU.mult).then_inc(s_nmr, 1)

            def modulate(b):
                wait(dve, xT_l, b.n(1, 0))
                for c in range(2):
                    dve.wait_ge(xT_ps, b.n(2, c + 1))
                    for k in range(2):
                        m = 2 * c + k
                        last = dve.tensor_scalar(xv[:, m], pj_ps[c][:, k * N:(k + 1) * N], mod_t[:, KC + m, bass.ds(b.index(), 1)],
                                                 mod_t[:, m, bass.ds(b.index(), 1)], ALU.mult, ALU.add)
                last.then_inc(xT_v, 1)

            def lows(b, c, high, low, bias, first_chunk):
                dve.wait_ge(high, b.n(2, c + 1))
                for m in range(2):
                    last = dve.scalar_tensor_tensor(out=nat[1][:, 2 * c + m], in0=pj_ps[c][:, m * N:(m + 1) * N],
                                                    scalar=bias[:, first_chunk + m:first_chunk + m + 1],
                                                    in1=nat[0][:, 2 * c + m].bitcast(F32), op0=ALU.add, op1=ALU.subtract)
                last.then_inc(low, 1)

            def add_bias(b, t):
                dve.wait_ge(proj_ps, b.n(2, t + 1))
                wait(dve, x1_out, b.n(32, 0))
                dve.tensor_tensor(y[:, t], pj_ps[t][0:QN, :], bproj[:], ALU.add).then_inc(proj_done, 1)

            def low_o(b):
                for g in range(KC):
                    dve.wait_ge(oT_h, b.n(KC, g + 1))
                    dve.scalar_tensor_tensor(out=yT[1][:, g], in0=ou[:, g], scalar=bqkv[:, 2 * KC + g:2 * KC + g + 1],
                                             in1=yT[0][:, g].bitcast(F32), op0=ALU.add, op1=ALU.subtract).then_inc(oT_l, 1)

            def low_y(b):
                for c in range(2):
                    dve.wait_ge(yT_h, b.n(2, c + 1))
                    dve.tensor_tensor(yT[1][:, 2 * c:2 * c + 2], pj_ps[c][:, 0:2 * N].rearrange("p (m n) -> p m n", m=2),
                                      yT[0][:, 2 * c:2 * c + 2].bitcast(F32), ALU.subtract).then_inc(yT_l, 1)

            def row_max(b, h):
                dve.wait_ge(scored, b.n(NH, h + 1))
                wait(dve, exped, b.n(NH, h - 1))
                dve.tensor_reduce(nmax[:, h % 2], sc_ps[h % 2][0:QN, 0:QT * N].rearrange("p (t k) -> p t k", t=QT), AX_X, ALU.max,
                                  negate=True).then_inc(maxed, 1)

            def copy_p(b, h):
                dve.wait_ge(pT_ps, b.n(NH, h + 1))
                if h % HPG == 0:
                    wait(dve, pv_done, b.n(KC, h // HPG))
                dve.tensor_copy(prT[:, h % HPG], tr_ps[h % 2][0:QN, 0:QT * N].rearrange("p (k t) -> p k t", k=QT)).then_inc(pT_done, 1)

            def invert(b, g):
                dve.wait_ge(exped, b.n(NH, HPG * g + HPG))
                wait(dve, rT_ps, b.n(KC, g))
                dve.reciprocal(rinv[:], rsum[:, g % 2]).then_inc(inverted, 1)

            def normalize(b, g):
                dve.wait_ge(rb_done, b.n(KC, g + 1))
                dve.wait_ge(pv_done, b.n(KC, g + 1))
                if g == 0:
                    wait(dve, oT_l, b.n(KC, 0))
                dve.tensor_tensor(ou[:, g], o_ps[:, 0:N], rb[:], ALU.mult).then_inc(o_done, 1)

            def body(b, att, nxt, prv):
                a, z = b.plus(1), b.plus(-1)
                for h in range(NH):
                    if att:
                        row_max(b, h)
                    if h > 0 and att:
                        copy_p(b, h - 1)
                    if h == 0 and prv:
                        copy_p(z, NH - 1)
                        invert(z, KC - 1)
                    if h % HPG == 0 and h > 0 and att:
                        invert(b, h // HPG - 1)
                    if h == 2 and prv:
                        normalize(z, KC - 1)
                    if h % HPG == 2 and h > 2 and att:
                        normalize(b, h // HPG - 1)
                    if nxt and h == 0:
                        stats(a, x_in, x_loaded, lambda t: a.n(16, 16), st1, mv1, stats1, mvs1)
                    if nxt and h == 1:
                        neg_mean(a, mv1, rs1, nm1, rstd1, nmr1)
                    if nxt and h == 2:
                        modulate(a)
                    if prv and h == 3:
                        low_o(z)
                    if nxt and h in (4, 5):
                        lows(a, h - 4, k_h, k_l, bqkv, KC + 2 * (h - 4))
                    if prv and h in (6, 7):
                        add_bias(z, h - 6)
                    if nxt and h in (9, 10):
                        lows(a, h - 9, q_h, q_l, bqs, 2 * (h - 9))
                    if prv and h == 9:
                        stats(z, y, summed, lambda t: z.n(2, t + 1), st2, mv2, stats2, mvs2)
                    if prv and h == 10:
                        neg_mean(z, mv2, rs2, nm2, rstd2, nmr2)
                    if prv and h == 12:
                        low_y(z)
                    if prv and h in (14, 15):
                        lows(z, h - 14, c_h, c_l, bqcs, 2 * (h - 14))

            dve.tensor_scalar(bqs[:], bqkv[:, 0:KC], SCALE, None, ALU.mult)
            dve.tensor_scalar(bqcs[:], bqc[:], SCALE, None, ALU.mult).then_inc(bias_scaled, 1)
            dve.wait_ge(bias_scaled, 1)
            a = Batch(0)
            stats(a, x_in, x_loaded, lambda t: 16, st1, mv1, stats1, mvs1)
            neg_mean(a, mv1, rs1, nm1, rstd1, nmr1)
            modulate(a)
            for c in range(2):
                lows(a, c, k_h, k_l, bqkv, KC + 2 * c)
            for c in range(2):
                lows(a, c, q_h, q_l, bqs, 2 * c)
            bodies(dve, body)

        @block.scalar
        def _(act):
            def apply_ln(b, src, dst, rs, nm, s_nmr, s_out):
                act.wait_ge(s_nmr, b.n(1, 1))
                for t in range(QT):
                    last = act.activation(dst[:, t], src[:, t], ACT.Identity, bias=nm[:, t:t + 1], scale=rs[:, t:t + 1])
                last.then_inc(s_out, 1)

            def high_x(b):
                act.wait_ge(xT_v, b.n(1, 1))
                wait(act, v_ps, b.n(2, 0))
                act.copy(xT[0][:], xv[:]).then_inc(xT_h, 1)

            def highs(b, c, ready, high, bias, first_chunk):
                act.wait_ge(ready, b.n(2, c + 1))
                for m in range(2):
                    last = act.activation(nat[0][:, 2 * c + m], pj_ps[c][:, m * N:(m + 1) * N], ACT.Identity,
                                          bias=bias[:, first_chunk + m:first_chunk + m + 1])
                last.then_inc(high, 1)

            def copy_v(b, t):
                act.wait_ge(v_ps, b.n(2, t + 1))
                wait(act, pv_done, b.n(KC, -KC))
                act.copy(vt[:, b.par, t], pj_ps[t][0:QN, :]).then_inc(v_done, 1)

            def exps(b, h):
                act.wait_ge(maxed, b.n(NH, h + 1))
                wait(act, pT_ps, b.n(NH, h - 1))
                if h % HPG == 0:
                    wait(act, inverted, b.n(KC, h // HPG - 1))
                for t in range(QT):
                    last = act.activation(pr[:, h % 2, t], sc_ps[h % 2][0:QN, t * N:(t + 1) * N], ACT.Exp,
                                          bias=nmax[:, h % 2, t:t + 1], accum_out=rsum[:, (h // HPG) % 2, h % HPG, t:t + 1])
                last.then_inc(exped, 1)

            def copy_rT(b, g):
                act.wait_ge(rT_ps, b.n(KC, g + 1))
                wait(act, rb_ps, b.n(KC, g))
                act.copy(rT[:], r_ps[0:HPG, 0:N]).then_inc(rT_done, 1)

            def copy_rb(b, g):
                act.wait_ge(rb_ps, b.n(KC, g + 1))
                wait(act, o_done, b.n(KC, g))
                act.copy(rb[:], r_ps[:, 0:N]).then_inc(rb_done, 1)

            def highs_o(b):
                wait(act, c_ps, b.n(2, 0))
                for g in range(KC):
                    act.wait_ge(o_done, b.n(KC, g + 1))
                    act.activation(yT[0][:, g], ou[:, g], ACT.Identity, bias=bqkv[:, 2 * KC + g:2 * KC + g + 1]).then_inc(oT_h, 1)

            def highs_y(b):
                act.wait_ge(proj_ps, b.n(2, 2))
                for c in range(2):
                    act.wait_ge(yT_ps, b.n(2, c + 1))
                    act.copy(yT[0][:, 2 * c:2 * c + 2], pj_ps[c][:, 0:2 * N].rearrange("p (m n) -> p m n", m=2)).then_inc(yT_h, 1)

            def body(b, att, nxt, prv):
                a, z = b.plus(1), b.plus(-1)
                for h in range(NH):
                    if att:
                        exps(b, h)
                    if h == 0 and prv:
                        copy_rT(z, KC - 1)
                    if h % HPG == 0 and h > 0 and att:
                        copy_rT(b, h // HPG - 1)
                    if h == 1 and prv:
                        copy_rb(z, KC - 1)
                    if h % HPG == 1 and h > 1 and att:
                        copy_rb(b, h // HPG - 1)
                    if nxt and h == 1:
                        apply_ln(a, x_in, x_in, rs1, nm1, nmr1, xhat1)
                    if prv and h == 2:
                        highs_o(z)
                    if nxt and h == 2:
                        high_x(a)
                    if nxt and h in (4, 5):
                        if h == 4:
                            act.wait_ge(q_stacked[b.par], b.pair(STACK, STACK))
                            wait(act, qc_out, z.n(32, 0))
                        highs(a, h - 4, k_ps, k_h, bqkv, KC + 2 * (h - 4))
                    if nxt and h in (9, 10):
                        if h == 9:
                            act.wait_ge(k_stacked[a.par], a.pair(STACK, STACK))
                        highs(a, h - 9, q_ps, q_h, bqs, 2 * (h - 9))
                    if prv and h == 10:
                        apply_ln(z, y, x_res, rs2, nm2, nmr2, xhat2)
                    if prv and h == 12:
                        highs_y(z)
                    if prv and h in (14, 15):
                        if nxt and h == 14:
                            act.wait_ge(q_stacked[a.par], a.pair(STACK, STACK))
                        if not nxt and h == 14:
                            act.wait_ge(qc_out, z.n(32, 0))
                        highs(z, h - 14, c_ps, c_h, bqcs, 2 * (h - 14))
                    if nxt and h == 15:
                        copy_v(a, 0)
                        copy_v(a, 1)

            act.wait_ge(bias_scaled, 1)
            a = Batch(0)
            apply_ln(a, x_in, x_in, rs1, nm1, nmr1, xhat1)
            high_x(a)
            for c in range(2):
                highs(a, c, k_ps, k_h, bqkv, KC + 2 * c)
            act.wait_ge(k_stacked[0], STACK)
            for c in range(2):
                highs(a, c, q_ps, q_h, bqs, 2 * c)
            copy_v(a, 0)
            copy_v(a, 1)
            bodies(act, body)

        @block.gpsimd
        def _(pool):
            def rstd(b, mv, ve, rs, s_mv, s_ve, s_rstd):
                pool.wait_ge(s_mv, b.n(1, 1))
                pool.tensor_tensor(ve[:], mv[:, :, 1], eps[0:QN, 0:QT], ALU.add).then_inc(s_ve, 1)
                pool.wait_ge(s_ve, b.n(1, 1))
                pool.tensor_tensor(rs[:], ve[:], neg_half[0:QN, 0:QT], ALU.pow).then_inc(s_rstd, 1)

            def low_x(b):
                pool.wait_ge(xT_h, b.n(1, 1))
                pool.tensor_tensor(xT[1][:], xv[:], xT[0][:].bitcast(F32), ALU.subtract).then_inc(xT_l, 1)

            def residual(b, t):
                if t == 0:
                    pool.wait_ge(gate_loaded, b.n(16, 16))
                    pool.wait_ge(res_loaded, b.n(16, 16))
                pool.wait_ge(proj_done, b.n(2, t + 1))
                pool.tensor_tensor(y[:, t], y[:, t], gate[:], ALU.mult).then_inc(gated, 1)
                pool.wait_ge(gated, b.n(2, t + 1))
                pool.tensor_tensor(y[:, t], y[:, t], x_res[:, t], ALU.add).then_inc(summed, 1)

            def body(b, att, nxt, prv):
                a, z = b.plus(1), b.plus(-1)
                if nxt:
                    rstd(a, mv1, ve1, rs1, mvs1, vareps1, rstd1)
                    low_x(a)
                if prv:
                    for t in range(QT):
                        residual(z, t)
                    rstd(z, mv2, ve2, rs2, mvs2, vareps2, rstd2)

            a = Batch(0)
            rstd(a, mv1, ve1, rs1, mvs1, vareps1, rstd1)
            low_x(a)
            bodies(pool, body)



def cross_phase(nc, ctx_in_dram, w_kvc, b_kvc_t, qc, o_dram, ident, select, neg_half, eps):
    with ExitStack() as ctx:
        sb, ps, sem = alloc(nc, ctx, "cross")
        wkv = [sb(f"wkv_{s}", [P, KC, 2 * H], F32R) for s in "hl"]
        bkv = sb("bkv", [P, 2 * KC])
        load_columns(nc, "cross", [(bkv[:], b_kvc_t)])
        split_weights(nc, "cross", [(w_kvc, wkv[0], wkv[1], 1.0)])
        kst = sb("kst", [TERMS * HD, KC, HPG, S], F32R)
        qst = sb("qst", [TERMS * HD, KC, HPG, N], F32R)
        nat = [sb(f"nat_{s}", [P, 2, S], F32R) for s in "hl"]
        cT = [sb(f"cT_{s}", [P, KC, S], F32R) for s in "hl"]
        vt = sb("vt", [SN, 2, ST, H])
        c_in = sb("c_in", [SN, ST, H])
        pr = sb("pr", [QN, 2, QT, S])
        prT = sb("prT", [SN, HPG, ST, N])
        ou = sb("ou", [P, 2, N])
        nmax = sb("nmax", [QN, 2, QT])
        rsum = sb("rsum", [QN, 2, HPG, QT])
        rinv = sb("rinv", [QN, HPG, QT])
        rT = sb("rT", [HPG, N])
        rb = sb("rb", [P, N])
        st = sb("st", [SN, ST, 6])
        turn = sb("turn", [1, 1])
        mv = sb("mv", [SN, ST, 2])
        ve, rs, nm = sb("ve", [SN, ST]), sb("rs", [SN, ST]), sb("nm", [SN, ST])

        sc_ps = [ps(f"sc_ps{i}", (P, 1024)) for i in range(2)]
        tr_ps = [ps(f"tr_ps{i}") for i in range(2)]
        pj_ps = ps("pj_ps")
        or_ps = ps("or_ps")
        SC0 = 512 - SHALF[0]
        R0 = 256

        c_loaded, stats_done, mvs, vareps, rstd, nmr, chat = (sem(s) for s in ("c_loaded", "stats_done", "mvs", "vareps", "rstd", "nmr", "chat"))
        cT_ps, cT_h, cT_l = sem("cT_ps"), sem("cT_h"), sem("cT_l")
        k_ps, k_h, k_l = sem("k_ps"), sem("k_h"), sem("k_l")
        v_ps, v_done = sem("v_ps"), sem("v_done")
        k_stacked = [sem(f"k_stacked{g}") for g in range(KC)]
        q_stacked = [sem(f"q_stacked{g}") for g in range(KC)]
        scored_t = [sem(f"scored_t{t}") for t in range(QT)]
        maxed, exped, pT_ps = sem("maxed"), sem("exped"), sem("pT_ps")
        pT_dve, pT_act = sem("pT_dve"), sem("pT_act")
        pv_done, inverted, rT_ps, rT_done, rb_ps, rb_done, o_done = (sem(s) for s in ("pv_done", "inverted", "rT_ps", "rT_done", "rb_ps", "rb_done", "o_done"))
        o_out = [sem(f"o_out{i}") for i in range(2)]
        STACK, QSTACK = 16 * HPG * TERMS, 16 * TERMS
        HALVES = ((0, SHALF[0]), (SHALF[0], SHALF[1]))
        FILL = [[("c", 0), ("c", 1)], [("c", 2), ("c", 3)], [("c", 4), ("c", 5)], [("v", 0)],
                [("k", 0, 0)], [("k", 0, 1)], [("v", 1)], [("k", 1, 0)], [("k", 1, 1)], [("k", 2, 0), ("v", 2)],
                [("k", 2, 1)], [("v", 3)], [("k", 3, 0)], [("k", 3, 1)], [("v", 4)], [("v", 5)]]
        ORDER = [f for step in FILL for f in step]
        BY_ACT = 1
        block = ctx.enter_context(nc.Block())

        def bodies(eng, body):
            body(Batch(0), True, True, False)
            body(Batch(1), True, True, True)
            with eng.Fori(0, (B - 4) // 2) as i:
                body(Batch(2, i), True, True, True)
                body(Batch(3, i), True, True, True)
            body(Batch(B - 2), True, True, True)
            body(Batch(B - 1), True, False, True)
            body(Batch(B), False, False, True)

        def bank_free(eng, b, fill):
            at = ORDER.index(fill)
            if at == 0:
                wait(eng, v_done, b.n(ST, 0))
                return
            kind, *where = ORDER[at - 1]
            if kind == "c":
                eng.wait_ge(cT_l, b.n(ST, where[0] + 1))
            elif kind == "k":
                eng.wait_ge(k_l, b.n(2 * KC, 2 * where[0] + where[1] + 1))
            else:
                eng.wait_ge(v_done, b.n(ST, where[0] + 1))

        def far(b):
            return not (isinstance(b.i, int) and b.c > B - 3)

        @block.sync
        def _(sp):
            def load_c(b):
                wait(sp, cT_ps, b.n(ST, 0))
                sp.dma_start(c_in[:], ctx_in_dram[bass.ds(b.index(), 1)].rearrange("a (t p) n -> p (a t) n", p=SN)).then_inc(c_loaded, 16)

            def load_q(b, g):
                wait(sp, scored_t[QT - 1], b.n(NH, HPG * (g + 1) - NH))
                for r, s in enumerate((0, 0, 1)):
                    src = qc[bass.ds(b.index(), 1), s, g * P:(g + 1) * P].rearrange("a (j d) t -> d (a j) t", d=HD)
                    sp.dma_start(qst[HD * r:HD * r + HD, g].bitcast(F32), src).then_inc(q_stacked[g], 16)

            def stack_k(b, g):
                sp.wait_ge(k_l, b.n(2 * KC, 2 * g + 2))
                wait(sp, scored_t[QT - 1], b.n(NH, HPG * (g + 1) - NH))
                for j in range(HPG):
                    for r, s in enumerate((0, 1, 0)):
                        sp.dma_start(kst[HD * r:HD * r + HD, g, j].bitcast(F32),
                                     nat[s][HD * j:HD * j + HD, g % 2].bitcast(F32)).then_inc(k_stacked[g], 16)

            def body(b, att, nxt, prv):
                a = b.plus(1)
                if far(b):
                    load_c(b.plus(2))
                for g in range(KC):
                    if nxt:
                        load_q(a, g)
                        stack_k(a, g)

            load_c(Batch(0))
            load_c(Batch(1))
            for g in range(KC):
                load_q(Batch(0), g)
            for g in range(KC):
                stack_k(Batch(0), g)
            bodies(sp, body)

        @block.tensor
        def _(pe):
            def fill_(b, fill):
                bank_free(pe, b, fill)
                kind, *where = fill
                if kind == "c":
                    t, = where
                    pe.wait_ge(chat, b.n(2, t // 3 + 1))
                    for k in range(KC):
                        last = pe.transpose(pj_ps[:, k * SN:(k + 1) * SN], c_in[:, t, k * P:(k + 1) * P], ident[0:SN, 0:SN])
                    last.then_inc(cT_ps, 1)
                elif kind == "k":
                    g, half = where
                    pe.wait_ge(cT_l, b.n(ST, ST))
                    c0, cn = HALVES[half]
                    for k in range(KC):
                        last = product(pe, pj_ps[:, 0:cn], tuple(w[:, k, g * P:(g + 1) * P] for w in wkv),
                                       tuple(c[:, k, c0:c0 + cn] for c in cT), k == 0, k == KC - 1)
                    last.then_inc(k_ps, 1)
                else:
                    t, = where
                    pe.wait_ge(cT_l, b.n(ST, ST))
                    for k in range(KC):
                        last = product(pe, pj_ps[0:SN, :], tuple(c[:, k, t * SN:(t + 1) * SN] for c in cT),
                                       tuple(w[:, k, H:2 * H] for w in wkv), k == 0, k == KC - 1)
                    last.then_inc(v_ps, 1)

            def score(b, h):
                g, j = h // HPG, h % HPG
                if j == 0:
                    pe.wait_ge(k_stacked[g], b.n(STACK, STACK))
                    pe.wait_ge(q_stacked[g], b.n(QSTACK, QSTACK))
                for t in range(QT):
                    wait(pe, exped, b.n(NH * QT, h * QT + t - 1))
                    for c0, cn in HALVES:
                        last = pe.matmul(sc_ps[t][0:QN, SC0 + c0:SC0 + c0 + cn], qst[:, g, j, t * QN:(t + 1) * QN],
                                         kst[:, g, j, c0:c0 + cn], start=True, stop=True)
                    last.then_inc(scored_t[t], 1)

            def trans_p(b, h):
                for c in range(ST // 2):
                    u = h * (ST // 2) + c
                    if c == 0:
                        pe.wait_ge(exped, b.n(NH * QT, (h + 1) * QT))
                    free_bank(b, u)
                    for m in range(2):
                        for t in range(QT):
                            at = m * N + t * QN
                            kt = 2 * c + m
                            last = pe.transpose(tr_ps[u % 2][0:SN, at:at + QN], pr[:, h % 2, t, kt * SN:(kt + 1) * SN], ident[0:QN, 0:QN])
                    last.then_inc(pT_ps, 1)

            def free_bank(b, u):
                w = u - 2
                h, c = (w // 3, w % 3)
                if c == BY_ACT:
                    wait(pe, pT_act, b.n(NH, h + 1))
                else:
                    wait(pe, pT_dve, b.n(2 * NH, 2 * h + (1 if c == 0 else 2)))

            def pv(b, g):
                pe.wait_ge(pT_dve, b.n(2 * NH, 2 * HPG * (g + 1)))
                pe.wait_ge(pT_act, b.n(NH, HPG * (g + 1)))
                if g == 0:
                    pe.wait_ge(v_done, b.n(ST, ST))
                wait(pe, o_done, b.n(KC, g))
                for kt in range(ST):
                    for j in range(HPG):
                        ch = g * P + j * HD
                        last = pe.matmul(or_ps[HD * j:HD * j + HD, 0:N], vt[:, b.par, kt, ch:ch + HD], prT[:, j, kt],
                                         start=kt == 0, stop=kt == ST - 1)
                last.then_inc(pv_done, 1)
                pe.wait_ge(inverted, b.n(KC, g + 1))
                for t in range(QT):
                    last = pe.transpose(or_ps[0:HPG, R0 + t * QN:R0 + (t + 1) * QN], rinv[:, :, t], ident[0:QN, 0:QN])
                last.then_inc(rT_ps, 1)

            def spread(b, g):
                pe.wait_ge(rT_done, b.n(KC, g + 1))
                pe.matmul(or_ps[:, R0:R0 + N], select[:], rT[:], start=True, stop=True).then_inc(rb_ps, 1)

            def body(b, att, nxt, prv):
                a, z = b.plus(1), b.plus(-1)
                for h in range(NH):
                    if att:
                        score(b, h)
                    if nxt:
                        fill_(a, FILL[h][0])
                    if h > 0 and att:
                        trans_p(b, h - 1)
                    if h == 0 and prv:
                        trans_p(z, NH - 1)
                    if nxt and len(FILL[h]) > 1:
                        fill_(a, FILL[h][1])
                    if h == 0 and prv:
                        pv(z, KC - 1)
                    if h % HPG == 0 and h > 0 and att:
                        pv(b, h // HPG - 1)
                    if h == 1 and prv:
                        spread(z, KC - 1)
                    if h % HPG == 1 and h > 1 and att:
                        spread(b, h // HPG - 1)

            for f in ORDER:
                fill_(Batch(0), f)
            bodies(pe, body)

        @block.vector
        def _(dve):
            def stats(b, half):
                if half == 0:
                    dve.wait_ge(c_loaded, b.n(16, 16))
                at = range(3 * half, 3 * half + 3)
                for t in at:
                    last = dve.bn_stats(st[:, t], c_in[:, t])
                last.then_inc(stats_done, 1)
                dve.wait_ge(stats_done, b.n(2, half + 1))
                dve.memset(turn[:], 0.0)
                for t in at:
                    last = dve.bn_aggr(mv[:, t], st[:, t])
                last.then_inc(mvs, 1)

            def neg_mean(b, half):
                dve.wait_ge(rstd, b.n(2, half + 1))
                at = slice(3 * half, 3 * half + 3)
                dve.scalar_tensor_tensor(out=nm[:, at], in0=mv[:, at, 0], scalar=-1.0, in1=rs[:, at], op0=ALU.mult, op1=ALU.mult).then_inc(nmr, 1)

            def low(b, fill):
                kind, *where = fill
                if kind == "c":
                    t, = where
                    dve.wait_ge(cT_h, b.n(ST, t + 1))
                    at = slice(t * SN, (t + 1) * SN)
                    dve.tensor_tensor(cT[1][:, :, at], pj_ps[:, 0:KC * SN].rearrange("p (k n) -> p k n", k=KC),
                                      cT[0][:, :, at].bitcast(F32), ALU.subtract).then_inc(cT_l, 1)
                if kind == "k":
                    g, half = where
                    c0, cn = HALVES[half]
                    dve.wait_ge(k_h, b.n(2 * KC, 2 * g + half + 1))
                    dve.scalar_tensor_tensor(out=nat[1][:, g % 2, c0:c0 + cn], in0=pj_ps[:, 0:cn], scalar=bkv[:, g:g + 1],
                                             in1=nat[0][:, g % 2, c0:c0 + cn].bitcast(F32), op0=ALU.add, op1=ALU.subtract).then_inc(k_l, 1)

            def row_max(b, h):
                for t in range(QT):
                    dve.wait_ge(scored_t[t], b.n(NH, h + 1))
                    wait(dve, exped, b.n(NH * QT, (h - 2) * QT + t + 1))
                    dve.tensor_reduce(nmax[:, h % 2, t:t + 1], sc_ps[t][0:QN, SC0:SC0 + S], AX_X, ALU.max, negate=True).then_inc(maxed, 1)

            def copy_p(b, h):
                for c in (0, 2):
                    dve.wait_ge(pT_ps, b.n(3 * NH, 3 * h + c + 1))
                    if h % HPG == 0 and c == 0:
                        wait(dve, pv_done, b.n(KC, h // HPG))
                    dve.tensor_copy(prT[:, h % HPG, 2 * c:2 * c + 2], tr_ps[(3 * h + c) % 2][0:SN, 0:2 * N].rearrange("p (k t) -> p k t", k=2)).then_inc(pT_dve, 1)

            def invert(b, g):
                dve.wait_ge(exped, b.n(NH * QT, HPG * QT * (g + 1)))
                wait(dve, rT_ps, b.n(KC, g))
                dve.reciprocal(rinv[:], rsum[:, g % 2]).then_inc(inverted, 1)

            def normalize(b, g):
                dve.wait_ge(rb_done, b.n(KC, g + 1))
                wait(dve, o_out[g % 2], b.n(32, 16 * (g // 2)))
                dve.tensor_tensor(ou[:, g % 2], or_ps[:, 0:N], rb[:], ALU.mult).then_inc(o_done, 1)

            def body(b, att, nxt, prv):
                a, z = b.plus(1), b.plus(-1)
                for h in range(NH):
                    if att:
                        row_max(b, h)
                    if nxt:
                        low(a, FILL[h][0])
                    if h > 0 and att:
                        copy_p(b, h - 1)
                    if h == 0 and prv:
                        copy_p(z, NH - 1)
                        invert(z, KC - 1)
                    if h % HPG == 0 and h > 0 and att:
                        invert(b, h // HPG - 1)
                    if nxt and len(FILL[h]) > 1:
                        low(a, FILL[h][1])
                    if h == 2 and prv:
                        normalize(z, KC - 1)
                    if h % HPG == 2 and h > 2 and att:
                        normalize(b, h // HPG - 1)
                    if far(b) and h in (8, 11):
                        stats(b.plus(2), 0 if h == 8 else 1)
                    if far(b) and h in (9, 12):
                        neg_mean(b.plus(2), 0 if h == 9 else 1)

            for half in range(2):
                stats(Batch(0), half)
                neg_mean(Batch(0), half)
            for f in ORDER:
                low(Batch(0), f)
            for half in range(2):
                stats(Batch(1), half)
                neg_mean(Batch(1), half)
            bodies(dve, body)

        @block.scalar
        def _(act):
            def apply_ln(b, half):
                act.wait_ge(nmr, b.n(2, half + 1))
                for t in range(3 * half, 3 * half + 3):
                    last = act.activation(c_in[:, t], c_in[:, t], ACT.Identity, bias=nm[:, t:t + 1], scale=rs[:, t:t + 1])
                last.then_inc(chat, 1)

            def high(b, fill):
                kind, *where = fill
                if kind == "c":
                    t, = where
                    act.wait_ge(cT_ps, b.n(ST, t + 1))
                    if t == 0:
                        wait(act, v_ps, b.n(ST, 0))
                        wait(act, k_ps, b.n(2 * KC, 0))
                    act.copy(cT[0][:, :, t * SN:(t + 1) * SN], pj_ps[:, 0:KC * SN].rearrange("p (k n) -> p k n", k=KC)).then_inc(cT_h, 1)
                elif kind == "k":
                    g, half = where
                    c0, cn = HALVES[half]
                    act.wait_ge(k_ps, b.n(2 * KC, 2 * g + half + 1))
                    if half == 0:
                        if g >= 2:
                            act.wait_ge(k_stacked[g - 2], b.n(STACK, STACK))
                        else:
                            wait(act, k_stacked[g + 2], b.n(STACK, 0))
                    act.activation(nat[0][:, g % 2, c0:c0 + cn], pj_ps[:, 0:cn], ACT.Identity, bias=bkv[:, g:g + 1]).then_inc(k_h, 1)
                else:
                    t, = where
                    act.wait_ge(v_ps, b.n(ST, t + 1))
                    wait(act, pv_done, b.n(KC, -KC))
                    act.copy(vt[:, b.par, t], pj_ps[0:SN, :]).then_inc(v_done, 1)

            def exps(b, h):
                wait(act, pT_ps, b.n(3 * NH, 3 * (h - 1)))
                if h % HPG == 0:
                    wait(act, inverted, b.n(KC, h // HPG - 1))
                for t in range(QT):
                    act.wait_ge(maxed, b.n(NH * QT, h * QT + t + 1))
                    act.activation(pr[:, h % 2, t], sc_ps[t][0:QN, SC0:SC0 + S], ACT.Exp, bias=nmax[:, h % 2, t:t + 1],
                                   accum_out=rsum[:, (h // HPG) % 2, h % HPG, t:t + 1]).then_inc(exped, 1)

            def copy_p(b, h):
                c = BY_ACT
                act.wait_ge(pT_ps, b.n(3 * NH, 3 * h + c + 1))
                if h % HPG == 0:
                    wait(act, pv_done, b.n(KC, h // HPG))
                act.copy(prT[:, h % HPG, 2 * c:2 * c + 2], tr_ps[(3 * h + c) % 2][0:SN, 0:2 * N].rearrange("p (k t) -> p k t", k=2)).then_inc(pT_act, 1)

            def copy_rT(b, g):
                act.wait_ge(rT_ps, b.n(KC, g + 1))
                wait(act, rb_ps, b.n(KC, g))
                act.copy(rT[:], or_ps[0:HPG, R0:R0 + N]).then_inc(rT_done, 1)

            def copy_rb(b, g):
                act.wait_ge(rb_ps, b.n(KC, g + 1))
                wait(act, o_done, b.n(KC, g))
                act.copy(rb[:], or_ps[:, R0:R0 + N]).then_inc(rb_done, 1)

            def body(b, att, nxt, prv):
                a, z = b.plus(1), b.plus(-1)
                for h in range(NH):
                    if att:
                        exps(b, h)
                    if nxt:
                        high(a, FILL[h][0])
                    if h > 0 and att:
                        copy_p(b, h - 1)
                    if h == 0 and prv:
                        copy_p(z, NH - 1)
                    if nxt and len(FILL[h]) > 1:
                        high(a, FILL[h][1])
                    if h == 0 and prv:
                        copy_rT(z, KC - 1)
                    if h % HPG == 0 and h > 0 and att:
                        copy_rT(b, h // HPG - 1)
                    if h == 1 and prv:
                        copy_rb(z, KC - 1)
                    if h % HPG == 1 and h > 1 and att:
                        copy_rb(b, h // HPG - 1)
                    if far(b) and h in (10, 13):
                        apply_ln(b.plus(2), 0 if h == 10 else 1)

            for half in range(2):
                apply_ln(Batch(0), half)
            for f in ORDER:
                high(Batch(0), f)
            for half in range(2):
                apply_ln(Batch(1), half)
            bodies(act, body)

        @block.gpsimd
        def _(pool):
            def inverse_std(b, half):
                at = slice(3 * half, 3 * half + 3)
                pool.wait_ge(mvs, b.n(2, half + 1))
                pool.tensor_tensor(ve[:, at], mv[:, at, 1], eps[0:SN, 0:3], ALU.add).then_inc(vareps, 1)
                pool.wait_ge(vareps, b.n(2, half + 1))
                pool.tensor_tensor(rs[:, at], ve[:, at], neg_half[0:SN, 0:3], ALU.pow).then_inc(rstd, 1)

            def store(b, g):
                pool.wait_ge(o_done, b.n(KC, g + 1))
                pool.dma_start(o_dram[bass.ds(b.index(), 1), g * P:(g + 1) * P].rearrange("a p t -> p (a t)"), ou[:, g % 2]).then_inc(o_out[g % 2], 16)

            def body(b, att, nxt, prv):
                z = b.plus(-1)
                if prv:
                    store(z, KC - 1)
                if att:
                    store(b, 0)
                if far(b):
                    inverse_std(b.plus(2), 0)
                if att:
                    store(b, 1)
                if far(b):
                    inverse_std(b.plus(2), 1)
                if att:
                    store(b, 2)

            for b in (Batch(0), Batch(1)):
                for half in range(2):
                    inverse_std(b, half)
            bodies(pool, body)
            for i in range(2):
                pool.wait_ge(o_out[i], 32 * B)


def mlp_phase(nc, x1, o_dram, b_vc_t, w_cproj, b_cproj, w_mlp1, b_mlp1_t, w_mlp2, b_mlp2, gates, out, mod_t, ident, neg_half, eps):
    MC = MLP // P
    PAIRS = MC // 2
    GR = 3
    with ExitStack() as ctx:
        sb, ps, sem = alloc(nc, ctx, "mlp")
        wcp = [sb(f"wcp_{s}", [P, KC, H], F32R) for s in "hl"]
        w1 = [sb(f"w1_{s}", [P, KC, MLP], F32R) for s in "hl"]
        w2 = [sb(f"w2_{s}", [P, MC, H], F32R) for s in "hl"]
        bv = sb("bv", [P, KC])
        b1 = sb("b1", [P, MC])
        bcp, b2 = sb("bcp", [QN, H]), sb("b2", [QN, H])
        rows = lambda v: v.rearrange("(a n) -> a n", a=1).broadcast_to([QN, H])
        load_columns(nc, "mlp", [(bv[:], b_vc_t), (b1[:], b_mlp1_t), (bcp[:], rows(b_cproj)), (b2[:], rows(b_mlp2))])
        split_weights(nc, "mlp", [(w_cproj, wcp[0], wcp[1], 1.0), (w_mlp1, w1[0], w1[1], 1.0), (w_mlp2, w2[0], w2[1], 1.0)])
        o_in = sb("o_in", [P, KC, N])
        oT = [sb(f"oT_{s}", [P, KC, N], F32R) for s in "hl"]
        x_in = sb("x_in", [QN, QT, H])
        x2 = sb("x2", [QN, 2, QT, H])
        y = sb("y", [QN, QT, H])
        gate = sb("gate", [QN, H])
        xv = sb("xv", [P, KC, N])
        xT = [sb(f"xT_{s}", [P, KC, N], F32R) for s in "hl"]
        hv = sb("hv", [P, 2, 2, N])
        hT = [sb(f"hT_{s}", [P, GR, 2, N], F32R) for s in "hl"]
        turn = sb("turn", [1, 1])
        st, mv = sb("st", [QN, QT, 6]), sb("mv", [QN, QT, 2])
        ve, rs, nm = sb("ve", [QN, QT]), sb("rs", [QN, QT]), sb("nm", [QN, QT])

        h_ps = [ps(f"h_ps{i}") for i in range(2)]
        a_ps = [ps(f"a_ps{i}") for i in range(2)]
        c_ps = [ps(f"c_ps{i}") for i in range(2)]
        t_ps = [ps(f"t_ps{i}") for i in range(2)]

        o_loaded, x_loaded, gate_loaded = sem("o_loaded"), sem("x_loaded"), sem("gate_loaded")
        oT_h, oT_l, cp_ps, cp_done, x2_done = (sem(s) for s in ("oT_h", "oT_l", "cp_ps", "cp_done", "x2_done"))
        stats_done, mvs, vareps, rstd, nmr, xhat = (sem(s) for s in ("stats_done", "mvs", "vareps", "rstd", "nmr", "xhat"))
        xT_ps, xT_v, xT_h, xT_l = sem("xT_ps"), sem("xT_v"), sem("xT_h"), sem("xT_l")
        h_mm, h_act, h_h, h_l, h_used = (sem(s) for s in ("h_mm", "h_act", "h_h", "h_l", "h_used"))
        y_done, gated, summed, out_done = (sem(s) for s in ("y_done", "gated", "summed", "out_done"))
        block = ctx.enter_context(nc.Block())

        def bodies(eng, body):
            body(Batch(0), True, True, False)
            body(Batch(1), True, True, True)
            with eng.Fori(0, (B - 4) // 2) as i:
                body(Batch(2, i), True, True, True)
                body(Batch(3, i), True, True, True)
            body(Batch(B - 2), True, True, True)
            body(Batch(B - 1), True, False, True)
            body(Batch(B), False, False, True)

        @block.sync
        def _(sp):
            def load(b):
                wait(sp, oT_l, b.n(KC, 0))
                sp.dma_start(o_in[:], o_dram[bass.ds(b.index(), 1)].rearrange("a (g p) t -> p (a g) t", p=P)).then_inc(o_loaded, 16)
                wait(sp, xT_ps, b.n(2, 0))
                sp.dma_start(x_in[:], x1[bass.ds(b.index(), 1)].rearrange("a (t p) n -> p (a t) n", p=QN)).then_inc(x_loaded, 16)

            def finish(b):
                wait(sp, gated, b.n(2, 0))
                sp.dma_start(gate[:], gates[1, bass.ds(b.index(), 1)].broadcast_to([QN, H])).then_inc(gate_loaded, 16)
                for t in range(QT):
                    sp.wait_ge(summed, b.n(2, t + 1))
                    sp.dma_start(out[bass.ds(b.index(), 1), t * QN:(t + 1) * QN].rearrange("a p n -> p (a n)"), y[:, t]).then_inc(out_done, 16)

            def body(b, att, nxt, prv):
                if prv:
                    finish(b.plus(-1))
                if nxt and not (isinstance(b.i, int) and b.c == B - 2):
                    load(b.plus(2))

            load(Batch(0))
            load(Batch(1))
            bodies(sp, body)
            sp.wait_ge(out_done, 32 * B)

        @block.tensor
        def _(pe):
            def cproj(b, t):
                pe.wait_ge(oT_l, b.n(KC, KC))
                wait(pe, cp_done, b.n(2, t - 1))
                for k in range(KC):
                    last = product(pe, c_ps[t][0:QN, :], tuple(o[:, k, t * QN:(t + 1) * QN] for o in oT),
                                   tuple(w[:, k] for w in wcp), k == 0, k == KC - 1)
                last.then_inc(cp_ps, 1)

            def trans_x(b):
                pe.wait_ge(xhat, b.n(1, 1))
                wait(pe, xT_v, b.n(1, 0))
                for c in range(2):
                    for k in range(2):
                        for t in range(QT):
                            at = k * N + t * QN
                            last = pe.transpose(t_ps[c][:, at:at + QN], x_in[:, t, (2 * c + k) * P:(2 * c + k + 1) * P], ident[0:QN, 0:QN])
                    last.then_inc(xT_ps, 1)

            def hidden(b, p):
                if p == 0:
                    pe.wait_ge(xT_l, b.n(1, 1))
                wait(pe, h_act, b.n(PAIRS, p - 1))
                for m in range(2):
                    at = (2 * p + m) * P
                    for k in range(KC):
                        last = product(pe, h_ps[p % 2][:, m * N:(m + 1) * N], tuple(w[:, k, at:at + P] for w in w1),
                                       tuple(v[:, k] for v in xT), k == 0, k == KC - 1)
                last.then_inc(h_mm, 1)

            def output(b, p, u):
                pe.wait_ge(h_l, b.n(PAIRS, p + 1))
                if p == 0:
                    wait(pe, y_done, b.n(2, 0))
                for m in range(2):
                    for t in range(QT):
                        last = product(pe, a_ps[t][0:QN, :], tuple(v[:, u % GR, m, t * QN:(t + 1) * QN] for v in hT),
                                       tuple(w[:, 2 * p + m] for w in w2), p == 0 and m == 0, p == PAIRS - 1 and m == 1)
                last.then_inc(h_used, 1)

            def body(b, att, nxt, prv):
                a = b.plus(1)
                for p in range(PAIRS):
                    if att:
                        hidden(b, p)
                        if p >= 2:
                            output(b, p - 2, p - 2)
                    if nxt and p in (1, 2):
                        cproj(a, p - 1)
                    if nxt and p == 6:
                        trans_x(a)
                if att:
                    output(b, PAIRS - 2, PAIRS - 2)
                    output(b, PAIRS - 1, PAIRS - 1)

            for t in range(QT):
                cproj(Batch(0), t)
            trans_x(Batch(0))
            bodies(pe, body)

        @block.vector
        def _(dve):
            def low_o(b):
                for g in range(KC):
                    dve.wait_ge(oT_h, b.n(KC, g + 1))
                    dve.scalar_tensor_tensor(out=oT[1][:, g], in0=o_in[:, g], scalar=bv[:, g:g + 1],
                                             in1=oT[0][:, g].bitcast(F32), op0=ALU.add, op1=ALU.subtract).then_inc(oT_l, 1)

            def residual(b, t):
                dve.wait_ge(cp_ps, b.n(2, t + 1))
                wait(dve, summed, b.n(2, -2))
                dve.tensor_tensor(x2[:, b.par, t], c_ps[t][0:QN, :], bcp[:], ALU.add).then_inc(cp_done, 1)

            def stats(b):
                for t in range(QT):
                    dve.wait_ge(x2_done, b.n(2, t + 1))
                    last = dve.bn_stats(st[:, t], x2[:, b.par, t])
                last.then_inc(stats_done, 1)
                dve.wait_ge(stats_done, b.n(1, 1))
                dve.memset(turn[:], 0.0)
                for t in range(QT):
                    last = dve.bn_aggr(mv[:, t], st[:, t])
                last.then_inc(mvs, 1)

            def neg_mean(b):
                dve.wait_ge(rstd, b.n(1, 1))
                dve.scalar_tensor_tensor(out=nm[:], in0=mv[:, :, 0], scalar=-1.0, in1=rs[:], op0=ALU.mult, op1=ALU.mult).then_inc(nmr, 1)

            def modulate(b):
                wait(dve, xT_l, b.n(1, 0))
                for c in range(2):
                    dve.wait_ge(xT_ps, b.n(2, c + 1))
                    for k in range(2):
                        m = 2 * c + k
                        last = dve.tensor_scalar(xv[:, m], t_ps[c][:, k * N:(k + 1) * N], mod_t[:, KC + m, bass.ds(b.index(), 1)],
                                                 mod_t[:, m, bass.ds(b.index(), 1)], ALU.mult, ALU.add)
                last.then_inc(xT_v, 1)

            def split_h(b, p):
                dve.wait_ge(h_act, b.n(PAIRS, p + 1))
                wait(dve, h_used, b.n(PAIRS, p - GR + 1))
                dve.tensor_copy(hT[0][:, p % GR], hv[:, p % 2]).then_inc(h_h, 1)
                dve.wait_ge(h_h, b.n(PAIRS, p + 1))
                dve.tensor_tensor(hT[1][:, p % GR], hv[:, p % 2], hT[0][:, p % GR].bitcast(F32), ALU.subtract).then_inc(h_l, 1)

            def add_bias(b, t):
                dve.wait_ge(h_used, b.n(PAIRS, PAIRS))
                wait(dve, out_done, b.n(32, 0))
                dve.tensor_tensor(y[:, t], a_ps[t][0:QN, :], b2[:], ALU.add).then_inc(y_done, 1)

            def body(b, att, nxt, prv):
                a, z = b.plus(1), b.plus(-1)
                if prv:
                    add_bias(z, 0)
                    add_bias(z, 1)
                for p in range(PAIRS):
                    if att:
                        split_h(b, p)
                    if nxt and p == 0:
                        low_o(a)
                    if nxt and p in (2, 3):
                        residual(a, p - 2)
                    if nxt and p == 4:
                        stats(a)
                    if nxt and p == 5:
                        neg_mean(a)
                    if nxt and p == 6:
                        modulate(a)

            a = Batch(0)
            low_o(a)
            residual(a, 0)
            residual(a, 1)
            stats(a)
            neg_mean(a)
            modulate(a)
            bodies(dve, body)

        @block.scalar
        def _(act):
            def high_o(b):
                act.wait_ge(o_loaded, b.n(16, 16))
                wait(act, cp_ps, b.n(2, 0))
                for g in range(KC):
                    act.activation(oT[0][:, g], o_in[:, g], ACT.Identity, bias=bv[:, g:g + 1]).then_inc(oT_h, 1)

            def apply_ln(b):
                act.wait_ge(nmr, b.n(1, 1))
                for t in range(QT):
                    last = act.activation(x_in[:, t], x2[:, b.par, t], ACT.Identity, bias=nm[:, t:t + 1], scale=rs[:, t:t + 1])
                last.then_inc(xhat, 1)

            def high_x(b):
                act.wait_ge(xT_v, b.n(1, 1))
                wait(act, h_mm, b.n(PAIRS, 0))
                act.copy(xT[0][:], xv[:]).then_inc(xT_h, 1)

            def gelu(b, p):
                act.wait_ge(h_mm, b.n(PAIRS, p + 1))
                wait(act, h_l, b.n(PAIRS, p - 1))
                for m in range(2):
                    c = 2 * p + m
                    last = act.activation(hv[:, p % 2, m], h_ps[p % 2][:, m * N:(m + 1) * N], ACT.Gelu_apprx_tanh, bias=b1[:, c:c + 1])
                last.then_inc(h_act, 1)

            def body(b, att, nxt, prv):
                a = b.plus(1)
                for p in range(PAIRS):
                    if att:
                        gelu(b, p)
                    if nxt and p == 0:
                        high_o(a)
                    if nxt and p == 5:
                        apply_ln(a)
                if nxt:
                    high_x(a)

            a = Batch(0)
            high_o(a)
            apply_ln(a)
            high_x(a)
            bodies(act, body)

        @block.gpsimd
        def _(pool):
            def add_x1(b, t):
                pool.wait_ge(cp_done, b.n(2, t + 1))
                if t == 0:
                    pool.wait_ge(x_loaded, b.n(16, 16))
                pool.tensor_tensor(x2[:, b.par, t], x2[:, b.par, t], x_in[:, t], ALU.add).then_inc(x2_done, 1)

            def inverse_std(b):
                pool.wait_ge(mvs, b.n(1, 1))
                pool.tensor_tensor(ve[:], mv[:, :, 1], eps[0:QN, 0:QT], ALU.add).then_inc(vareps, 1)
                pool.wait_ge(vareps, b.n(1, 1))
                pool.tensor_tensor(rs[:], ve[:], neg_half[0:QN, 0:QT], ALU.pow).then_inc(rstd, 1)

            def low_x(b):
                pool.wait_ge(xT_h, b.n(1, 1))
                pool.tensor_tensor(xT[1][:], xv[:], xT[0][:].bitcast(F32), ALU.subtract).then_inc(xT_l, 1)

            def gated_sum(b, t):
                if t == 0:
                    pool.wait_ge(gate_loaded, b.n(16, 16))
                pool.wait_ge(y_done, b.n(2, t + 1))
                pool.tensor_tensor(y[:, t], y[:, t], gate[:], ALU.mult).then_inc(gated, 1)
                pool.wait_ge(gated, b.n(2, t + 1))
                pool.tensor_tensor(y[:, t], y[:, t], x2[:, b.par, t], ALU.add).then_inc(summed, 1)

            def front(b):
                for t in range(QT):
                    add_x1(b, t)
                inverse_std(b)
                low_x(b)

            def body(b, att, nxt, prv):
                if prv:
                    for t in range(QT):
                        gated_sum(b.plus(-1), t)
                if nxt:
                    front(b.plus(1))

            front(Batch(0))
            bodies(pool, body)


def build(nc, x, context, cond_t, w_mod, b_mod, w_qkv, b_qkv_t, w_proj, b_proj, w_qc, b_qc_t, w_kvc, b_kvc_t,
          w_cproj, b_cproj, w_mlp1, b_mlp1_t, w_mlp2, b_mlp2, out):
    x1 = nc.dram_tensor("x1", (B, N, H), F32, kind="Internal").ap()
    qc = nc.dram_tensor("qc", (B, 2, H, N), F32, kind="Internal").ap()
    o_cross = nc.dram_tensor("o_cross", (B, H, N), F32, kind="Internal").ap()
    gates = nc.dram_tensor("gates", (2, B, H), F32, kind="Internal").ap()
    with ExitStack() as ctx:
        sb, ps, sem = alloc(nc, ctx, "shared")
        ident = sb("ident", [P, P])
        select = sb("select", [HPG, P])
        neg_half, eps = sb("neg_half", [P, 8]), sb("eps", [P, 8])
        mod_t = sb("mod_t", [P, 4 * KC, B])
        constants_phase(nc, ident, select, neg_half, eps)
        condition_phase(nc, cond_t, w_mod, b_mod, gates, mod_t, ident)
        self_phase(nc, x, w_qkv, b_qkv_t, w_proj, b_proj, w_qc, b_qc_t, gates, x1, qc, mod_t[:, 0:2 * KC], ident, select, neg_half, eps)
        cross_phase(nc, context, w_kvc, b_kvc_t, qc, o_cross, ident, select, neg_half, eps)
        mlp_phase(nc, x1, o_cross, b_kvc_t[:, KC:2 * KC], w_cproj, b_cproj, w_mlp1, b_mlp1_t, w_mlp2, b_mlp2, gates, out,
                  mod_t[:, 2 * KC:4 * KC], ident, neg_half, eps)


def kernel(x, cond_1024, ctx_1024, **weights):
    import numpy as np
    import concourse.bacc as bacc
    from concourse.bass_utils import run_bass_kernel_spmd

    w = {name.replace("L0_xcond_", ""): np.asarray(a) for name, a in weights.items()}

    def columns(v):
        return v.reshape(-1, P).T

    arrays = {
        "x": x, "context": ctx_1024, "cond_t": np.asarray(cond_1024).T.reshape(KC, P, B).transpose(1, 0, 2),
        "w_mod": w["W_mod"], "b_mod": w["b_mod"], "w_qkv": w["W_qkv"], "b_qkv_t": columns(w["b_qkv"]),
        "w_proj": w["W_proj"], "b_proj": w["b_proj"], "w_qc": w["W_qc"], "b_qc_t": columns(w["b_qc"]),
        "w_kvc": w["W_kvc"], "b_kvc_t": columns(w["b_kvc"]), "w_cproj": w["W_cproj"], "b_cproj": w["b_cproj"],
        "w_mlp1": w["W_mlp1"], "b_mlp1_t": columns(w["b_mlp1"]), "w_mlp2": w["W_mlp2"], "b_mlp2": w["b_mlp2"],
    }
    arrays = {f"in_{name}": np.ascontiguousarray(a) for name, a in arrays.items()}
    nc = bacc.Bacc("TRN2", target_bir_lowering=False, num_devices=1)
    aps = {name[3:]: nc.dram_tensor(name, a.shape, F32, kind="ExternalInput").ap() for name, a in arrays.items()}
    out = nc.dram_tensor("out", (B, N, H), F32, kind="ExternalOutput").ap()
    build(nc, out=out, **aps)
    r = run_bass_kernel_spmd(nc, [arrays], core_ids=[0])
    return r.results[0]["out"]
```

```python
from contextlib import ExitStack

import concourse.bass as bass
from concourse import mybir

ALU = mybir.AluOpType
ACT = mybir.ActivationFunctionType
F32 = mybir.dt.float32
F32R = mybir.dt.float32r
AX_X = mybir.AxisListType.X

P = 128
B, N, H = 16, 224, 512
S = 750
NH, HD = 16, 32
MLP = 4 * H
KC = H // P
HPG = P // HD
QT, QN = 2, N // 2
ST, SN = 6, S // 6
SHALF = (376, S - 376)
TERMS = 3
SCALE = float(HD) ** -0.5
EPS = 1e-6
SHIFT_A, SCALE_A, GATE_A, SHIFT_M, SCALE_M, GATE_M = range(6)


class Batch:

    def __init__(self, c, i=0):
        self.c, self.i = c, i
        self.par = c % 2

    def plus(self, d):
        return Batch(self.c + d, self.i)

    def index(self):
        return self.i * 2 + self.c

    def n(self, per, k):
        return self.i * (2 * per) + (self.c * per + k)

    def pair(self, per, k=0):
        return self.i * per + ((self.c // 2) * per + k)


def wait(eng, sem, value):
    if not (isinstance(value, int) and value <= 0):
        eng.wait_ge(sem, value)


def product(pe, out, lhs, rhs, first, last):
    pe.matmul(out, lhs[0], rhs[1], start=first, stop=False)
    pe.matmul(out, lhs[1], rhs[0], start=False, stop=False)
    return pe.matmul(out, lhs[0], rhs[0], start=False, stop=last)


def alloc(nc, ctx, phase):
    def sb(name, shape, dt=F32):
        return ctx.enter_context(nc.sbuf_tensor(f"{phase}_{name}", shape, dt))

    def ps(name, shape=(P, 512)):
        return ctx.enter_context(nc.psum_tensor(f"{phase}_{name}", list(shape), F32))

    sems = []

    def sem(name):
        sems.append(nc.alloc_semaphore(f"{phase}_{name}"))
        return sems[-1]

    def clear():
        nc.clear_and_free_semaphores(sems)
        nc.all_engine_barrier()

    ctx.callback(clear)

    return sb, ps, sem


def constants_phase(nc, ident, select, neg_half, eps):
    with ExitStack() as ctx:
        sb, ps, sem = alloc(nc, ctx, "constants")
        filled, shaped = sem("filled"), sem("shaped")
        block = ctx.enter_context(nc.Block())

        @block.gpsimd
        def _(pool):
            pool.memset(ident[:], 0.0)
            pool.memset(select[:], 1.0)
            pool.memset(neg_half[:], -0.5)
            pool.memset(eps[:], EPS).then_inc(filled, 1)
            pool.wait_ge(filled, 1)
            pool.affine_select(out=ident[:], in_=ident[:], compare_op=ALU.not_equal, fill=1.0, base=0,
                               pattern=[[-1, P]], channel_multiplier=1)
            pool.affine_select(out=select[:], in_=select[:], compare_op=ALU.is_ge, fill=0.0, base=0,
                               pattern=[[1, P]], channel_multiplier=-HD).then_inc(shaped, 1)
            pool.wait_ge(shaped, 1)
            pool.affine_select(out=select[:], in_=select[:], compare_op=ALU.is_ge, fill=0.0, base=HD - 1,
                               pattern=[[-1, P]], channel_multiplier=HD).then_inc(shaped, 1)
            pool.wait_ge(shaped, 2)


def condition_phase(nc, cond_t, w_mod, b_mod, gates, mod_t, ident):
    NM = 6 * H
    with ExitStack() as ctx:
        sb, ps, sem = alloc(nc, ctx, "condition")
        c_in = sb("c_in", [P, KC, B])
        c_exp = sb("c_exp", [P, KC, B])
        c_den = sb("c_den", [P, KC, B])
        c_inv = sb("c_inv", [P, KC, B])
        c_silu = sb("c_silu", [P, KC, B])
        wm = sb("wm", [P, 6, KC, H])
        bm = sb("bm", [B, NM])
        rows = sb("rows", [B, NM])
        acc = [ps(f"acc{m}") for m in range(6)]
        cols = ps("cols")
        cond_in, bm_in = sem("cond_in"), sem("bm_in")
        wm_in = [sem(f"wm_in{m}") for m in range(6)]
        exp_done, den_done, inv_done, silu_done = sem("exp_done"), sem("den_done"), sem("inv_done"), sem("silu_done")
        acc_done, rows_done, cols_done, mod_done = sem("acc_done"), sem("rows_done"), sem("cols_done"), sem("mod_done")
        gates_out = sem("gates_out")
        ORDER = [SHIFT_A, SCALE_A, SHIFT_M, SCALE_M, GATE_A, GATE_M]
        block = ctx.enter_context(nc.Block())

        @block.sync
        def _(sp):
            sp.dma_start(c_in[:], cond_t).then_inc(cond_in, 16)
            sp.dma_start(bm[:], b_mod.rearrange("(a n) -> a n", a=1).broadcast_to([B, NM])).then_inc(bm_in, 16)
            for m in ORDER:
                sp.dma_start(wm[:, m], w_mod[:, m * H:(m + 1) * H].rearrange("(k p) n -> p k n", p=P)).then_inc(wm_in[m], 16)
            sp.wait_ge(rows_done, 6)
            for n, m in enumerate((GATE_A, GATE_M)):
                sp.dma_start(gates[n], rows[:, m * H:(m + 1) * H]).then_inc(gates_out, 16)
            sp.wait_ge(gates_out, 32)

        @block.scalar
        def _(act):
            act.wait_ge(cond_in, 16)
            act.activation(c_exp[:], c_in[:], ACT.Exp, scale=-1.0).then_inc(exp_done, 1)

        @block.vector
        def _(dve):
            dve.wait_ge(exp_done, 1)
            dve.tensor_scalar(c_den[:], c_exp[:], 1.0, None, ALU.add).then_inc(den_done, 1)
            dve.wait_ge(den_done, 1)
            dve.reciprocal(c_inv[:], c_den[:]).then_inc(inv_done, 1)
            dve.wait_ge(inv_done, 1)
            dve.tensor_tensor(c_silu[:], c_in[:], c_inv[:], ALU.mult).then_inc(silu_done, 1)
            dve.wait_ge(bm_in, 16)
            for n, m in enumerate(ORDER):
                dve.wait_ge(acc_done, n + 1)
                at = slice(m * H, (m + 1) * H)
                one = 1.0 if m in (SCALE_A, SCALE_M) else 0.0
                dve.scalar_tensor_tensor(out=rows[:, at], in0=acc[m][0:B, :], scalar=one, in1=bm[:, at],
                                         op0=ALU.add, op1=ALU.add).then_inc(rows_done, 1)
            dve.wait_ge(cols_done, 1)
            dve.tensor_copy(mod_t[:], cols[:, 0:4 * KC * B].rearrange("p (m b) -> p m b", b=B)).then_inc(mod_done, 1)
            dve.wait_ge(mod_done, 1)

        @block.tensor
        def _(pe):
            pe.wait_ge(silu_done, 1)
            for m in ORDER:
                pe.wait_ge(wm_in[m], 16)
                for k in range(KC):
                    last = pe.matmul(acc[m][0:B, :], c_silu[:, k], wm[:, m, k], start=k == 0, stop=k == KC - 1)
                last.then_inc(acc_done, 1)
            pe.wait_ge(rows_done, 4)
            for n, m in enumerate((SHIFT_A, SCALE_A, SHIFT_M, SCALE_M)):
                for k in range(KC):
                    at = (n * KC + k) * B
                    last = pe.transpose(cols[:, at:at + B], rows[:, m * H + k * P:m * H + (k + 1) * P], ident[0:B, 0:B])
            last.then_inc(cols_done, 1)


def split_weights(nc, phase, parts):
    RING = 4
    with ExitStack() as ctx:
        sb, ps, sem = alloc(nc, ctx, f"{phase}_split")
        stage = [sb(f"stage{s}", [P, MLP]) for s in range(RING)]
        w_in = [sem(f"w_in{s}") for s in range(RING)]
        high_done, low_done = sem("high_done"), sem("low_done")
        items = [(w, hi, lo, k, c, f) for w, hi, lo, f in parts for k in range(w.shape[0] // P)
                 for c in range(0, w.shape[1], MLP)]
        block = ctx.enter_context(nc.Block())

        def views(item, s):
            w, hi, lo, k, c, f = item
            n = min(MLP, w.shape[1] - c)
            return w[k * P:(k + 1) * P, c:c + n], hi[:, k, c:c + n], lo[:, k, c:c + n], stage[s][:, 0:n], f

        @block.sync
        def _(sp):
            for t, item in enumerate(items):
                src, _, _, st, _ = views(item, t % RING)
                wait(sp, low_done, t - RING + 1)
                sp.dma_start(st, src).then_inc(w_in[t % RING], 16)

        @block.scalar
        def _(act):
            for t, item in enumerate(items):
                _, hi, _, st, f = views(item, t % RING)
                act.wait_ge(w_in[t % RING], 16 * (t // RING + 1))
                act.activation(hi, st, ACT.Identity, scale=f).then_inc(high_done, 1)

        @block.vector
        def _(dve):
            for t, item in enumerate(items):
                _, hi, lo, st, f = views(item, t % RING)
                dve.wait_ge(high_done, t + 1)
                dve.scalar_tensor_tensor(out=lo, in0=st, scalar=f, in1=hi.bitcast(F32), op0=ALU.mult,
                                         op1=ALU.subtract).then_inc(low_done, 1)


def load_columns(nc, phase, pairs):
    with ExitStack() as ctx:
        sb, ps, sem = alloc(nc, ctx, f"{phase}_columns")
        small_in = sem("small_in")
        block = ctx.enter_context(nc.Block())

        @block.sync
        def _(sp):
            for dst, src in pairs:
                sp.dma_start(dst, src).then_inc(small_in, 16)
            sp.wait_ge(small_in, 16 * len(pairs))


def self_phase(nc, x, w_qkv, b_qkv_t, w_proj, b_proj, w_qc, b_qc_t, gates, x1, qc, mod_t, ident, select, neg_half, eps):
    with ExitStack() as ctx:
        sb, ps, sem = alloc(nc, ctx, "self")
        wqkv = [sb(f"wqkv_{s}", [P, KC, 3 * H], F32R) for s in "hl"]
        wproj = [sb(f"wproj_{s}", [P, KC, H], F32R) for s in "hl"]
        wqc = [sb(f"wqc_{s}", [P, KC, H], F32R) for s in "hl"]
        bqkv = sb("bqkv", [P, 3 * KC])
        bqc = sb("bqc", [P, KC])
        bproj = sb("bproj", [QN, H])
        load_columns(nc, "self", [(bqkv[:], b_qkv_t), (bqc[:], b_qc_t), (bproj[:], b_proj.rearrange("(a n) -> a n", a=1).broadcast_to([QN, H]))])
        split_weights(nc, "self", [(w_qkv[:, 0:H], wqkv[0][:, :, 0:H], wqkv[1][:, :, 0:H], SCALE),
                           (w_qkv[:, H:3 * H], wqkv[0][:, :, H:3 * H], wqkv[1][:, :, H:3 * H], 1.0),
                           (w_proj, wproj[0], wproj[1], 1.0), (w_qc, wqc[0], wqc[1], SCALE)])
        x_in = sb("x_in", [QN, QT, H])
        x_res = sb("x_res", [QN, QT, H])
        y = sb("y", [QN, QT, H])
        gate = sb("gate", [QN, H])
        xv = sb("xv", [P, KC, N])
        xT = [sb(f"xT_{s}", [P, KC, N], F32R) for s in "hl"]
        yT = [sb(f"yT_{s}", [P, KC, N], F32R) for s in "hl"]
        nat = [sb(f"nat_{s}", [P, KC, N], F32R) for s in "hl"]
        natq = [sb(f"natq_{s}", [P, KC, N], F32R) for s in "hl"]
        kst = sb("kst", [TERMS * HD, 2, HPG, KC, N], F32R)
        qst = sb("qst", [TERMS * HD, 2, HPG, KC, N], F32R)
        vt = sb("vt", [QN, 2, QT, H])
        pr = sb("pr", [QN, 2, QT, N])
        prT = sb("prT", [QN, HPG, QT, N])
        ou = sb("ou", [P, KC, N])
        nmax = sb("nmax", [QN, 2, QT])
        rsum = sb("rsum", [QN, 2, HPG, QT])
        rinv = sb("rinv", [QN, HPG, QT])
        rT = sb("rT", [HPG, N])
        rb = sb("rb", [P, N])
        bqs, bqcs = sb("bqs", [P, KC]), sb("bqcs", [P, KC])
        st1, st2 = sb("st1", [QN, QT, 6]), sb("st2", [QN, QT, 6])
        turn = sb("turn", [1, 1])
        mv1, mv2 = sb("mv1", [QN, QT, 2]), sb("mv2", [QN, QT, 2])
        ve1, ve2 = sb("ve1", [QN, QT]), sb("ve2", [QN, QT])
        rs1, rs2 = sb("rs1", [QN, QT]), sb("rs2", [QN, QT])
        nm1, nm2 = sb("nm1", [QN, QT]), sb("nm2", [QN, QT])

        sc_ps = [ps(f"sc_ps{i}") for i in range(2)]
        tr_ps = [ps(f"tr_ps{i}") for i in range(2)]
        pj_ps = [ps(f"pj_ps{i}") for i in range(2)]
        tx_ps = ps("tx_ps")
        or_ps = ps("or_ps")
        R0 = 256

        x_loaded, res_loaded, gate_loaded = sem("x_loaded"), sem("res_loaded"), sem("gate_loaded")
        stats1, mvs1, vareps1, rstd1, nmr1, xhat1 = (sem(s) for s in ("stats1", "mvs1", "vareps1", "rstd1", "nmr1", "xhat1"))
        stats2, mvs2, vareps2, rstd2, nmr2, xhat2 = (sem(s) for s in ("stats2", "mvs2", "vareps2", "rstd2", "nmr2", "xhat2"))
        xT_ps, xT_v, xT_h, xT_l = sem("xT_ps"), sem("xT_v"), sem("xT_h"), sem("xT_l")
        k_ps, k_h, k_l = sem("k_ps"), sem("k_h"), sem("k_l")
        q_ps, q_h, q_l = sem("q_ps"), sem("q_h"), sem("q_l")
        c_ps, c_h, c_l = sem("c_ps"), sem("c_h"), sem("c_l")
        v_ps, v_done = sem("v_ps"), sem("v_done")
        k_stacked = [sem(f"k_stacked{p}") for p in range(2)]
        q_stacked = [sem(f"q_stacked{p}") for p in range(2)]
        scored, maxed, exped, pT_ps, pT_done = (sem(s) for s in ("scored", "maxed", "exped", "pT_ps", "pT_done"))
        pv_done, inverted, rT_ps, rT_done, rb_ps, rb_done, o_done = (sem(s) for s in ("pv_done", "inverted", "rT_ps", "rT_done", "rb_ps", "rb_done", "o_done"))
        oT_h, oT_l = sem("oT_h"), sem("oT_l")
        proj_ps, proj_done, gated, summed, x1_out = (sem(s) for s in ("proj_ps", "proj_done", "gated", "summed", "x1_out"))
        yT_ps, yT_h, yT_l = sem("yT_ps"), sem("yT_h"), sem("yT_l")
        qc_out = sem("qc_out")
        bias_scaled = sem("bias_scaled")
        STACK = 16 * HPG * TERMS
        block = ctx.enter_context(nc.Block())

        def bodies(eng, body):
            body(Batch(0), True, True, False, False)
            body(Batch(1), True, True, True, False)
            with eng.Fori(0, (B - 4) // 2) as i:
                body(Batch(2, i), True, True, True, True)
                body(Batch(3, i), True, True, True, True)
            body(Batch(B - 2), True, True, True, True)
            body(Batch(B - 1), True, False, True, True)
            body(Batch(B), False, False, True, True)

        def far(b):
            return not (isinstance(b.i, int) and b.c > B - 3)

        FILL = [[("c", 0, 0), ("c", 0, 1)], [("c", 1, 0)], [("c", 1, 1)], [("k", 0, 0), ("k", 0, 1)],
                [("k", 1, 0)], [("k", 1, 1)], [("p", 0, 0), ("p", 0, 1)], [("p", 1, 0)],
                [("p", 1, 1), ("q", 0, 0)], [("q", 0, 1)], [("q", 1, 0)], [("q", 1, 1), ("v", 0, 0)],
                [("v", 0, 1)], [("ty", 0, 0), ("v", 1, 0)], [("ty", 1, 0), ("v", 1, 1), ("tx", 0, 0)], [("tx", 1, 0)]]

        def fills(b, h, nxt, prv, old):
            of = {"tx": (far(b), 2), "k": (nxt, 1), "q": (nxt, 1), "v": (nxt, 1), "p": (prv, -1), "ty": (prv, -1), "c": (old, -2)}
            return [(kind, c, part, b.plus(of[kind][1])) for kind, c, part in FILL[h] if of[kind][0]]

        @block.sync
        def _(sp):
            def load_x(b):
                wait(sp, xT_ps, b.n(2, 0))
                sp.dma_start(x_in[:], x[bass.ds(b.index(), 1)].rearrange("a (t p) n -> p (a t) n", p=QN)).then_inc(x_loaded, 16)

            def stack(b, low_done, src, dst, sems, terms):
                sp.wait_ge(low_done, b.n(2, 2))
                for j in range(HPG):
                    for r in range(TERMS):
                        sp.dma_start(dst[HD * r:HD * r + HD, b.par, j].bitcast(F32),
                                     src[terms[r]][HD * j:HD * j + HD].bitcast(F32)).then_inc(sems[b.par], 16)

            def load_res(b):
                wait(sp, yT_ps, b.n(2, 0))
                sp.dma_start(x_res[:], x[bass.ds(b.index(), 1)].rearrange("a (t p) n -> p (a t) n", p=QN)).then_inc(res_loaded, 16)
                wait(sp, gated, b.n(2, 0))
                sp.dma_start(gate[:], gates[0, bass.ds(b.index(), 1)].broadcast_to([QN, H])).then_inc(gate_loaded, 16)

            def store_x1(b):
                for t in range(QT):
                    sp.wait_ge(summed, b.n(2, t + 1))
                    sp.dma_start(x1[bass.ds(b.index(), 1), t * QN:(t + 1) * QN].rearrange("a p n -> p (a n)"), y[:, t]).then_inc(x1_out, 16)

            def store_qc(b):
                sp.wait_ge(c_l, b.n(2, 2))
                for s in range(2):
                    sp.dma_start(qc[bass.ds(b.index(), 1), s].rearrange("a (g p) n -> p (a g) n", p=P), natq[s][:].bitcast(F32)).then_inc(qc_out, 16)

            def body(b, att, nxt, prv, old):
                a, z = b.plus(1), b.plus(-1)
                if prv:
                    load_res(z)
                if far(b):
                    load_x(b.plus(2))
                if old:
                    store_qc(b.plus(-2))
                if nxt:
                    stack(a, k_l, nat, kst, k_stacked, (0, 1, 0))
                if prv:
                    store_x1(z)
                if nxt:
                    stack(a, q_l, natq, qst, q_stacked, (0, 0, 1))

            load_x(Batch(0))
            load_x(Batch(1))
            stack(Batch(0), k_l, nat, kst, k_stacked, (0, 1, 0))
            stack(Batch(0), q_l, natq, qst, q_stacked, (0, 0, 1))
            bodies(sp, body)
            store_qc(Batch(B - 1))
            sp.wait_ge(x1_out, 32 * B)
            sp.wait_ge(qc_out, 32 * B)

        @block.tensor
        def _(pe):
            def trans(src, c, ready, b, done):
                pe.wait_ge(ready, b.n(1, 1))
                for k in range(2):
                    for t in range(QT):
                        at = k * N + t * QN
                        last = pe.transpose(tx_ps[:, at:at + QN], src[:, t, (2 * c + k) * P:(2 * c + k + 1) * P], ident[0:QN, 0:QN])
                last.then_inc(done, 1)

            def channels(c, m, w, first_chunk, src, done):
                at = (first_chunk + m) * P
                for k in range(KC):
                    last = product(pe, pj_ps[c][:, m * N:(m + 1) * N], (w[0][:, k, at:at + P], w[1][:, k, at:at + P]),
                                   (src[0][:, k], src[1][:, k]), k == 0, k == KC - 1)
                if m == 1:
                    last.then_inc(done, 1)

            def tokens(t, part, w, at, src, done):
                for k in range(2 * part, 2 * part + 2):
                    last = product(pe, pj_ps[t][0:QN, :], tuple(s[:, k, t * QN:(t + 1) * QN] for s in src),
                                   (w[0][:, k, at:at + H], w[1][:, k, at:at + H]), k == 0, k == KC - 1)
                if part == 1:
                    last.then_inc(done, 1)

            def score(b, h):
                if h == 0:
                    pe.wait_ge(k_stacked[b.par], b.pair(STACK, STACK))
                    pe.wait_ge(q_stacked[b.par], b.pair(STACK, STACK))
                wait(pe, exped, b.n(NH, h - 1))
                g, j = h // HPG, h % HPG
                for t in range(QT):
                    last = pe.matmul(sc_ps[h % 2][0:QN, t * N:(t + 1) * N], qst[:, b.par, j, g, t * QN:(t + 1) * QN],
                                     kst[:, b.par, j, g, :], start=True, stop=True)
                last.then_inc(scored, 1)

            def trans_p(b, h):
                pe.wait_ge(exped, b.n(NH, h + 1))
                wait(pe, pT_done, b.n(NH, h - 1))
                for kt in range(QT):
                    for t in range(QT):
                        at = kt * N + t * QN
                        last = pe.transpose(tr_ps[h % 2][0:QN, at:at + QN], pr[:, h % 2, t, kt * QN:(kt + 1) * QN], ident[0:QN, 0:QN])
                last.then_inc(pT_ps, 1)

            def pv(b, g):
                pe.wait_ge(pT_done, b.n(NH, HPG * g + HPG))
                if g == 0:
                    pe.wait_ge(v_done, b.n(2, 2))
                wait(pe, o_done, b.n(KC, g))
                for kt in range(QT):
                    for j in range(HPG):
                        ch = g * P + j * HD
                        last = pe.matmul(or_ps[HD * j:HD * j + HD, 0:N], vt[:, b.par, kt, ch:ch + HD], prT[:, j, kt],
                                         start=kt == 0, stop=kt == QT - 1)
                last.then_inc(pv_done, 1)
                pe.wait_ge(inverted, b.n(KC, g + 1))
                for t in range(QT):
                    last = pe.transpose(or_ps[0:HPG, R0 + t * QN:R0 + (t + 1) * QN], rinv[:, :, t], ident[0:QN, 0:QN])
                last.then_inc(rT_ps, 1)

            def spread(b, g):
                pe.wait_ge(rT_done, b.n(KC, g + 1))
                pe.matmul(or_ps[:, R0:R0 + N], select[:], rT[:], start=True, stop=True).then_inc(rb_ps, 1)

            def fill(kind, c, part, o, b, att, nxt, prv, old):
                a, z, y2 = b.plus(1), b.plus(-1), b.plus(-2)
                if kind == "tx":
                    if c == 0 and prv:
                        pe.wait_ge(yT_l, z.n(2, 2))
                    elif c == 0:
                        pe.wait_ge(xT_v, o.n(2, 0))
                    else:
                        pe.wait_ge(xT_v, o.n(2, 1))
                    trans(x_in, c, xhat1, o, xT_ps)
                if kind == "ty":
                    if c == 0 and nxt:
                        pe.wait_ge(xT_v, a.n(2, 2))
                    elif c == 0:
                        pe.wait_ge(yT_l, o.n(2, 0))
                    else:
                        pe.wait_ge(yT_l, o.n(2, 1))
                    trans(x_res, c, xhat2, o, yT_ps)
                if kind == "c":
                    if part == 0:
                        if att:
                            pe.wait_ge(v_done, b.n(2, c + 1))
                        pe.wait_ge(yT_l, o.n(2, 2))
                    channels(c, part, wqc, 2 * c, yT, c_ps)
                if kind == "k":
                    if part == 0:
                        if old:
                            pe.wait_ge(c_l, y2.n(2, c + 1))
                        else:
                            pe.wait_ge(v_done, b.n(2, c + 1))
                        pe.wait_ge(xT_l, o.n(1, 1))
                    channels(c, part, wqkv, KC + 2 * c, xT, k_ps)
                if kind == "p":
                    if part == 0:
                        if nxt:
                            pe.wait_ge(k_l, a.n(2, c + 1))
                        else:
                            pe.wait_ge(c_l, y2.n(2, c + 1))
                        pe.wait_ge(oT_l, o.n(KC, KC))
                    tokens(c, part, wproj, 0, yT, proj_ps)
                if kind == "q":
                    if part == 0:
                        if prv:
                            pe.wait_ge(proj_done, z.n(2, c + 1))
                        else:
                            pe.wait_ge(k_l, o.n(2, c + 1))
                    channels(c, part, wqkv, 2 * c, xT, q_ps)
                if kind == "v":
                    if part == 0:
                        pe.wait_ge(q_l, o.n(2, c + 1))
                    tokens(c, part, wqkv, 2 * H, xT, v_ps)

            def body(b, att, nxt, prv, old):
                a, z = b.plus(1), b.plus(-1)
                for h in range(NH):
                    if h == 1 and prv:
                        pv(z, KC - 1)
                    if h % HPG == 1 and h > 1 and att:
                        pv(b, h // HPG - 1)
                    if h == 2 and prv:
                        spread(z, KC - 1)
                    if h % HPG == 2 and h > 2 and att:
                        spread(b, h // HPG - 1)
                    if h > 0 and att:
                        trans_p(b, h - 1)
                    if h == 0 and prv:
                        trans_p(z, NH - 1)
                    for kind, c, part, o in fills(b, h, nxt, prv, old):
                        fill(kind, c, part, o, b, att, nxt, prv, old)
                    if h < NH - 1 and att:
                        score(b, h + 1)
                    if h == NH - 1 and nxt:
                        score(a, 0)

            a = Batch(0)
            for c in range(2):
                wait(pe, xT_v, c)
                trans(x_in, c, xhat1, a, xT_ps)
            pe.wait_ge(xT_l, 1)
            for c in range(2):
                for m in range(2):
                    channels(c, m, wqkv, KC + 2 * c, xT, k_ps)
            for c in range(2):
                pe.wait_ge(k_l, c + 1)
                for m in range(2):
                    channels(c, m, wqkv, 2 * c, xT, q_ps)
            for c in range(2):
                pe.wait_ge(q_l, c + 1)
                for part in range(2):
                    tokens(c, part, wqkv, 2 * H, xT, v_ps)
            for c in range(2):
                pe.wait_ge(xT_v, 2 + c)
                trans(x_in, c, xhat1, a.plus(1), xT_ps)
            score(a, 0)
            bodies(pe, body)
            for c in range(2):
                pe.wait_ge(c_l, 2 * (B - 1) + c)
                for m in range(2):
                    if m == 0 and c == 0:
                        pe.wait_ge(yT_l, 2 * B)
                    channels(c, m, wqc, 2 * c, yT, c_ps)

        @block.vector
        def _(dve):
            def stats(b, src, ready, value, st, mv, s_stats, s_mv):
                for t in range(QT):
                    dve.wait_ge(ready, value(t))
                    last = dve.bn_stats(st[:, t], src[:, t])
                last.then_inc(s_stats, 1)
                dve.wait_ge(s_stats, b.n(1, 1))
                dve.memset(turn[:], 0.0)
                for t in range(QT):
                    last = dve.bn_aggr(mv[:, t], st[:, t])
                last.then_inc(s_mv, 1)

            def neg_mean(b, mv, rs, nm, s_rstd, s_nmr):
                dve.wait_ge(s_rstd, b.n(1, 1))
                dve.scalar_tensor_tensor(out=nm[:], in0=mv[:, :, 0], scalar=-1.0, in1=rs[:], op0=ALU.mult, op1=ALU.mult).then_inc(s_nmr, 1)

            def modulate(b, c):
                if c == 0:
                    wait(dve, xT_l, b.n(1, 0))
                dve.wait_ge(xT_ps, b.n(2, c + 1))
                for k in range(2):
                    m = 2 * c + k
                    last = dve.tensor_scalar(xv[:, m], tx_ps[:, k * N:(k + 1) * N], mod_t[:, KC + m, bass.ds(b.index(), 1)],
                                             mod_t[:, m, bass.ds(b.index(), 1)], ALU.mult, ALU.add)
                last.then_inc(xT_v, 1)

            def lows(b, c, high, low, bias, first_chunk, dst=nat):
                dve.wait_ge(high, b.n(2, c + 1))
                for m in range(2):
                    last = dve.scalar_tensor_tensor(out=dst[1][:, 2 * c + m], in0=pj_ps[c][:, m * N:(m + 1) * N],
                                                    scalar=bias[:, first_chunk + m:first_chunk + m + 1],
                                                    in1=dst[0][:, 2 * c + m].bitcast(F32), op0=ALU.add, op1=ALU.subtract)
                last.then_inc(low, 1)

            def add_bias(b, t):
                dve.wait_ge(proj_ps, b.n(2, t + 1))
                wait(dve, x1_out, b.n(32, 0))
                dve.tensor_tensor(y[:, t], pj_ps[t][0:QN, :], bproj[:], ALU.add).then_inc(proj_done, 1)

            def low_o(b):
                for g in range(KC):
                    dve.wait_ge(oT_h, b.n(KC, g + 1))
                    dve.scalar_tensor_tensor(out=yT[1][:, g], in0=ou[:, g], scalar=bqkv[:, 2 * KC + g:2 * KC + g + 1],
                                             in1=yT[0][:, g].bitcast(F32), op0=ALU.add, op1=ALU.subtract).then_inc(oT_l, 1)

            def low_y(b, c):
                dve.wait_ge(yT_h, b.n(2, c + 1))
                dve.tensor_tensor(yT[1][:, 2 * c:2 * c + 2], tx_ps[:, 0:2 * N].rearrange("p (m n) -> p m n", m=2),
                                  yT[0][:, 2 * c:2 * c + 2].bitcast(F32), ALU.subtract).then_inc(yT_l, 1)

            def row_max(b, h):
                dve.wait_ge(scored, b.n(NH, h + 1))
                wait(dve, exped, b.n(NH, h - 1))
                dve.tensor_reduce(nmax[:, h % 2], sc_ps[h % 2][0:QN, 0:QT * N].rearrange("p (t k) -> p t k", t=QT), AX_X, ALU.max,
                                  negate=True).then_inc(maxed, 1)

            def copy_p(b, h):
                dve.wait_ge(pT_ps, b.n(NH, h + 1))
                if h % HPG == 0:
                    wait(dve, pv_done, b.n(KC, h // HPG))
                dve.tensor_copy(prT[:, h % HPG], tr_ps[h % 2][0:QN, 0:QT * N].rearrange("p (k t) -> p k t", k=QT)).then_inc(pT_done, 1)

            def invert(b, g):
                dve.wait_ge(exped, b.n(NH, HPG * g + HPG))
                wait(dve, rT_ps, b.n(KC, g))
                dve.reciprocal(rinv[:], rsum[:, g % 2]).then_inc(inverted, 1)

            def normalize(b, g):
                dve.wait_ge(rb_done, b.n(KC, g + 1))
                dve.wait_ge(pv_done, b.n(KC, g + 1))
                if g == 0:
                    wait(dve, oT_l, b.n(KC, 0))
                dve.tensor_tensor(ou[:, g], or_ps[:, 0:N], rb[:], ALU.mult).then_inc(o_done, 1)

            def body(b, att, nxt, prv, old):
                a, z, far_b = b.plus(1), b.plus(-1), b.plus(2)
                for h in range(NH):
                    if h == 0 and prv:
                        invert(z, KC - 1)
                    if h % HPG == 0 and h > 0 and att:
                        invert(b, h // HPG - 1)
                    if h > 0 and att:
                        copy_p(b, h - 1)
                    if h == 0 and prv:
                        copy_p(z, NH - 1)
                    for kind, c, part, o in fills(b, h, nxt, prv, old):
                        if kind == "tx":
                            modulate(o, c)
                        if kind == "ty":
                            low_y(o, c)
                        if kind == "p" and part == 1:
                            add_bias(o, c)
                    if h == 3 and prv:
                        normalize(z, KC - 1)
                    if h % HPG == 3 and h > 3 and att:
                        normalize(b, h // HPG - 1)
                    if h < NH - 1 and att:
                        row_max(b, h + 1)
                    if h == NH - 1 and nxt:
                        row_max(a, 0)
                    for kind, c, part, o in fills(b, h, nxt, prv, old):
                        if kind == "k" and part == 1:
                            lows(o, c, k_h, k_l, bqkv, KC + 2 * c)
                        if kind == "q" and part == 1:
                            lows(o, c, q_h, q_l, bqs, 2 * c, natq)
                        if kind == "c" and part == 1:
                            lows(o, c, c_h, c_l, bqcs, 2 * c, natq)
                    if prv and h == 4:
                        low_o(z)
                    if far(b) and h == 5:
                        stats(far_b, x_in, x_loaded, lambda t: far_b.n(16, 16), st1, mv1, stats1, mvs1)
                    if far(b) and h == 7:
                        neg_mean(far_b, mv1, rs1, nm1, rstd1, nmr1)
                    if prv and h == 10:
                        stats(z, y, summed, lambda t: z.n(2, t + 1), st2, mv2, stats2, mvs2)
                    if prv and h == 11:
                        neg_mean(z, mv2, rs2, nm2, rstd2, nmr2)

            dve.tensor_scalar(bqs[:], bqkv[:, 0:KC], SCALE, None, ALU.mult)
            dve.tensor_scalar(bqcs[:], bqc[:], SCALE, None, ALU.mult).then_inc(bias_scaled, 1)
            dve.wait_ge(bias_scaled, 1)
            a = Batch(0)
            stats(a, x_in, x_loaded, lambda t: 16, st1, mv1, stats1, mvs1)
            neg_mean(a, mv1, rs1, nm1, rstd1, nmr1)
            for c in range(2):
                modulate(a, c)
            for c in range(2):
                lows(a, c, k_h, k_l, bqkv, KC + 2 * c)
            for c in range(2):
                lows(a, c, q_h, q_l, bqs, 2 * c, natq)
            stats(a.plus(1), x_in, x_loaded, lambda t: 32, st1, mv1, stats1, mvs1)
            neg_mean(a.plus(1), mv1, rs1, nm1, rstd1, nmr1)
            for c in range(2):
                modulate(a.plus(1), c)
            row_max(a, 0)
            bodies(dve, body)
            for c in range(2):
                lows(Batch(B - 1), c, c_h, c_l, bqcs, 2 * c, natq)

        @block.scalar
        def _(act):
            def apply_ln(b, src, dst, rs, nm, s_nmr, s_out):
                act.wait_ge(s_nmr, b.n(1, 1))
                for t in range(QT):
                    last = act.activation(dst[:, t], src[:, t], ACT.Identity, bias=nm[:, t:t + 1], scale=rs[:, t:t + 1])
                last.then_inc(s_out, 1)

            def high_x(b):
                act.wait_ge(xT_v, b.n(2, 2))
                wait(act, v_ps, b.n(2, 0))
                act.copy(xT[0][:], xv[:]).then_inc(xT_h, 1)

            def highs(b, c, ready, high, bias, first_chunk, dst=nat):
                act.wait_ge(ready, b.n(2, c + 1))
                for m in range(2):
                    last = act.activation(dst[0][:, 2 * c + m], pj_ps[c][:, m * N:(m + 1) * N], ACT.Identity,
                                          bias=bias[:, first_chunk + m:first_chunk + m + 1])
                last.then_inc(high, 1)

            def copy_v(b, t):
                act.wait_ge(v_ps, b.n(2, t + 1))
                wait(act, pv_done, b.n(KC, -KC))
                act.copy(vt[:, b.par, t], pj_ps[t][0:QN, :]).then_inc(v_done, 1)

            def exps(b, h):
                act.wait_ge(maxed, b.n(NH, h + 1))
                wait(act, pT_ps, b.n(NH, h - 1))
                if h % HPG == 0:
                    wait(act, inverted, b.n(KC, h // HPG - 1))
                for t in range(QT):
                    last = act.activation(pr[:, h % 2, t], sc_ps[h % 2][0:QN, t * N:(t + 1) * N], ACT.Exp,
                                          bias=nmax[:, h % 2, t:t + 1], accum_out=rsum[:, (h // HPG) % 2, h % HPG, t:t + 1])
                last.then_inc(exped, 1)

            def copy_rT(b, g):
                act.wait_ge(rT_ps, b.n(KC, g + 1))
                wait(act, rb_ps, b.n(KC, g))
                act.copy(rT[:], or_ps[0:HPG, R0:R0 + N]).then_inc(rT_done, 1)

            def copy_rb(b, g):
                act.wait_ge(rb_ps, b.n(KC, g + 1))
                wait(act, o_done, b.n(KC, g))
                act.copy(rb[:], or_ps[:, R0:R0 + N]).then_inc(rb_done, 1)

            def highs_o(b):
                wait(act, c_ps, b.n(2, 0))
                for g in range(KC):
                    act.wait_ge(o_done, b.n(KC, g + 1))
                    act.activation(yT[0][:, g], ou[:, g], ACT.Identity, bias=bqkv[:, 2 * KC + g:2 * KC + g + 1]).then_inc(oT_h, 1)

            def highs_y(b, c):
                act.wait_ge(proj_ps, b.n(2, 2))
                act.wait_ge(yT_ps, b.n(2, c + 1))
                act.copy(yT[0][:, 2 * c:2 * c + 2], tx_ps[:, 0:2 * N].rearrange("p (m n) -> p m n", m=2)).then_inc(yT_h, 1)

            def body(b, att, nxt, prv, old):
                a, z = b.plus(1), b.plus(-1)
                for h in range(NH):
                    if h == 1 and prv:
                        copy_rT(z, KC - 1)
                    if h % HPG == 1 and h > 1 and att:
                        copy_rT(b, h // HPG - 1)
                    if h == 2 and prv:
                        copy_rb(z, KC - 1)
                    if h % HPG == 2 and h > 2 and att:
                        copy_rb(b, h // HPG - 1)
                    for kind, c, part, o in fills(b, h, nxt, prv, old):
                        if kind == "ty":
                            highs_y(o, c)
                        if kind == "k" and part == 1:
                            if c == 0:
                                act.wait_ge(k_stacked[b.par], b.pair(STACK, STACK))
                            highs(o, c, k_ps, k_h, bqkv, KC + 2 * c)
                        if kind == "q" and part == 1:
                            if c == 0 and old:
                                act.wait_ge(qc_out, b.plus(-2).n(32, 32))
                            elif c == 0:
                                act.wait_ge(q_stacked[b.par], b.pair(STACK, STACK))
                            highs(o, c, q_ps, q_h, bqs, 2 * c, natq)
                        if kind == "c" and part == 1:
                            if c == 0 and att:
                                act.wait_ge(q_stacked[b.par], b.pair(STACK, STACK))
                            if c == 0 and not att:
                                act.wait_ge(qc_out, o.n(32, 0))
                            highs(o, c, c_ps, c_h, bqcs, 2 * c, natq)
                        if kind == "v" and part == 1:
                            copy_v(o, c)
                    if h < NH - 1 and att:
                        exps(b, h + 1)
                    if h == NH - 1 and nxt:
                        exps(a, 0)
                    if far(b) and h == 15:
                        high_x(b.plus(2))
                    if prv and h == 3:
                        highs_o(z)
                    if far(b) and h == 8:
                        apply_ln(b.plus(2), x_in, x_in, rs1, nm1, nmr1, xhat1)
                    if prv and h == 11:
                        apply_ln(z, y, x_res, rs2, nm2, nmr2, xhat2)

            act.wait_ge(bias_scaled, 1)
            a = Batch(0)
            apply_ln(a, x_in, x_in, rs1, nm1, nmr1, xhat1)
            high_x(a)
            for c in range(2):
                highs(a, c, k_ps, k_h, bqkv, KC + 2 * c)
            for c in range(2):
                highs(a, c, q_ps, q_h, bqs, 2 * c, natq)
            copy_v(a, 0)
            copy_v(a, 1)
            apply_ln(a.plus(1), x_in, x_in, rs1, nm1, nmr1, xhat1)
            high_x(a.plus(1))
            exps(a, 0)
            bodies(act, body)
            act.wait_ge(qc_out, 32 * (B - 1))
            for c in range(2):
                highs(Batch(B - 1), c, c_ps, c_h, bqcs, 2 * c, natq)

        @block.gpsimd
        def _(pool):
            def rstd(b, mv, ve, rs, s_mv, s_ve, s_rstd):
                pool.wait_ge(s_mv, b.n(1, 1))
                pool.tensor_tensor(ve[:], mv[:, :, 1], eps[0:QN, 0:QT], ALU.add).then_inc(s_ve, 1)
                pool.wait_ge(s_ve, b.n(1, 1))
                pool.tensor_tensor(rs[:], ve[:], neg_half[0:QN, 0:QT], ALU.pow).then_inc(s_rstd, 1)

            def low_x(b):
                pool.wait_ge(xT_h, b.n(1, 1))
                pool.tensor_tensor(xT[1][:], xv[:], xT[0][:].bitcast(F32), ALU.subtract).then_inc(xT_l, 1)

            def residual(b, t):
                if t == 0:
                    pool.wait_ge(gate_loaded, b.n(16, 16))
                    pool.wait_ge(res_loaded, b.n(16, 16))
                pool.wait_ge(proj_done, b.n(2, t + 1))
                pool.tensor_tensor(y[:, t], y[:, t], gate[:], ALU.mult).then_inc(gated, 1)
                pool.wait_ge(gated, b.n(2, t + 1))
                pool.tensor_tensor(y[:, t], y[:, t], x_res[:, t], ALU.add).then_inc(summed, 1)

            def body(b, att, nxt, prv, old):
                a, z = b.plus(1), b.plus(-1)
                if far(b):
                    rstd(b.plus(2), mv1, ve1, rs1, mvs1, vareps1, rstd1)
                if prv:
                    for t in range(QT):
                        residual(z, t)
                    rstd(z, mv2, ve2, rs2, mvs2, vareps2, rstd2)
                if far(b):
                    low_x(b.plus(2))

            a = Batch(0)
            rstd(a, mv1, ve1, rs1, mvs1, vareps1, rstd1)
            low_x(a)
            rstd(a.plus(1), mv1, ve1, rs1, mvs1, vareps1, rstd1)
            low_x(a.plus(1))
            bodies(pool, body)


def cross_phase(nc, ctx_in_dram, w_kvc, b_kvc_t, qc, o_dram, ident, select, neg_half, eps):
    with ExitStack() as ctx:
        sb, ps, sem = alloc(nc, ctx, "cross")
        wkv = [sb(f"wkv_{s}", [P, KC, 2 * H], F32R) for s in "hl"]
        bkv = sb("bkv", [P, 2 * KC])
        load_columns(nc, "cross", [(bkv[:], b_kvc_t)])
        split_weights(nc, "cross", [(w_kvc, wkv[0], wkv[1], 1.0)])
        kst = sb("kst", [TERMS * HD, KC, HPG, S], F32R)
        qst = sb("qst", [TERMS * HD, KC, HPG, N], F32R)
        nat = [sb(f"nat_{s}", [P, 2, S], F32R) for s in "hl"]
        cT = [sb(f"cT_{s}", [P, KC, S], F32R) for s in "hl"]
        vt = sb("vt", [SN, 2, ST, H])
        c_in = sb("c_in", [SN, ST, H])
        pr = sb("pr", [QN, 2, QT, S])
        prT = sb("prT", [SN, HPG, ST, N])
        ou = sb("ou", [P, 2, N])
        nmax = sb("nmax", [QN, 2, QT])
        rsum = sb("rsum", [QN, 2, HPG, QT])
        rinv = sb("rinv", [QN, HPG, QT])
        rT = sb("rT", [HPG, N])
        rb = sb("rb", [P, N])
        st = sb("st", [SN, ST, 6])
        turn = sb("turn", [1, 1])
        mv = sb("mv", [SN, ST, 2])
        ve, rs, nm = sb("ve", [SN, ST]), sb("rs", [SN, ST]), sb("nm", [SN, ST])

        sc_ps = [ps(f"sc_ps{i}", (P, 1024)) for i in range(QT)]
        tr_ps = [ps(f"tr_ps{i}") for i in range(2)]
        pj_ps = ps("pj_ps")
        or_ps = ps("or_ps")
        SC0 = 512 - SHALF[0]
        R0 = 256

        c_loaded, stats_done, mvs, vareps, rstd, nmr, chat = (sem(s) for s in ("c_loaded", "stats_done", "mvs", "vareps", "rstd", "nmr", "chat"))
        cT_ps, cT_h, cT_l = sem("cT_ps"), sem("cT_h"), sem("cT_l")
        k_ps, k_h, k_l = sem("k_ps"), sem("k_h"), sem("k_l")
        v_ps, v_done = sem("v_ps"), sem("v_done")
        k_stacked = [sem(f"k_stacked{g}") for g in range(KC)]
        q_stacked = [sem(f"q_stacked{g}") for g in range(KC)]
        scored_t = [sem(f"scored_t{t}") for t in range(QT)]
        maxed, exped, pT_ps = sem("maxed"), sem("exped"), sem("pT_ps")
        pT_dve, pT_act = sem("pT_dve"), sem("pT_act")
        pv_done, inverted, rT_ps, rT_done, rb_ps, rb_done, o_done = (sem(s) for s in ("pv_done", "inverted", "rT_ps", "rT_done", "rb_ps", "rb_done", "o_done"))
        o_out = [sem(f"o_out{i}") for i in range(2)]
        STACK, QSTACK = 16 * HPG * TERMS, 16 * TERMS
        HALVES = ((0, SHALF[0]), (SHALF[0], SHALF[1]))
        FILL = [[("c", 0), ("c", 1)], [("c", 2), ("c", 3)], [("c", 4), ("c", 5)], [("v", 0)],
                [("k", 0, 0)], [("k", 0, 1)], [("v", 1)], [("k", 1, 0)], [("k", 1, 1)], [("k", 2, 0)],
                [("k", 2, 1), ("v", 2)], [("v", 3)], [("k", 3, 0)], [("k", 3, 1)], [("v", 4)], [("v", 5)]]
        ORDER = [f for step in FILL for f in step]
        block = ctx.enter_context(nc.Block())

        def bodies(eng, body):
            body(Batch(0), True, True, False)
            body(Batch(1), True, True, True)
            with eng.Fori(0, (B - 4) // 2) as i:
                body(Batch(2, i), True, True, True)
                body(Batch(3, i), True, True, True)
            body(Batch(B - 2), True, True, True)
            body(Batch(B - 1), True, False, True)
            body(Batch(B), False, False, True)

        def bank_free(eng, b, fill):
            at = ORDER.index(fill)
            if at == 0:
                wait(eng, v_done, b.n(ST, 0))
                return
            kind, *where = ORDER[at - 1]
            if kind == "c":
                eng.wait_ge(cT_l, b.n(ST, where[0] + 1))
            elif kind == "k":
                eng.wait_ge(k_l, b.n(2 * KC, 2 * where[0] + where[1] + 1))
            else:
                eng.wait_ge(v_done, b.n(ST, where[0] + 1))

        def far(b):
            return not (isinstance(b.i, int) and b.c > B - 3)

        @block.sync
        def _(sp):
            def load_c(b):
                wait(sp, cT_ps, b.n(ST, 0))
                sp.dma_start(c_in[:], ctx_in_dram[bass.ds(b.index(), 1)].rearrange("a (t p) n -> p (a t) n", p=SN)).then_inc(c_loaded, 16)

            def load_q(b, g):
                wait(sp, scored_t[QT - 1], b.n(NH, HPG * (g + 1) - NH))
                for r, s in enumerate((0, 0, 1)):
                    src = qc[bass.ds(b.index(), 1), s, g * P:(g + 1) * P].rearrange("a (j d) t -> d (a j) t", d=HD)
                    sp.dma_start(qst[HD * r:HD * r + HD, g].bitcast(F32), src).then_inc(q_stacked[g], 16)

            def stack_k(b, g):
                sp.wait_ge(k_l, b.n(2 * KC, 2 * g + 2))
                wait(sp, scored_t[QT - 1], b.n(NH, HPG * (g + 1) - NH))
                for j in range(HPG):
                    for r, s in enumerate((0, 1, 0)):
                        sp.dma_start(kst[HD * r:HD * r + HD, g, j].bitcast(F32),
                                     nat[s][HD * j:HD * j + HD, g % 2].bitcast(F32)).then_inc(k_stacked[g], 16)

            def body(b, att, nxt, prv):
                a = b.plus(1)
                if far(b):
                    load_c(b.plus(2))
                for g in range(KC):
                    if nxt:
                        load_q(a, g)
                        stack_k(a, g)

            load_c(Batch(0))
            load_c(Batch(1))
            for g in range(KC):
                load_q(Batch(0), g)
            for g in range(KC):
                stack_k(Batch(0), g)
            bodies(sp, body)

        @block.tensor
        def _(pe):
            def fill_(b, fill):
                bank_free(pe, b, fill)
                kind, *where = fill
                if kind == "c":
                    t, = where
                    pe.wait_ge(chat, b.n(ST, t + 1))
                    for k in range(KC):
                        last = pe.transpose(pj_ps[:, k * SN:(k + 1) * SN], c_in[:, t, k * P:(k + 1) * P], ident[0:SN, 0:SN])
                    last.then_inc(cT_ps, 1)
                elif kind == "k":
                    g, half = where
                    pe.wait_ge(cT_l, b.n(ST, ST))
                    c0, cn = HALVES[half]
                    for k in range(KC):
                        last = product(pe, pj_ps[:, 0:cn], tuple(w[:, k, g * P:(g + 1) * P] for w in wkv),
                                       tuple(c[:, k, c0:c0 + cn] for c in cT), k == 0, k == KC - 1)
                    last.then_inc(k_ps, 1)
                else:
                    t, = where
                    pe.wait_ge(cT_l, b.n(ST, ST))
                    for k in range(KC):
                        last = product(pe, pj_ps[0:SN, :], tuple(c[:, k, t * SN:(t + 1) * SN] for c in cT),
                                       tuple(w[:, k, H:2 * H] for w in wkv), k == 0, k == KC - 1)
                    last.then_inc(v_ps, 1)

            def score(b, h):
                g, j = h // HPG, h % HPG
                if j == 0:
                    pe.wait_ge(k_stacked[g], b.n(STACK, STACK))
                    pe.wait_ge(q_stacked[g], b.n(QSTACK, QSTACK))
                for t in range(QT):
                    wait(pe, exped, b.n(NH * QT, h * QT + t - 1))
                    for c0, cn in HALVES:
                        last = pe.matmul(sc_ps[t][0:QN, SC0 + c0:SC0 + c0 + cn], qst[:, g, j, t * QN:(t + 1) * QN],
                                         kst[:, g, j, c0:c0 + cn], start=True, stop=True)
                    last.then_inc(scored_t[t], 1)

            def trans_p(b, h, c):
                if c == 0:
                    pe.wait_ge(exped, b.n(NH * QT, (h + 1) * QT))
                    wait(pe, pT_act, b.n(2 * NH, 2 * h - 1))
                if c == 1:
                    wait(pe, pT_act, b.n(2 * NH, 2 * h))
                if c == 2:
                    pe.wait_ge(pT_dve, b.n(NH, h + 1))
                for m in range(2):
                    for t in range(QT):
                        at = m * N + t * QN
                        kt = 2 * c + m
                        last = pe.transpose(tr_ps[(3 * h + c) % 2][0:SN, at:at + QN], pr[:, h % 2, t, kt * SN:(kt + 1) * SN], ident[0:QN, 0:QN])
                last.then_inc(pT_ps, 1)

            def pv(b, g):
                pe.wait_ge(pT_dve, b.n(NH, HPG * (g + 1)))
                pe.wait_ge(pT_act, b.n(2 * NH, 2 * HPG * (g + 1)))
                if g == 0:
                    pe.wait_ge(v_done, b.n(ST, ST))
                wait(pe, o_done, b.n(KC, g))
                for kt in range(ST):
                    for j in range(HPG):
                        ch = g * P + j * HD
                        last = pe.matmul(or_ps[HD * j:HD * j + HD, 0:N], vt[:, b.par, kt, ch:ch + HD], prT[:, j, kt],
                                         start=kt == 0, stop=kt == ST - 1)
                last.then_inc(pv_done, 1)
                pe.wait_ge(inverted, b.n(KC, g + 1))
                for t in range(QT):
                    last = pe.transpose(or_ps[0:HPG, R0 + t * QN:R0 + (t + 1) * QN], rinv[:, :, t], ident[0:QN, 0:QN])
                last.then_inc(rT_ps, 1)

            def spread(b, g):
                pe.wait_ge(rT_done, b.n(KC, g + 1))
                pe.matmul(or_ps[:, R0:R0 + N], select[:], rT[:], start=True, stop=True).then_inc(rb_ps, 1)

            def body(b, att, nxt, prv):
                a, z = b.plus(1), b.plus(-1)
                for h in range(NH):
                    if h == 1 and prv:
                        pv(z, KC - 1)
                    if h % HPG == 1 and h > 1 and att:
                        pv(b, h // HPG - 1)
                    for c in range(ST // 2):
                        if c == 2 and nxt:
                            fill_(a, FILL[h][0])
                        if h > 0 and att:
                            trans_p(b, h - 1, c)
                        if h == 0 and prv:
                            trans_p(z, NH - 1, c)
                    if nxt and len(FILL[h]) > 1:
                        fill_(a, FILL[h][1])
                    if h == 2 and prv:
                        spread(z, KC - 1)
                    if h % HPG == 2 and h > 2 and att:
                        spread(b, h // HPG - 1)
                    if h < NH - 1 and att:
                        score(b, h + 1)
                    if h == NH - 1 and nxt:
                        score(a, 0)

            for f in ORDER:
                fill_(Batch(0), f)
            score(Batch(0), 0)
            bodies(pe, body)

        @block.vector
        def _(dve):
            def stats(b, t):
                if t == 0:
                    dve.wait_ge(c_loaded, b.n(16, 16))
                dve.bn_stats(st[:, t], c_in[:, t]).then_inc(stats_done, 1)

            def aggregate(b, half):
                at = range(3 * half, 3 * half + 3)
                dve.wait_ge(stats_done, b.n(ST, 3 * half + 3))
                dve.memset(turn[:], 0.0)
                for t in at:
                    last = dve.bn_aggr(mv[:, t], st[:, t])
                last.then_inc(mvs, 1)

            def neg_mean(b, half):
                dve.wait_ge(rstd, b.n(2, half + 1))
                at = slice(3 * half, 3 * half + 3)
                dve.scalar_tensor_tensor(out=nm[:, at], in0=mv[:, at, 0], scalar=-1.0, in1=rs[:, at], op0=ALU.mult, op1=ALU.mult).then_inc(nmr, 1)

            def low(b, fill):
                kind, *where = fill
                if kind == "c":
                    t, = where
                    dve.wait_ge(cT_h, b.n(ST, t + 1))
                    at = slice(t * SN, (t + 1) * SN)
                    dve.tensor_tensor(cT[1][:, :, at], pj_ps[:, 0:KC * SN].rearrange("p (k n) -> p k n", k=KC),
                                      cT[0][:, :, at].bitcast(F32), ALU.subtract).then_inc(cT_l, 1)
                if kind == "k":
                    g, half = where
                    c0, cn = HALVES[half]
                    dve.wait_ge(k_h, b.n(2 * KC, 2 * g + half + 1))
                    dve.scalar_tensor_tensor(out=nat[1][:, g % 2, c0:c0 + cn], in0=pj_ps[:, 0:cn], scalar=bkv[:, g:g + 1],
                                             in1=nat[0][:, g % 2, c0:c0 + cn].bitcast(F32), op0=ALU.add, op1=ALU.subtract).then_inc(k_l, 1)
                if kind == "v":
                    t, = where
                    dve.wait_ge(v_ps, b.n(ST, t + 1))
                    wait(dve, pv_done, b.n(KC, -KC))
                    dve.tensor_copy(vt[:, b.par, t], pj_ps[0:SN, :]).then_inc(v_done, 1)

            def row_max(b, h, t):
                dve.wait_ge(scored_t[t], b.n(NH, h + 1))
                wait(dve, exped, b.n(NH * QT, (h - 2) * QT + t + 1))
                dve.tensor_reduce(nmax[:, h % 2, t:t + 1], sc_ps[t][0:QN, SC0:SC0 + S], AX_X, ALU.max, negate=True).then_inc(maxed, 1)

            def copy_p(b, h):
                dve.wait_ge(pT_ps, b.n(3 * NH, 3 * h + 1))
                if h % HPG == 0:
                    wait(dve, pv_done, b.n(KC, h // HPG))
                dve.tensor_copy(prT[:, h % HPG, 0:2], tr_ps[3 * h % 2][0:SN, 0:2 * N].rearrange("p (k t) -> p k t", k=2)).then_inc(pT_dve, 1)

            def invert(b, g):
                dve.wait_ge(exped, b.n(NH * QT, HPG * QT * (g + 1)))
                wait(dve, rT_ps, b.n(KC, g))
                dve.reciprocal(rinv[:], rsum[:, g % 2]).then_inc(inverted, 1)

            def normalize(b, g):
                dve.wait_ge(rb_done, b.n(KC, g + 1))
                wait(dve, o_out[g % 2], b.n(32, 16 * (g // 2)))
                dve.tensor_tensor(ou[:, g % 2], or_ps[:, 0:N], rb[:], ALU.mult).then_inc(o_done, 1)

            def body(b, att, nxt, prv):
                a, z = b.plus(1), b.plus(-1)
                for h in range(NH):
                    if h == 0 and prv:
                        invert(z, KC - 1)
                    if h % HPG == 0 and h > 0 and att:
                        invert(b, h // HPG - 1)
                    if h > 0 and att:
                        copy_p(b, h - 1)
                    if h == 0 and prv:
                        copy_p(z, NH - 1)
                    if nxt:
                        low(a, FILL[h][0])
                    if nxt and len(FILL[h]) > 1:
                        low(a, FILL[h][1])
                    for t in range(QT):
                        if h < NH - 1 and att:
                            row_max(b, h + 1, t)
                        if h == NH - 1 and nxt:
                            row_max(a, 0, t)
                    if h == 3 and prv:
                        normalize(z, KC - 1)
                    if h % HPG == 3 and h > 3 and att:
                        normalize(b, h // HPG - 1)
                    if far(b) and 3 <= h < 3 + ST:
                        stats(b.plus(2), h - 3)
                    if far(b) and h in (6, 9):
                        aggregate(b.plus(2), h // 3 - 2)
                    if far(b) and h in (7, 10):
                        neg_mean(b.plus(2), h // 3 - 2)

            def norm(b):
                for t in range(ST):
                    stats(b, t)
                for half in range(2):
                    aggregate(b, half)
                    neg_mean(b, half)

            norm(Batch(0))
            for f in ORDER:
                low(Batch(0), f)
            norm(Batch(1))
            for t in range(QT):
                row_max(Batch(0), 0, t)
            bodies(dve, body)

        @block.scalar
        def _(act):
            def apply_ln(b, t):
                if t % 3 == 0:
                    act.wait_ge(nmr, b.n(2, t // 3 + 1))
                act.activation(c_in[:, t], c_in[:, t], ACT.Identity, bias=nm[:, t:t + 1], scale=rs[:, t:t + 1]).then_inc(chat, 1)

            def high(b, fill):
                kind, *where = fill
                if kind == "c":
                    t, = where
                    act.wait_ge(cT_ps, b.n(ST, t + 1))
                    if t == 0:
                        wait(act, v_ps, b.n(ST, 0))
                        wait(act, k_ps, b.n(2 * KC, 0))
                    act.copy(cT[0][:, :, t * SN:(t + 1) * SN], pj_ps[:, 0:KC * SN].rearrange("p (k n) -> p k n", k=KC)).then_inc(cT_h, 1)
                elif kind == "k":
                    g, half = where
                    c0, cn = HALVES[half]
                    act.wait_ge(k_ps, b.n(2 * KC, 2 * g + half + 1))
                    if half == 0:
                        if g >= 2:
                            act.wait_ge(k_stacked[g - 2], b.n(STACK, STACK))
                        else:
                            wait(act, k_stacked[g + 2], b.n(STACK, 0))
                    act.activation(nat[0][:, g % 2, c0:c0 + cn], pj_ps[:, 0:cn], ACT.Identity, bias=bkv[:, g:g + 1]).then_inc(k_h, 1)

            def exps(b, h):
                wait(act, pT_ps, b.n(3 * NH, 3 * (h - 1)))
                if h % HPG == 0:
                    wait(act, inverted, b.n(KC, h // HPG - 1))
                for t in range(QT):
                    act.wait_ge(maxed, b.n(NH * QT, h * QT + t + 1))
                    act.activation(pr[:, h % 2, t], sc_ps[t][0:QN, SC0:SC0 + S], ACT.Exp, bias=nmax[:, h % 2, t:t + 1],
                                   accum_out=rsum[:, (h // HPG) % 2, h % HPG, t:t + 1]).then_inc(exped, 1)

            def copy_p(b, h, c):
                act.wait_ge(pT_ps, b.n(3 * NH, 3 * h + c + 1))
                if h % HPG == 0 and c == 1:
                    wait(act, pv_done, b.n(KC, h // HPG))
                act.copy(prT[:, h % HPG, 2 * c:2 * c + 2], tr_ps[(3 * h + c) % 2][0:SN, 0:2 * N].rearrange("p (k t) -> p k t", k=2)).then_inc(pT_act, 1)

            def copy_rT(b, g):
                act.wait_ge(rT_ps, b.n(KC, g + 1))
                wait(act, rb_ps, b.n(KC, g))
                act.copy(rT[:], or_ps[0:HPG, R0:R0 + N]).then_inc(rT_done, 1)

            def copy_rb(b, g):
                act.wait_ge(rb_ps, b.n(KC, g + 1))
                wait(act, o_done, b.n(KC, g))
                act.copy(rb[:], or_ps[:, R0:R0 + N]).then_inc(rb_done, 1)

            def body(b, att, nxt, prv):
                a, z = b.plus(1), b.plus(-1)
                for h in range(NH):
                    for c in (1, 2):
                        if c == 2 and nxt:
                            high(a, FILL[h][0])
                        if h > 0 and att:
                            copy_p(b, h - 1, c)
                        if h == 0 and prv:
                            copy_p(z, NH - 1, c)
                    if h == 1 and prv:
                        copy_rT(z, KC - 1)
                    if h % HPG == 1 and h > 1 and att:
                        copy_rT(b, h // HPG - 1)
                    if h == 2 and prv:
                        copy_rb(z, KC - 1)
                    if h % HPG == 2 and h > 2 and att:
                        copy_rb(b, h // HPG - 1)
                    if nxt and len(FILL[h]) > 1:
                        high(a, FILL[h][1])
                    if h < NH - 1 and att:
                        exps(b, h + 1)
                    if h == NH - 1 and nxt:
                        exps(a, 0)
                    if far(b) and 8 <= h < 8 + ST:
                        apply_ln(b.plus(2), h - 8)

            for t in range(ST):
                apply_ln(Batch(0), t)
            for f in ORDER:
                high(Batch(0), f)
            for t in range(ST):
                apply_ln(Batch(1), t)
            exps(Batch(0), 0)
            bodies(act, body)

        @block.gpsimd
        def _(pool):
            def inverse_std(b, half):
                at = slice(3 * half, 3 * half + 3)
                pool.wait_ge(mvs, b.n(2, half + 1))
                pool.tensor_tensor(ve[:, at], mv[:, at, 1], eps[0:SN, 0:3], ALU.add).then_inc(vareps, 1)
                pool.wait_ge(vareps, b.n(2, half + 1))
                pool.tensor_tensor(rs[:, at], ve[:, at], neg_half[0:SN, 0:3], ALU.pow).then_inc(rstd, 1)

            def store(b, g):
                pool.wait_ge(o_done, b.n(KC, g + 1))
                pool.dma_start(o_dram[bass.ds(b.index(), 1), g * P:(g + 1) * P].rearrange("a p t -> p (a t)"), ou[:, g % 2]).then_inc(o_out[g % 2], 16)

            def body(b, att, nxt, prv):
                z = b.plus(-1)
                if prv:
                    store(z, KC - 1)
                if far(b):
                    inverse_std(b.plus(2), 0)
                if att:
                    store(b, 0)
                if far(b):
                    inverse_std(b.plus(2), 1)
                if att:
                    store(b, 1)
                    store(b, 2)

            for b in (Batch(0), Batch(1)):
                for half in range(2):
                    inverse_std(b, half)
            bodies(pool, body)
            for i in range(2):
                pool.wait_ge(o_out[i], 32 * B)


def mlp_phase(nc, x1, o_dram, b_vc_t, w_cproj, b_cproj, w_mlp1, b_mlp1_t, w_mlp2, b_mlp2, gates, out, mod_t, ident, neg_half, eps):
    MC = MLP // P
    PAIRS = MC // 2
    GR = 3
    with ExitStack() as ctx:
        sb, ps, sem = alloc(nc, ctx, "mlp")
        wcp = [sb(f"wcp_{s}", [P, KC, H], F32R) for s in "hl"]
        w1 = [sb(f"w1_{s}", [P, KC, MLP], F32R) for s in "hl"]
        w2 = [sb(f"w2_{s}", [P, MC, H], F32R) for s in "hl"]
        bv = sb("bv", [P, KC])
        b1 = sb("b1", [P, MC])
        bcp, b2 = sb("bcp", [QN, H]), sb("b2", [QN, H])
        rows = lambda v: v.rearrange("(a n) -> a n", a=1).broadcast_to([QN, H])
        load_columns(nc, "mlp", [(bv[:], b_vc_t), (b1[:], b_mlp1_t), (bcp[:], rows(b_cproj)), (b2[:], rows(b_mlp2))])
        split_weights(nc, "mlp", [(w_cproj, wcp[0], wcp[1], 1.0), (w_mlp1, w1[0], w1[1], 1.0), (w_mlp2, w2[0], w2[1], 1.0)])
        o_in = sb("o_in", [P, KC, N])
        oT = [sb(f"oT_{s}", [P, KC, N], F32R) for s in "hl"]
        x_in = sb("x_in", [QN, QT, H])
        x2 = sb("x2", [QN, 2, QT, H])
        y = sb("y", [QN, QT, H])
        gate = sb("gate", [QN, H])
        xv = sb("xv", [P, KC, N])
        xT = [sb(f"xT_{s}", [P, KC, N], F32R) for s in "hl"]
        hv = sb("hv", [P, 2, 2, N])
        hT = [sb(f"hT_{s}", [P, GR, 2, N], F32R) for s in "hl"]
        turn = sb("turn", [1, 1])
        st, mv = sb("st", [QN, QT, 6]), sb("mv", [QN, QT, 2])
        ve, rs, nm = sb("ve", [QN, QT]), sb("rs", [QN, QT]), sb("nm", [QN, QT])

        h_ps = [ps(f"h_ps{i}") for i in range(2)]
        a_ps = [ps(f"a_ps{i}") for i in range(2)]
        c_ps = [ps(f"c_ps{i}") for i in range(2)]
        t_ps = [ps(f"t_ps{i}") for i in range(2)]

        o_loaded, x_loaded, gate_loaded = sem("o_loaded"), sem("x_loaded"), sem("gate_loaded")
        oT_h, oT_l, cp_ps, cp_done, x2_done = (sem(s) for s in ("oT_h", "oT_l", "cp_ps", "cp_done", "x2_done"))
        stats_done, mvs, vareps, rstd, nmr, xhat = (sem(s) for s in ("stats_done", "mvs", "vareps", "rstd", "nmr", "xhat"))
        xT_ps, xT_v, xT_h, xT_l = sem("xT_ps"), sem("xT_v"), sem("xT_h"), sem("xT_l")
        h_mm, h_act, h_h, h_l, h_used = (sem(s) for s in ("h_mm", "h_act", "h_h", "h_l", "h_used"))
        y_done, gated, summed, out_done = (sem(s) for s in ("y_done", "gated", "summed", "out_done"))
        block = ctx.enter_context(nc.Block())

        def bodies(eng, body):
            body(Batch(0), True, True, False)
            body(Batch(1), True, True, True)
            with eng.Fori(0, (B - 4) // 2) as i:
                body(Batch(2, i), True, True, True)
                body(Batch(3, i), True, True, True)
            body(Batch(B - 2), True, True, True)
            body(Batch(B - 1), True, False, True)
            body(Batch(B), False, False, True)

        @block.sync
        def _(sp):
            def load(b):
                wait(sp, oT_l, b.n(KC, 0))
                sp.dma_start(o_in[:], o_dram[bass.ds(b.index(), 1)].rearrange("a (g p) t -> p (a g) t", p=P)).then_inc(o_loaded, 16)
                wait(sp, xT_ps, b.n(2, 0))
                sp.dma_start(x_in[:], x1[bass.ds(b.index(), 1)].rearrange("a (t p) n -> p (a t) n", p=QN)).then_inc(x_loaded, 16)

            def finish(b):
                wait(sp, gated, b.n(2, 0))
                sp.dma_start(gate[:], gates[1, bass.ds(b.index(), 1)].broadcast_to([QN, H])).then_inc(gate_loaded, 16)
                for t in range(QT):
                    sp.wait_ge(summed, b.n(2, t + 1))
                    sp.dma_start(out[bass.ds(b.index(), 1), t * QN:(t + 1) * QN].rearrange("a p n -> p (a n)"), y[:, t]).then_inc(out_done, 16)

            def body(b, att, nxt, prv):
                if prv:
                    finish(b.plus(-1))
                if nxt and not (isinstance(b.i, int) and b.c == B - 2):
                    load(b.plus(2))

            load(Batch(0))
            load(Batch(1))
            bodies(sp, body)
            sp.wait_ge(out_done, 32 * B)

        @block.tensor
        def _(pe):
            def cproj(b, t):
                pe.wait_ge(oT_l, b.n(KC, KC))
                wait(pe, cp_done, b.n(2, t - 1))
                for k in range(KC):
                    last = product(pe, c_ps[t][0:QN, :], tuple(o[:, k, t * QN:(t + 1) * QN] for o in oT),
                                   tuple(w[:, k] for w in wcp), k == 0, k == KC - 1)
                last.then_inc(cp_ps, 1)

            def trans_x(b):
                pe.wait_ge(xhat, b.n(1, 1))
                wait(pe, xT_v, b.n(1, 0))
                for c in range(2):
                    for k in range(2):
                        for t in range(QT):
                            at = k * N + t * QN
                            last = pe.transpose(t_ps[c][:, at:at + QN], x_in[:, t, (2 * c + k) * P:(2 * c + k + 1) * P], ident[0:QN, 0:QN])
                    last.then_inc(xT_ps, 1)

            def hidden(b, p):
                if p == 0:
                    pe.wait_ge(xT_l, b.n(1, 1))
                wait(pe, h_act, b.n(PAIRS, p - 1))
                for m in range(2):
                    at = (2 * p + m) * P
                    for k in range(KC):
                        last = product(pe, h_ps[p % 2][:, m * N:(m + 1) * N], tuple(w[:, k, at:at + P] for w in w1),
                                       tuple(v[:, k] for v in xT), k == 0, k == KC - 1)
                last.then_inc(h_mm, 1)

            def output(b, p, u):
                pe.wait_ge(h_l, b.n(PAIRS, p + 1))
                if p == 0:
                    wait(pe, y_done, b.n(2, 0))
                for m in range(2):
                    for t in range(QT):
                        last = product(pe, a_ps[t][0:QN, :], tuple(v[:, u % GR, m, t * QN:(t + 1) * QN] for v in hT),
                                       tuple(w[:, 2 * p + m] for w in w2), p == 0 and m == 0, p == PAIRS - 1 and m == 1)
                last.then_inc(h_used, 1)

            def body(b, att, nxt, prv):
                a = b.plus(1)
                for p in range(PAIRS):
                    if att:
                        hidden(b, p)
                        if p >= 2:
                            output(b, p - 2, p - 2)
                    if nxt and p in (1, 2):
                        cproj(a, p - 1)
                    if nxt and p == 6:
                        trans_x(a)
                if att:
                    output(b, PAIRS - 2, PAIRS - 2)
                    output(b, PAIRS - 1, PAIRS - 1)

            for t in range(QT):
                cproj(Batch(0), t)
            trans_x(Batch(0))
            bodies(pe, body)

        @block.vector
        def _(dve):
            def low_o(b):
                for g in range(KC):
                    dve.wait_ge(oT_h, b.n(KC, g + 1))
                    dve.scalar_tensor_tensor(out=oT[1][:, g], in0=o_in[:, g], scalar=bv[:, g:g + 1],
                                             in1=oT[0][:, g].bitcast(F32), op0=ALU.add, op1=ALU.subtract).then_inc(oT_l, 1)

            def residual(b, t):
                dve.wait_ge(cp_ps, b.n(2, t + 1))
                wait(dve, summed, b.n(2, -2))
                dve.tensor_tensor(x2[:, b.par, t], c_ps[t][0:QN, :], bcp[:], ALU.add).then_inc(cp_done, 1)

            def stats(b):
                for t in range(QT):
                    dve.wait_ge(x2_done, b.n(2, t + 1))
                    last = dve.bn_stats(st[:, t], x2[:, b.par, t])
                last.then_inc(stats_done, 1)
                dve.wait_ge(stats_done, b.n(1, 1))
                dve.memset(turn[:], 0.0)
                for t in range(QT):
                    last = dve.bn_aggr(mv[:, t], st[:, t])
                last.then_inc(mvs, 1)

            def neg_mean(b):
                dve.wait_ge(rstd, b.n(1, 1))
                dve.scalar_tensor_tensor(out=nm[:], in0=mv[:, :, 0], scalar=-1.0, in1=rs[:], op0=ALU.mult, op1=ALU.mult).then_inc(nmr, 1)

            def modulate(b):
                wait(dve, xT_l, b.n(1, 0))
                for c in range(2):
                    dve.wait_ge(xT_ps, b.n(2, c + 1))
                    for k in range(2):
                        m = 2 * c + k
                        last = dve.tensor_scalar(xv[:, m], t_ps[c][:, k * N:(k + 1) * N], mod_t[:, KC + m, bass.ds(b.index(), 1)],
                                                 mod_t[:, m, bass.ds(b.index(), 1)], ALU.mult, ALU.add)
                last.then_inc(xT_v, 1)

            def split_h(b, p):
                dve.wait_ge(h_act, b.n(PAIRS, p + 1))
                wait(dve, h_used, b.n(PAIRS, p - GR + 1))
                dve.tensor_copy(hT[0][:, p % GR], hv[:, p % 2]).then_inc(h_h, 1)
                dve.wait_ge(h_h, b.n(PAIRS, p + 1))
                dve.tensor_tensor(hT[1][:, p % GR], hv[:, p % 2], hT[0][:, p % GR].bitcast(F32), ALU.subtract).then_inc(h_l, 1)

            def add_bias(b, t):
                dve.wait_ge(h_used, b.n(PAIRS, PAIRS))
                wait(dve, out_done, b.n(32, 0))
                dve.tensor_tensor(y[:, t], a_ps[t][0:QN, :], b2[:], ALU.add).then_inc(y_done, 1)

            def body(b, att, nxt, prv):
                a, z = b.plus(1), b.plus(-1)
                if prv:
                    add_bias(z, 0)
                    add_bias(z, 1)
                for p in range(PAIRS):
                    if att:
                        split_h(b, p)
                    if nxt and p == 0:
                        low_o(a)
                    if nxt and p in (2, 3):
                        residual(a, p - 2)
                    if nxt and p == 4:
                        stats(a)
                    if nxt and p == 5:
                        neg_mean(a)
                    if nxt and p == 6:
                        modulate(a)

            a = Batch(0)
            low_o(a)
            residual(a, 0)
            residual(a, 1)
            stats(a)
            neg_mean(a)
            modulate(a)
            bodies(dve, body)

        @block.scalar
        def _(act):
            def high_o(b):
                act.wait_ge(o_loaded, b.n(16, 16))
                wait(act, cp_ps, b.n(2, 0))
                for g in range(KC):
                    act.activation(oT[0][:, g], o_in[:, g], ACT.Identity, bias=bv[:, g:g + 1]).then_inc(oT_h, 1)

            def apply_ln(b):
                act.wait_ge(nmr, b.n(1, 1))
                for t in range(QT):
                    last = act.activation(x_in[:, t], x2[:, b.par, t], ACT.Identity, bias=nm[:, t:t + 1], scale=rs[:, t:t + 1])
                last.then_inc(xhat, 1)

            def high_x(b):
                act.wait_ge(xT_v, b.n(1, 1))
                wait(act, h_mm, b.n(PAIRS, 0))
                act.copy(xT[0][:], xv[:]).then_inc(xT_h, 1)

            def gelu(b, p):
                act.wait_ge(h_mm, b.n(PAIRS, p + 1))
                wait(act, h_l, b.n(PAIRS, p - 1))
                for m in range(2):
                    c = 2 * p + m
                    last = act.activation(hv[:, p % 2, m], h_ps[p % 2][:, m * N:(m + 1) * N], ACT.Gelu_apprx_tanh, bias=b1[:, c:c + 1])
                last.then_inc(h_act, 1)

            def body(b, att, nxt, prv):
                a = b.plus(1)
                for p in range(PAIRS):
                    if att:
                        gelu(b, p)
                    if nxt and p == 0:
                        high_o(a)
                    if nxt and p == 5:
                        apply_ln(a)
                if nxt:
                    high_x(a)

            a = Batch(0)
            high_o(a)
            apply_ln(a)
            high_x(a)
            bodies(act, body)

        @block.gpsimd
        def _(pool):
            def add_x1(b, t):
                pool.wait_ge(cp_done, b.n(2, t + 1))
                if t == 0:
                    pool.wait_ge(x_loaded, b.n(16, 16))
                pool.tensor_tensor(x2[:, b.par, t], x2[:, b.par, t], x_in[:, t], ALU.add).then_inc(x2_done, 1)

            def inverse_std(b):
                pool.wait_ge(mvs, b.n(1, 1))
                pool.tensor_tensor(ve[:], mv[:, :, 1], eps[0:QN, 0:QT], ALU.add).then_inc(vareps, 1)
                pool.wait_ge(vareps, b.n(1, 1))
                pool.tensor_tensor(rs[:], ve[:], neg_half[0:QN, 0:QT], ALU.pow).then_inc(rstd, 1)

            def low_x(b):
                pool.wait_ge(xT_h, b.n(1, 1))
                pool.tensor_tensor(xT[1][:], xv[:], xT[0][:].bitcast(F32), ALU.subtract).then_inc(xT_l, 1)

            def gated_sum(b, t):
                if t == 0:
                    pool.wait_ge(gate_loaded, b.n(16, 16))
                pool.wait_ge(y_done, b.n(2, t + 1))
                pool.tensor_tensor(y[:, t], y[:, t], gate[:], ALU.mult).then_inc(gated, 1)
                pool.wait_ge(gated, b.n(2, t + 1))
                pool.tensor_tensor(y[:, t], y[:, t], x2[:, b.par, t], ALU.add).then_inc(summed, 1)

            def front(b):
                for t in range(QT):
                    add_x1(b, t)
                inverse_std(b)
                low_x(b)

            def body(b, att, nxt, prv):
                if prv:
                    for t in range(QT):
                        gated_sum(b.plus(-1), t)
                if nxt:
                    front(b.plus(1))

            front(Batch(0))
            bodies(pool, body)


def build(nc, x, context, cond_t, w_mod, b_mod, w_qkv, b_qkv_t, w_proj, b_proj, w_qc, b_qc_t, w_kvc, b_kvc_t,
          w_cproj, b_cproj, w_mlp1, b_mlp1_t, w_mlp2, b_mlp2, out):
    x1 = nc.dram_tensor("x1", (B, N, H), F32, kind="Internal").ap()
    qc = nc.dram_tensor("qc", (B, 2, H, N), F32, kind="Internal").ap()
    o_cross = nc.dram_tensor("o_cross", (B, H, N), F32, kind="Internal").ap()
    gates = nc.dram_tensor("gates", (2, B, H), F32, kind="Internal").ap()
    with ExitStack() as ctx:
        sb, ps, sem = alloc(nc, ctx, "shared")
        ident = sb("ident", [P, P])
        select = sb("select", [HPG, P])
        neg_half, eps = sb("neg_half", [P, 8]), sb("eps", [P, 8])
        mod_t = sb("mod_t", [P, 4 * KC, B])
        constants_phase(nc, ident, select, neg_half, eps)
        condition_phase(nc, cond_t, w_mod, b_mod, gates, mod_t, ident)
        self_phase(nc, x, w_qkv, b_qkv_t, w_proj, b_proj, w_qc, b_qc_t, gates, x1, qc, mod_t[:, 0:2 * KC], ident, select, neg_half, eps)
        cross_phase(nc, context, w_kvc, b_kvc_t, qc, o_cross, ident, select, neg_half, eps)
        mlp_phase(nc, x1, o_cross, b_kvc_t[:, KC:2 * KC], w_cproj, b_cproj, w_mlp1, b_mlp1_t, w_mlp2, b_mlp2, gates, out,
                  mod_t[:, 2 * KC:4 * KC], ident, neg_half, eps)


def kernel(x, cond_1024, ctx_1024, **weights):
    import numpy as np
    import concourse.bacc as bacc
    from concourse.bass_utils import run_bass_kernel_spmd

    w = {name.replace("L0_xcond_", ""): np.asarray(a) for name, a in weights.items()}

    def columns(v):
        return v.reshape(-1, P).T

    arrays = {
        "x": x, "context": ctx_1024, "cond_t": np.asarray(cond_1024).T.reshape(KC, P, B).transpose(1, 0, 2),
        "w_mod": w["W_mod"], "b_mod": w["b_mod"], "w_qkv": w["W_qkv"], "b_qkv_t": columns(w["b_qkv"]),
        "w_proj": w["W_proj"], "b_proj": w["b_proj"], "w_qc": w["W_qc"], "b_qc_t": columns(w["b_qc"]),
        "w_kvc": w["W_kvc"], "b_kvc_t": columns(w["b_kvc"]), "w_cproj": w["W_cproj"], "b_cproj": w["b_cproj"],
        "w_mlp1": w["W_mlp1"], "b_mlp1_t": columns(w["b_mlp1"]), "w_mlp2": w["W_mlp2"], "b_mlp2": w["b_mlp2"],
    }
    arrays = {f"in_{name}": np.ascontiguousarray(a) for name, a in arrays.items()}
    nc = bacc.Bacc("TRN2", target_bir_lowering=False, num_devices=1, dynamic_dma_scratch_size=4096)
    aps = {name[3:]: nc.dram_tensor(name, a.shape, F32, kind="ExternalInput").ap() for name, a in arrays.items()}
    out = nc.dram_tensor("out", (B, N, H), F32, kind="ExternalOutput").ap()
    build(nc, out=out, **aps)
    r = run_bass_kernel_spmd(nc, [arrays], core_ids=[0])
    return r.results[0]["out"]
```

```python
from contextlib import ExitStack

import concourse.bass as bass
from concourse import mybir

ALU = mybir.AluOpType
ACT = mybir.ActivationFunctionType
F32 = mybir.dt.float32
F32R = mybir.dt.float32r
AX_X = mybir.AxisListType.X

P = 128
B, N, H = 16, 224, 512
S = 750
NH, HD = 16, 32
MLP = 4 * H
KC = H // P
HPG = P // HD
QT, QN = 2, N // 2
ST, SN = 6, S // 6
SHALF = (4 * SN, 2 * SN)
TERMS = 3
SCALE = float(HD) ** -0.5
EPS = 1e-6
RING = 4
SHIFT_A, SCALE_A, GATE_A, SHIFT_M, SCALE_M, GATE_M = range(6)


class Batch:

    def __init__(self, c, i=0):
        self.c, self.i = c, i
        self.par = c % 2

    def plus(self, d):
        return Batch(self.c + d, self.i)

    def index(self):
        return self.i * 2 + self.c

    def n(self, per, k):
        return self.i * (2 * per) + (self.c * per + k)

    def pair(self, per, k=0):
        return self.i * per + ((self.c // 2) * per + k)


def wait(eng, sem, value):
    if not (isinstance(value, int) and value <= 0):
        eng.wait_ge(sem, value)


def product(pe, out, lhs, rhs, first, last):
    pe.matmul(out, lhs[0], rhs[1], start=first, stop=False)
    pe.matmul(out, lhs[1], rhs[0], start=False, stop=False)
    return pe.matmul(out, lhs[0], rhs[0], start=False, stop=last)


def alloc(nc, ctx, phase):
    def sb(name, shape, dt=F32):
        return ctx.enter_context(nc.sbuf_tensor(f"{phase}_{name}", shape, dt))

    def ps(name, shape=(P, 512)):
        return ctx.enter_context(nc.psum_tensor(f"{phase}_{name}", list(shape), F32))

    sems = []

    def sem(name):
        sems.append(nc.alloc_semaphore(f"{phase}_{name}"))
        return sems[-1]

    def clear():
        nc.clear_and_free_semaphores(sems)
        nc.all_engine_barrier()

    ctx.callback(clear)

    return sb, ps, sem


def constants_phase(nc, ident, select, neg_half, eps):
    with ExitStack() as ctx:
        sb, ps, sem = alloc(nc, ctx, "constants")
        filled, shaped = sem("filled"), sem("shaped")
        block = ctx.enter_context(nc.Block())

        @block.gpsimd
        def _(pool):
            pool.memset(ident[:], 0.0)
            pool.memset(select[:], 1.0)
            pool.memset(neg_half[:], -0.5)
            pool.memset(eps[:], EPS).then_inc(filled, 1)
            pool.wait_ge(filled, 1)
            pool.affine_select(out=ident[:], in_=ident[:], compare_op=ALU.not_equal, fill=1.0, base=0,
                               pattern=[[-1, P]], channel_multiplier=1)
            pool.affine_select(out=select[:], in_=select[:], compare_op=ALU.is_ge, fill=0.0, base=0,
                               pattern=[[1, P]], channel_multiplier=-HD).then_inc(shaped, 1)
            pool.wait_ge(shaped, 1)
            pool.affine_select(out=select[:], in_=select[:], compare_op=ALU.is_ge, fill=0.0, base=HD - 1,
                               pattern=[[-1, P]], channel_multiplier=HD).then_inc(shaped, 1)
            pool.wait_ge(shaped, 2)


def condition_phase(nc, cond_t, w_mod, b_mod, gates, mod_t, ident, parts, columns):
    NM = 6 * H
    with ExitStack() as ctx:
        sb, ps, sem = alloc(nc, ctx, "condition")
        c_in = sb("c_in", [P, KC, B])
        c_exp = sb("c_exp", [P, KC, B])
        c_den = sb("c_den", [P, KC, B])
        c_inv = sb("c_inv", [P, KC, B])
        c_silu = sb("c_silu", [P, KC, B])
        wm = sb("wm", [P, 6, KC, H])
        bm = sb("bm", [B, NM])
        rows = sb("rows", [B, NM])
        acc = [ps(f"acc{m}") for m in range(6)]
        cols = ps("cols")
        cond_in, bm_in = sem("cond_in"), sem("bm_in")
        wm_in = [sem(f"wm_in{m}") for m in range(6)]
        exp_done, den_done, inv_done, silu_done = sem("exp_done"), sem("den_done"), sem("inv_done"), sem("silu_done")
        acc_done, rows_done, cols_done, mod_done = sem("acc_done"), sem("rows_done"), sem("cols_done"), sem("mod_done")
        gates_out = sem("gates_out")
        ORDER = [SHIFT_A, SCALE_A, SHIFT_M, SCALE_M, GATE_A, GATE_M]
        stage = [sb(f"stage{s}", [P, 2 * H]) for s in range(RING)]
        w_in = [sem(f"w_in{s}") for s in range(RING)]
        high_done, low_done, columns_in = sem("high_done"), sem("low_done"), sem("columns_in")
        views = split_views(parts, stage)
        block = ctx.enter_context(nc.Block())

        @block.sync
        def _(sp):
            sp.dma_start(c_in[:], cond_t).then_inc(cond_in, 16)
            sp.dma_start(bm[:], b_mod.rearrange("(a n) -> a n", a=1).broadcast_to([B, NM])).then_inc(bm_in, 16)
            for t, (src, st, _, _, _) in enumerate(views):
                wait(sp, low_done, t - RING + 1)
                sp.dma_start(st, src).then_inc(w_in[t % RING], 16)
            for dst, src in columns:
                sp.dma_start(dst, src).then_inc(columns_in, 16)
            for m in ORDER:
                sp.dma_start(wm[:, m], w_mod[:, m * H:(m + 1) * H].rearrange("(k p) n -> p k n", p=P)).then_inc(wm_in[m], 16)
            sp.wait_ge(rows_done, 6)
            for n, m in enumerate((GATE_A, GATE_M)):
                sp.dma_start(gates[n], rows[:, m * H:(m + 1) * H]).then_inc(gates_out, 16)
            sp.wait_ge(gates_out, 32)
            sp.wait_ge(columns_in, 16 * len(columns))

        @block.scalar
        def _(act):
            act.wait_ge(cond_in, 16)
            act.activation(c_exp[:], c_in[:], ACT.Exp, scale=-1.0).then_inc(exp_done, 1)
            for t, (_, st, hi, _, f) in enumerate(views):
                act.wait_ge(w_in[t % RING], 16 * (t // RING + 1))
                act.activation(hi, st, ACT.Identity, scale=f).then_inc(high_done, 1)

        @block.vector
        def _(dve):
            dve.wait_ge(exp_done, 1)
            dve.tensor_scalar(c_den[:], c_exp[:], 1.0, None, ALU.add).then_inc(den_done, 1)
            dve.wait_ge(den_done, 1)
            dve.reciprocal(c_inv[:], c_den[:]).then_inc(inv_done, 1)
            dve.wait_ge(inv_done, 1)
            dve.tensor_tensor(c_silu[:], c_in[:], c_inv[:], ALU.mult).then_inc(silu_done, 1)
            for t, (_, st, hi, lo, f) in enumerate(views):
                dve.wait_ge(high_done, t + 1)
                dve.scalar_tensor_tensor(out=lo, in0=st, scalar=f, in1=hi.bitcast(F32), op0=ALU.mult,
                                         op1=ALU.subtract).then_inc(low_done, 1)
            dve.wait_ge(bm_in, 16)
            for n, m in enumerate(ORDER):
                dve.wait_ge(acc_done, n + 1)
                at = slice(m * H, (m + 1) * H)
                one = 1.0 if m in (SCALE_A, SCALE_M) else 0.0
                dve.scalar_tensor_tensor(out=rows[:, at], in0=acc[m][0:B, :], scalar=one, in1=bm[:, at],
                                         op0=ALU.add, op1=ALU.add).then_inc(rows_done, 1)
            dve.wait_ge(cols_done, 1)
            dve.tensor_copy(mod_t[:], cols[:, 0:4 * KC * B].rearrange("p (m b) -> p m b", b=B)).then_inc(mod_done, 1)
            dve.wait_ge(mod_done, 1)

        @block.tensor
        def _(pe):
            pe.wait_ge(silu_done, 1)
            for m in ORDER:
                pe.wait_ge(wm_in[m], 16)
                for k in range(KC):
                    last = pe.matmul(acc[m][0:B, :], c_silu[:, k], wm[:, m, k], start=k == 0, stop=k == KC - 1)
                last.then_inc(acc_done, 1)
            pe.wait_ge(rows_done, 4)
            for n, m in enumerate((SHIFT_A, SCALE_A, SHIFT_M, SCALE_M)):
                for k in range(KC):
                    at = (n * KC + k) * B
                    last = pe.transpose(cols[:, at:at + B], rows[:, m * H + k * P:m * H + (k + 1) * P], ident[0:B, 0:B])
            last.then_inc(cols_done, 1)


def split_views(parts, stage):
    views = []
    for w, hi, lo, f in parts:
        for k in range(w.shape[0] // P):
            n = w.shape[1]
            views.append((w[k * P:(k + 1) * P], stage[len(views) % len(stage)][:, 0:n], hi[:, k, 0:n], lo[:, k, 0:n], f))
    return views


def load_phase(nc, phase, parts, columns):
    with ExitStack() as ctx:
        sb, ps, sem = alloc(nc, ctx, f"{phase}_load")
        stage = [sb(f"stage{s}", [P, MLP]) for s in range(RING)]
        w_in = [sem(f"w_in{s}") for s in range(RING)]
        high_done, low_done, columns_in = sem("high_done"), sem("low_done"), sem("columns_in")
        views = split_views(parts, stage)
        block = ctx.enter_context(nc.Block())

        @block.sync
        def _(sp):
            for t, (src, st, _, _, _) in enumerate(views):
                wait(sp, low_done, t - RING + 1)
                sp.dma_start(st, src).then_inc(w_in[t % RING], 16)
            for dst, src in columns:
                sp.dma_start(dst, src).then_inc(columns_in, 16)
            sp.wait_ge(columns_in, 16 * len(columns))

        @block.scalar
        def _(act):
            for t, (_, st, hi, _, f) in enumerate(views):
                act.wait_ge(w_in[t % RING], 16 * (t // RING + 1))
                act.activation(hi, st, ACT.Identity, scale=f).then_inc(high_done, 1)

        @block.vector
        def _(dve):
            for t, (_, st, hi, lo, f) in enumerate(views):
                dve.wait_ge(high_done, t + 1)
                dve.scalar_tensor_tensor(out=lo, in0=st, scalar=f, in1=hi.bitcast(F32), op0=ALU.mult,
                                         op1=ALU.subtract).then_inc(low_done, 1)


def self_phase(nc, x, cond_t, w_mod, b_mod, w_qkv, b_qkv_t, w_proj, b_proj, w_qc, b_qc_t, gates, x1, qc, mod_t, ident, select, neg_half, eps):
    with ExitStack() as ctx:
        sb, ps, sem = alloc(nc, ctx, "self")
        wqkv = [sb(f"wqkv_{s}", [P, KC, 3 * H], F32R) for s in "hl"]
        wproj = [sb(f"wproj_{s}", [P, KC, H], F32R) for s in "hl"]
        wqc = [sb(f"wqc_{s}", [P, KC, H], F32R) for s in "hl"]
        bqkv = sb("bqkv", [P, 3 * KC])
        bqc = sb("bqc", [P, KC])
        bproj = sb("bproj", [QN, H])
        x_in = sb("x_in", [QN, QT, H])
        condition_phase(nc, cond_t, w_mod, b_mod, gates, mod_t, ident,
                        [(w_qkv[:, 0:H], wqkv[0][:, :, 0:H], wqkv[1][:, :, 0:H], SCALE),
                         (w_qkv[:, H:3 * H], wqkv[0][:, :, H:3 * H], wqkv[1][:, :, H:3 * H], 1.0),
                         (w_proj, wproj[0], wproj[1], 1.0), (w_qc, wqc[0], wqc[1], SCALE)],
                        [(bqkv[:], b_qkv_t), (bqc[:], b_qc_t), (bproj[:], b_proj.rearrange("(a n) -> a n", a=1).broadcast_to([QN, H])),
                         (x_in[:], x[0].rearrange("(t p) n -> p t n", p=QN))])
        mod_t = mod_t[:, 0:2 * KC]
        x_res = sb("x_res", [QN, QT, H])
        y = sb("y", [QN, QT, H])
        gate = sb("gate", [QN, H])
        xv = sb("xv", [P, KC, N])
        xT = [sb(f"xT_{s}", [P, KC, N], F32R) for s in "hl"]
        yT = [sb(f"yT_{s}", [P, KC, N], F32R) for s in "hl"]
        nat = [sb(f"nat_{s}", [P, KC, N], F32R) for s in "hl"]
        natq = [sb(f"natq_{s}", [P, KC, N], F32R) for s in "hl"]
        kst = sb("kst", [TERMS * HD, 2, HPG, KC, N], F32R)
        qst = sb("qst", [TERMS * HD, 2, HPG, KC, N], F32R)
        vt = sb("vt", [QN, 2, QT, H])
        pr = sb("pr", [QN, 2, QT, N])
        prT = sb("prT", [QN, HPG, QT, N])
        ou = sb("ou", [P, KC, N])
        nmax = sb("nmax", [QN, 2, QT])
        rsum = sb("rsum", [QN, 2, HPG, QT])
        rinv = sb("rinv", [QN, HPG, QT])
        rT = sb("rT", [HPG, N])
        rb = sb("rb", [P, N])
        bqs, bqcs = sb("bqs", [P, KC]), sb("bqcs", [P, KC])
        st1, st2 = sb("st1", [QN, QT, 6]), sb("st2", [QN, QT, 6])
        turn = sb("turn", [1, 1])
        mv1, mv2 = sb("mv1", [QN, QT, 2]), sb("mv2", [QN, QT, 2])
        ve1, ve2 = sb("ve1", [QN, QT]), sb("ve2", [QN, QT])
        rs1, rs2 = sb("rs1", [QN, QT]), sb("rs2", [QN, QT])
        nm1, nm2 = sb("nm1", [QN, QT]), sb("nm2", [QN, QT])

        sc_ps = [ps(f"sc_ps{i}") for i in range(2)]
        tr_ps = [ps(f"tr_ps{i}") for i in range(2)]
        pj_ps = [ps(f"pj_ps{i}") for i in range(2)]
        tx_ps = ps("tx_ps")
        or_ps = ps("or_ps")
        R0 = 256

        x_loaded, res_loaded, gate_loaded = sem("x_loaded"), sem("res_loaded"), sem("gate_loaded")
        stats1, mvs1, vareps1, rstd1, nmr1, xhat1 = (sem(s) for s in ("stats1", "mvs1", "vareps1", "rstd1", "nmr1", "xhat1"))
        stats2, mvs2, vareps2, rstd2, nmr2, xhat2 = (sem(s) for s in ("stats2", "mvs2", "vareps2", "rstd2", "nmr2", "xhat2"))
        xT_ps, xT_v, xT_h, xT_l = sem("xT_ps"), sem("xT_v"), sem("xT_h"), sem("xT_l")
        k_ps, k_h, k_l = sem("k_ps"), sem("k_h"), sem("k_l")
        q_ps, q_h, q_l = sem("q_ps"), sem("q_h"), sem("q_l")
        c_ps, c_h, c_l = sem("c_ps"), sem("c_h"), sem("c_l")
        v_ps, v_done = sem("v_ps"), sem("v_done")
        k_stacked = [sem(f"k_stacked{p}") for p in range(2)]
        q_stacked = [sem(f"q_stacked{p}") for p in range(2)]
        scored, maxed, exped, pT_ps, pT_done = (sem(s) for s in ("scored", "maxed", "exped", "pT_ps", "pT_done"))
        pv_done, inverted, rT_ps, rT_done, rb_ps, rb_done, o_done = (sem(s) for s in ("pv_done", "inverted", "rT_ps", "rT_done", "rb_ps", "rb_done", "o_done"))
        oT_h, oT_l = sem("oT_h"), sem("oT_l")
        proj_ps, proj_done, gated, summed, x1_out = (sem(s) for s in ("proj_ps", "proj_done", "gated", "summed", "x1_out"))
        yT_ps, yT_h, yT_l = sem("yT_ps"), sem("yT_h"), sem("yT_l")
        qc_out = sem("qc_out")
        bias_scaled = sem("bias_scaled")
        STACK = 16 * HPG * TERMS
        block = ctx.enter_context(nc.Block())

        def bodies(eng, body):
            body(Batch(0), True, True, False, False)
            body(Batch(1), True, True, True, False)
            with eng.Fori(0, (B - 4) // 2) as i:
                body(Batch(2, i), True, True, True, True)
                body(Batch(3, i), True, True, True, True)
            body(Batch(B - 2), True, True, True, True)
            body(Batch(B - 1), True, False, True, True)
            body(Batch(B), False, False, True, True)

        def far(b):
            return not (isinstance(b.i, int) and b.c > B - 3)

        FILL = [[("tx1", 1, 0), ("c", 0, 0), ("c", 0, 1)], [("c", 1, 0)], [("c", 1, 1)], [("k", 0, 0), ("k", 0, 1)],
                [("k", 1, 0)], [("k", 1, 1)], [("p", 0, 0), ("p", 0, 1)], [("p", 1, 0)],
                [("p", 1, 1), ("q", 0, 0)], [("q", 0, 1)], [("q", 1, 0)], [("q", 1, 1), ("v", 0, 0)],
                [("v", 0, 1)], [("ty", 0, 0), ("v", 1, 0)], [("ty", 1, 0), ("v", 1, 1)], [("tx0", 0, 0)]]

        def fills(b, h, nxt, prv, old):
            of = {"tx0": (far(b), 2), "tx1": (nxt, 1), "k": (nxt, 1), "q": (nxt, 1), "v": (nxt, 1), "p": (prv, -1), "ty": (prv, -1), "c": (old, -2)}
            return [(kind, c, part, b.plus(of[name][1])) for name, c, part in FILL[h] for kind in (name[0:2],) if of[name][0]]

        @block.sync
        def _(sp):
            def load_x(b):
                wait(sp, xT_ps, b.n(2, 0))
                sp.dma_start(x_in[:], x[bass.ds(b.index(), 1)].rearrange("a (t p) n -> p (a t) n", p=QN)).then_inc(x_loaded, 16)

            def stack(b, low_done, src, dst, sems, terms):
                sp.wait_ge(low_done, b.n(2, 2))
                for j in range(HPG):
                    for r in range(TERMS):
                        sp.dma_start(dst[HD * r:HD * r + HD, b.par, j].bitcast(F32),
                                     src[terms[r]][HD * j:HD * j + HD].bitcast(F32)).then_inc(sems[b.par], 16)

            def load_res(b):
                wait(sp, yT_ps, b.n(2, 0))
                sp.dma_start(x_res[:], x[bass.ds(b.index(), 1)].rearrange("a (t p) n -> p (a t) n", p=QN)).then_inc(res_loaded, 16)
                wait(sp, gated, b.n(2, 0))
                sp.dma_start(gate[:], gates[0, bass.ds(b.index(), 1)].broadcast_to([QN, H])).then_inc(gate_loaded, 16)

            def store_x1(b):
                for t in range(QT):
                    sp.wait_ge(summed, b.n(2, t + 1))
                    sp.dma_start(x1[bass.ds(b.index(), 1), t * QN:(t + 1) * QN].rearrange("a p n -> p (a n)"), y[:, t]).then_inc(x1_out, 16)

            def store_qc(b):
                sp.wait_ge(c_l, b.n(2, 2))
                for s in range(2):
                    sp.dma_start(qc[bass.ds(b.index(), 1), s].rearrange("a (g p) n -> p (a g) n", p=P), natq[s][:].bitcast(F32)).then_inc(qc_out, 16)

            def body(b, att, nxt, prv, old):
                a, z = b.plus(1), b.plus(-1)
                if prv:
                    load_res(z)
                if far(b):
                    load_x(b.plus(2))
                if old:
                    store_qc(b.plus(-2))
                if nxt:
                    stack(a, k_l, nat, kst, k_stacked, (0, 1, 0))
                if prv:
                    store_x1(z)
                if nxt:
                    stack(a, q_l, natq, qst, q_stacked, (0, 0, 1))

            load_x(Batch(1))
            stack(Batch(0), k_l, nat, kst, k_stacked, (0, 1, 0))
            stack(Batch(0), q_l, natq, qst, q_stacked, (0, 0, 1))
            bodies(sp, body)
            store_qc(Batch(B - 1))
            sp.wait_ge(x1_out, 32 * B)
            sp.wait_ge(qc_out, 32 * B)

        @block.tensor
        def _(pe):
            def trans(src, c, ready, b, done):
                pe.wait_ge(ready, b.n(2, 2))
                for k in range(2):
                    for t in range(QT):
                        at = k * N + t * QN
                        last = pe.transpose(tx_ps[:, at:at + QN], src[:, t, (2 * c + k) * P:(2 * c + k + 1) * P], ident[0:QN, 0:QN])
                last.then_inc(done, 1)

            def channels(c, m, w, first_chunk, src, done):
                at = (first_chunk + m) * P
                for k in range(KC):
                    last = product(pe, pj_ps[c][:, m * N:(m + 1) * N], (w[0][:, k, at:at + P], w[1][:, k, at:at + P]),
                                   (src[0][:, k], src[1][:, k]), k == 0, k == KC - 1)
                if m == 1:
                    last.then_inc(done, 1)

            def tokens(t, part, w, at, src, done):
                for k in range(2 * part, 2 * part + 2):
                    last = product(pe, pj_ps[t][0:QN, :], tuple(s[:, k, t * QN:(t + 1) * QN] for s in src),
                                   (w[0][:, k, at:at + H], w[1][:, k, at:at + H]), k == 0, k == KC - 1)
                if part == 1:
                    last.then_inc(done, 1)

            def score(b, h):
                if h == 0:
                    pe.wait_ge(k_stacked[b.par], b.pair(STACK, STACK))
                    pe.wait_ge(q_stacked[b.par], b.pair(STACK, STACK))
                wait(pe, exped, b.n(NH, h - 1))
                g, j = h // HPG, h % HPG
                for t in range(QT):
                    last = pe.matmul(sc_ps[h % 2][0:QN, t * N:(t + 1) * N], qst[:, b.par, j, g, t * QN:(t + 1) * QN],
                                     kst[:, b.par, j, g, :], start=True, stop=True)
                last.then_inc(scored, 1)

            def trans_p(b, h):
                pe.wait_ge(exped, b.n(NH, h + 1))
                wait(pe, pT_done, b.n(NH, h - 1))
                for kt in range(QT):
                    for t in range(QT):
                        at = kt * N + t * QN
                        last = pe.transpose(tr_ps[h % 2][0:QN, at:at + QN], pr[:, h % 2, t, kt * QN:(kt + 1) * QN], ident[0:QN, 0:QN])
                last.then_inc(pT_ps, 1)

            def pv(b, g):
                pe.wait_ge(pT_done, b.n(NH, HPG * g + HPG))
                if g == 0:
                    pe.wait_ge(v_done, b.n(2, 2))
                wait(pe, o_done, b.n(KC, g))
                for kt in range(QT):
                    for j in range(HPG):
                        ch = g * P + j * HD
                        last = pe.matmul(or_ps[HD * j:HD * j + HD, 0:N], vt[:, b.par, kt, ch:ch + HD], prT[:, j, kt],
                                         start=kt == 0, stop=kt == QT - 1)
                last.then_inc(pv_done, 1)
                pe.wait_ge(inverted, b.n(KC, g + 1))
                for t in range(QT):
                    last = pe.transpose(or_ps[0:HPG, R0 + t * QN:R0 + (t + 1) * QN], rinv[:, :, t], ident[0:QN, 0:QN])
                last.then_inc(rT_ps, 1)

            def spread(b, g):
                pe.wait_ge(rT_done, b.n(KC, g + 1))
                pe.matmul(or_ps[:, R0:R0 + N], select[:], rT[:], start=True, stop=True).then_inc(rb_ps, 1)

            def fill(kind, c, part, o, b, att, nxt, prv, old):
                a, z, y2 = b.plus(1), b.plus(-1), b.plus(-2)
                if kind == "tx":
                    if c == 0 and prv:
                        pe.wait_ge(yT_l, z.n(2, 2))
                    elif c == 0:
                        pe.wait_ge(xT_v, o.n(2, 0))
                    else:
                        pe.wait_ge(xT_v, o.n(2, 1))
                    trans(x_in, c, xhat1, o, xT_ps)
                if kind == "ty":
                    if c == 0 and nxt:
                        pe.wait_ge(xT_v, a.n(2, 2))
                    elif c == 0:
                        pe.wait_ge(yT_l, o.n(2, 0))
                    else:
                        pe.wait_ge(yT_l, o.n(2, 1))
                    trans(x_res, c, xhat2, o, yT_ps)
                if kind == "c":
                    if part == 0:
                        if att:
                            pe.wait_ge(v_done, b.n(2, c + 1))
                        pe.wait_ge(yT_l, o.n(2, 2))
                    channels(c, part, wqc, 2 * c, yT, c_ps)
                if kind == "k":
                    if part == 0:
                        if old:
                            pe.wait_ge(c_l, y2.n(2, c + 1))
                        else:
                            pe.wait_ge(v_done, b.n(2, c + 1))
                        pe.wait_ge(xT_l, o.n(1, 1))
                    channels(c, part, wqkv, KC + 2 * c, xT, k_ps)
                if kind == "p":
                    if part == 0:
                        if nxt:
                            pe.wait_ge(k_l, a.n(2, c + 1))
                        else:
                            pe.wait_ge(c_l, y2.n(2, c + 1))
                        pe.wait_ge(oT_l, o.n(KC, KC))
                    tokens(c, part, wproj, 0, yT, proj_ps)
                if kind == "q":
                    if part == 0:
                        if prv:
                            pe.wait_ge(proj_done, z.n(2, c + 1))
                        else:
                            pe.wait_ge(k_l, o.n(2, c + 1))
                    channels(c, part, wqkv, 2 * c, xT, q_ps)
                if kind == "v":
                    if part == 0:
                        pe.wait_ge(q_l, o.n(2, c + 1))
                    tokens(c, part, wqkv, 2 * H, xT, v_ps)

            def body(b, att, nxt, prv, old):
                a, z = b.plus(1), b.plus(-1)
                for h in range(NH):
                    if h == 1 and prv:
                        pv(z, KC - 1)
                    if h % HPG == 1 and h > 1 and att:
                        pv(b, h // HPG - 1)
                    if h > 0 and att:
                        trans_p(b, h - 1)
                    if h == 0 and prv:
                        trans_p(z, NH - 1)
                    for kind, c, part, o in fills(b, h, nxt, prv, old):
                        fill(kind, c, part, o, b, att, nxt, prv, old)
                    if h == 2 and prv:
                        spread(z, KC - 1)
                    if h % HPG == 2 and h > 2 and att:
                        spread(b, h // HPG - 1)
                    if h < NH - 1 and att:
                        score(b, h + 1)
                    if h == NH - 1 and nxt:
                        score(a, 0)

            a = Batch(0)
            for c in range(2):
                wait(pe, xT_v, c)
                trans(x_in, c, xhat1, a, xT_ps)
            pe.wait_ge(xT_l, 1)
            for c in range(2):
                for m in range(2):
                    channels(c, m, wqkv, KC + 2 * c, xT, k_ps)
            for c in range(2):
                pe.wait_ge(k_l, c + 1)
                for m in range(2):
                    channels(c, m, wqkv, 2 * c, xT, q_ps)
            for c in range(2):
                pe.wait_ge(q_l, c + 1)
                for part in range(2):
                    tokens(c, part, wqkv, 2 * H, xT, v_ps)
            pe.wait_ge(xT_v, 2)
            trans(x_in, 0, xhat1, a.plus(1), xT_ps)
            score(a, 0)
            bodies(pe, body)
            for c in range(2):
                pe.wait_ge(c_l, 2 * (B - 1) + c)
                for m in range(2):
                    if m == 0 and c == 0:
                        pe.wait_ge(yT_l, 2 * B)
                    channels(c, m, wqc, 2 * c, yT, c_ps)

        @block.vector
        def _(dve):
            def stats(b, src, ready, value, st, mv, s_stats, s_mv):
                for t in range(QT):
                    wait(dve, ready, value(t))
                    last = dve.bn_stats(st[:, t], src[:, t])
                last.then_inc(s_stats, 1)
                dve.wait_ge(s_stats, b.n(1, 1))
                dve.memset(turn[:], 0.0)
                for t in range(QT):
                    last = dve.bn_aggr(mv[:, t], st[:, t])
                last.then_inc(s_mv, 1)

            def neg_mean(b, mv, rs, nm, s_rstd, s_nmr):
                dve.wait_ge(s_rstd, b.n(1, 1))
                dve.scalar_tensor_tensor(out=nm[:], in0=mv[:, :, 0], scalar=-1.0, in1=rs[:], op0=ALU.mult, op1=ALU.mult).then_inc(s_nmr, 1)

            def modulate(b, c):
                if c == 0:
                    wait(dve, xT_l, b.n(1, 0))
                dve.wait_ge(xT_ps, b.n(2, c + 1))
                for k in range(2):
                    m = 2 * c + k
                    last = dve.tensor_scalar(xv[:, m], tx_ps[:, k * N:(k + 1) * N], mod_t[:, KC + m, bass.ds(b.index(), 1)],
                                             mod_t[:, m, bass.ds(b.index(), 1)], ALU.mult, ALU.add)
                last.then_inc(xT_v, 1)

            def lows(b, c, high, low, bias, first_chunk, dst=nat):
                dve.wait_ge(high, b.n(2, c + 1))
                for m in range(2):
                    last = dve.scalar_tensor_tensor(out=dst[1][:, 2 * c + m], in0=pj_ps[c][:, m * N:(m + 1) * N],
                                                    scalar=bias[:, first_chunk + m:first_chunk + m + 1],
                                                    in1=dst[0][:, 2 * c + m].bitcast(F32), op0=ALU.add, op1=ALU.subtract)
                last.then_inc(low, 1)

            def add_bias(b, t):
                dve.wait_ge(proj_ps, b.n(2, t + 1))
                wait(dve, x1_out, b.n(32, 0))
                dve.tensor_tensor(y[:, t], pj_ps[t][0:QN, :], bproj[:], ALU.add).then_inc(proj_done, 1)

            def low_o(b, half):
                for g in range(2 * half, 2 * half + 2):
                    dve.wait_ge(oT_h, b.n(KC, g + 1))
                    dve.scalar_tensor_tensor(out=yT[1][:, g], in0=ou[:, g], scalar=bqkv[:, 2 * KC + g:2 * KC + g + 1],
                                             in1=yT[0][:, g].bitcast(F32), op0=ALU.add, op1=ALU.subtract).then_inc(oT_l, 1)

            def low_y(b, c):
                dve.wait_ge(yT_h, b.n(2, c + 1))
                dve.tensor_tensor(yT[1][:, 2 * c:2 * c + 2], tx_ps[:, 0:2 * N].rearrange("p (m n) -> p m n", m=2),
                                  yT[0][:, 2 * c:2 * c + 2].bitcast(F32), ALU.subtract).then_inc(yT_l, 1)

            def row_max(b, h):
                dve.wait_ge(scored, b.n(NH, h + 1))
                wait(dve, exped, b.n(NH, h - 1))
                dve.tensor_reduce(nmax[:, h % 2], sc_ps[h % 2][0:QN, 0:QT * N].rearrange("p (t k) -> p t k", t=QT), AX_X, ALU.max,
                                  negate=True).then_inc(maxed, 1)

            def copy_p(b, h):
                dve.wait_ge(pT_ps, b.n(NH, h + 1))
                if h % HPG == 0:
                    wait(dve, pv_done, b.n(KC, h // HPG))
                dve.tensor_copy(prT[:, h % HPG], tr_ps[h % 2][0:QN, 0:QT * N].rearrange("p (k t) -> p k t", k=QT)).then_inc(pT_done, 1)

            def invert(b, g):
                dve.wait_ge(exped, b.n(NH, HPG * g + HPG))
                wait(dve, rT_ps, b.n(KC, g))
                dve.reciprocal(rinv[:], rsum[:, g % 2]).then_inc(inverted, 1)

            def normalize(b, g):
                dve.wait_ge(rb_done, b.n(KC, g + 1))
                dve.wait_ge(pv_done, b.n(KC, g + 1))
                if g == 0:
                    wait(dve, oT_l, b.n(KC, 0))
                dve.tensor_tensor(ou[:, g], or_ps[:, 0:N], rb[:], ALU.mult).then_inc(o_done, 1)

            def body(b, att, nxt, prv, old):
                a, z, far_b = b.plus(1), b.plus(-1), b.plus(2)
                for h in range(NH):
                    if h == 0 and prv:
                        invert(z, KC - 1)
                    if h % HPG == 0 and h > 0 and att:
                        invert(b, h // HPG - 1)
                    if h > 0 and att:
                        copy_p(b, h - 1)
                    if h == 0 and prv:
                        copy_p(z, NH - 1)
                    for kind, c, part, o in fills(b, h, nxt, prv, old):
                        if kind == "tx":
                            modulate(o, c)
                        if kind == "ty":
                            low_y(o, c)
                        if kind == "p" and part == 1:
                            add_bias(o, c)
                    if h == 3 and prv:
                        normalize(z, KC - 1)
                    if h % HPG == 3 and h > 3 and att:
                        normalize(b, h // HPG - 1)
                    if h < NH - 1 and att:
                        row_max(b, h + 1)
                    if h == NH - 1 and nxt:
                        row_max(a, 0)
                    for kind, c, part, o in fills(b, h, nxt, prv, old):
                        if kind == "k" and part == 1:
                            lows(o, c, k_h, k_l, bqkv, KC + 2 * c)
                        if kind == "q" and part == 1:
                            lows(o, c, q_h, q_l, bqs, 2 * c, natq)
                        if kind == "c" and part == 1:
                            lows(o, c, c_h, c_l, bqcs, 2 * c, natq)
                    if prv and h == 4:
                        low_o(z, 0)
                        low_o(z, 1)
                    if far(b) and h == 6:
                        stats(far_b, x_in, x_loaded, lambda t: far_b.n(16, 0), st1, mv1, stats1, mvs1)
                    if far(b) and h == 8:
                        neg_mean(far_b, mv1, rs1, nm1, rstd1, nmr1)
                    if prv and h == 10:
                        stats(z, y, summed, lambda t: z.n(2, t + 1), st2, mv2, stats2, mvs2)
                    if prv and h == 11:
                        neg_mean(z, mv2, rs2, nm2, rstd2, nmr2)

            dve.tensor_scalar(bqs[:], bqkv[:, 0:KC], SCALE, None, ALU.mult)
            dve.tensor_scalar(bqcs[:], bqc[:], SCALE, None, ALU.mult).then_inc(bias_scaled, 1)
            dve.wait_ge(bias_scaled, 1)
            a = Batch(0)
            stats(a, x_in, x_loaded, lambda t: 0, st1, mv1, stats1, mvs1)
            neg_mean(a, mv1, rs1, nm1, rstd1, nmr1)
            for c in range(2):
                modulate(a, c)
            for c in range(2):
                lows(a, c, k_h, k_l, bqkv, KC + 2 * c)
            for c in range(2):
                lows(a, c, q_h, q_l, bqs, 2 * c, natq)
            stats(a.plus(1), x_in, x_loaded, lambda t: 16, st1, mv1, stats1, mvs1)
            neg_mean(a.plus(1), mv1, rs1, nm1, rstd1, nmr1)
            modulate(a.plus(1), 0)
            row_max(a, 0)
            bodies(dve, body)
            for c in range(2):
                lows(Batch(B - 1), c, c_h, c_l, bqcs, 2 * c, natq)

        @block.scalar
        def _(act):
            def apply_ln(b, t, src, dst, rs, nm, s_nmr, s_out):
                act.wait_ge(s_nmr, b.n(1, 1))
                act.activation(dst[:, t], src[:, t], ACT.Identity, bias=nm[:, t:t + 1], scale=rs[:, t:t + 1]).then_inc(s_out, 1)

            def high_x(b):
                act.wait_ge(xT_v, b.n(2, 2))
                wait(act, v_ps, b.n(2, 0))
                act.copy(xT[0][:], xv[:]).then_inc(xT_h, 1)

            def highs(b, c, ready, high, bias, first_chunk, dst=nat):
                act.wait_ge(ready, b.n(2, c + 1))
                for m in range(2):
                    last = act.activation(dst[0][:, 2 * c + m], pj_ps[c][:, m * N:(m + 1) * N], ACT.Identity,
                                          bias=bias[:, first_chunk + m:first_chunk + m + 1])
                last.then_inc(high, 1)

            def copy_v(b, t):
                act.wait_ge(v_ps, b.n(2, t + 1))
                wait(act, pv_done, b.n(KC, -KC))
                act.copy(vt[:, b.par, t], pj_ps[t][0:QN, :]).then_inc(v_done, 1)

            def exps(b, h):
                act.wait_ge(maxed, b.n(NH, h + 1))
                wait(act, pT_ps, b.n(NH, h - 1))
                if h % HPG == 0:
                    wait(act, inverted, b.n(KC, h // HPG - 1))
                for t in range(QT):
                    last = act.activation(pr[:, h % 2, t], sc_ps[h % 2][0:QN, t * N:(t + 1) * N], ACT.Exp,
                                          bias=nmax[:, h % 2, t:t + 1], accum_out=rsum[:, (h // HPG) % 2, h % HPG, t:t + 1])
                last.then_inc(exped, 1)

            def copy_rT(b, g):
                act.wait_ge(rT_ps, b.n(KC, g + 1))
                wait(act, rb_ps, b.n(KC, g))
                act.copy(rT[:], or_ps[0:HPG, R0:R0 + N]).then_inc(rT_done, 1)

            def copy_rb(b, g):
                act.wait_ge(rb_ps, b.n(KC, g + 1))
                wait(act, o_done, b.n(KC, g))
                act.copy(rb[:], or_ps[:, R0:R0 + N]).then_inc(rb_done, 1)

            def highs_o(b, half):
                wait(act, c_ps, b.n(2, 0))
                for g in range(2 * half, 2 * half + 2):
                    act.wait_ge(o_done, b.n(KC, g + 1))
                    act.activation(yT[0][:, g], ou[:, g], ACT.Identity, bias=bqkv[:, 2 * KC + g:2 * KC + g + 1]).then_inc(oT_h, 1)

            def highs_y(b, c):
                act.wait_ge(proj_ps, b.n(2, 2))
                act.wait_ge(yT_ps, b.n(2, c + 1))
                act.copy(yT[0][:, 2 * c:2 * c + 2], tx_ps[:, 0:2 * N].rearrange("p (m n) -> p m n", m=2)).then_inc(yT_h, 1)

            def body(b, att, nxt, prv, old):
                a, z = b.plus(1), b.plus(-1)
                for h in range(NH):
                    if h == 1 and prv:
                        copy_rT(z, KC - 1)
                    if h % HPG == 1 and h > 1 and att:
                        copy_rT(b, h // HPG - 1)
                    if h == 2 and prv:
                        copy_rb(z, KC - 1)
                    if h % HPG == 2 and h > 2 and att:
                        copy_rb(b, h // HPG - 1)
                    for kind, c, part, o in fills(b, h, nxt, prv, old):
                        if kind == "ty":
                            highs_y(o, c)
                        if kind == "k" and part == 1:
                            if c == 0:
                                act.wait_ge(k_stacked[b.par], b.pair(STACK, STACK))
                            highs(o, c, k_ps, k_h, bqkv, KC + 2 * c)
                        if kind == "q" and part == 1:
                            if c == 0 and old:
                                act.wait_ge(qc_out, b.plus(-2).n(32, 32))
                            elif c == 0:
                                act.wait_ge(q_stacked[b.par], b.pair(STACK, STACK))
                            highs(o, c, q_ps, q_h, bqs, 2 * c, natq)
                        if kind == "c" and part == 1:
                            if c == 0 and att:
                                act.wait_ge(q_stacked[b.par], b.pair(STACK, STACK))
                            if c == 0 and not att:
                                act.wait_ge(qc_out, o.n(32, 0))
                            highs(o, c, c_ps, c_h, bqcs, 2 * c, natq)
                        if kind == "v" and part == 1:
                            copy_v(o, c)
                    if h < NH - 1 and att:
                        exps(b, h + 1)
                    if h == NH - 1 and nxt:
                        exps(a, 0)
                    if nxt and h == 0:
                        high_x(a)
                    if prv and h == 3:
                        highs_o(z, 0)
                        highs_o(z, 1)
                    if far(b) and h in (9, 10):
                        apply_ln(b.plus(2), h - 9, x_in, x_in, rs1, nm1, nmr1, xhat1)
                    for t in range(QT) if prv and h == 11 else ():
                        apply_ln(z, t, y, x_res, rs2, nm2, nmr2, xhat2)

            act.wait_ge(bias_scaled, 1)
            a = Batch(0)
            for t in range(QT):
                apply_ln(a, t, x_in, x_in, rs1, nm1, nmr1, xhat1)
            high_x(a)
            for c in range(2):
                highs(a, c, k_ps, k_h, bqkv, KC + 2 * c)
            for c in range(2):
                highs(a, c, q_ps, q_h, bqs, 2 * c, natq)
            copy_v(a, 0)
            copy_v(a, 1)
            for t in range(QT):
                apply_ln(a.plus(1), t, x_in, x_in, rs1, nm1, nmr1, xhat1)
            exps(a, 0)
            bodies(act, body)
            act.wait_ge(qc_out, 32 * (B - 1))
            for c in range(2):
                highs(Batch(B - 1), c, c_ps, c_h, bqcs, 2 * c, natq)

        @block.gpsimd
        def _(pool):
            def rstd(b, mv, ve, rs, s_mv, s_ve, s_rstd):
                pool.wait_ge(s_mv, b.n(1, 1))
                pool.tensor_tensor(ve[:], mv[:, :, 1], eps[0:QN, 0:QT], ALU.add).then_inc(s_ve, 1)
                pool.wait_ge(s_ve, b.n(1, 1))
                pool.tensor_tensor(rs[:], ve[:], neg_half[0:QN, 0:QT], ALU.pow).then_inc(s_rstd, 1)

            def low_x(b):
                pool.wait_ge(xT_h, b.n(1, 1))
                pool.tensor_tensor(xT[1][:], xv[:], xT[0][:].bitcast(F32), ALU.subtract).then_inc(xT_l, 1)

            def residual(b, t):
                if t == 0:
                    pool.wait_ge(gate_loaded, b.n(16, 16))
                    pool.wait_ge(res_loaded, b.n(16, 16))
                pool.wait_ge(proj_done, b.n(2, t + 1))
                pool.tensor_tensor(y[:, t], y[:, t], gate[:], ALU.mult).then_inc(gated, 1)
                pool.wait_ge(gated, b.n(2, t + 1))
                pool.tensor_tensor(y[:, t], y[:, t], x_res[:, t], ALU.add).then_inc(summed, 1)

            def body(b, att, nxt, prv, old):
                a, z = b.plus(1), b.plus(-1)
                if nxt:
                    low_x(a)
                if far(b):
                    rstd(b.plus(2), mv1, ve1, rs1, mvs1, vareps1, rstd1)
                if prv:
                    for t in range(QT):
                        residual(z, t)
                    rstd(z, mv2, ve2, rs2, mvs2, vareps2, rstd2)

            a = Batch(0)
            rstd(a, mv1, ve1, rs1, mvs1, vareps1, rstd1)
            low_x(a)
            rstd(a.plus(1), mv1, ve1, rs1, mvs1, vareps1, rstd1)
            bodies(pool, body)


def cross_phase(nc, ctx_in_dram, w_kvc, b_kvc_t, qc, m_dram, o_dram, ident, neg_half, eps):
    with ExitStack() as ctx:
        sb, ps, sem = alloc(nc, ctx, "cross")
        ROWS = TERMS * HD + 2
        wkv = [sb(f"wkv_{s}", [P, KC, 2 * H], F32R) for s in "hl"]
        bkv = sb("bkv", [P, 2 * KC])
        c_in = sb("c_in", [SN, ST, H])
        load_phase(nc, "cross", [(w_kvc, wkv[0], wkv[1], 1.0)],
                   [(bkv[:], b_kvc_t), (c_in[:], ctx_in_dram[0].rearrange("(t p) n -> p t n", p=SN))])
        kst = sb("kst", [ROWS, KC, HPG, S], F32R)
        qst = sb("qst", [ROWS, KC, HPG, N], F32R)
        nat = [sb(f"nat_{s}", [P, KC, S], F32R) for s in "hl"]
        cT = [sb(f"cT_{s}", [P, KC, S], F32R) for s in "hl"]
        vt = sb("vt", [SN, 2, ST, H])
        prT = sb("prT", [SN, HPG, ST, N])
        ou = sb("ou", [P, 2, N])
        part = sb("part", [SN, 2, N])
        psum = sb("psum", [SN, HPG, N])
        ones = sb("ones", [SN, HD])
        nmax = sb("nmax", [QN, 2, HPG, QT])
        mrow = [sb(f"mrow_{s}", [HPG, N], F32R) for s in "hl"]
        rb = sb("rb", [P, N])
        st = sb("st", [SN, ST, 6])
        turn = sb("turn", [1, 1])
        mv = sb("mv", [SN, ST, 2])
        ve, rs, nm = sb("ve", [SN, ST]), sb("rs", [SN, ST]), sb("nm", [SN, ST])

        sc_ps = [ps(f"sc_ps{i}", (P, 1024)) for i in range(QT)]
        tr_ps = [ps(f"tr_ps{i}") for i in range(2)]
        pj_ps = ps("pj_ps")
        or_ps = ps("or_ps")
        SC0 = 512 - SHALF[0]
        R0 = 256

        c_loaded, stats_done, mvs, vareps, rstd, nmr, chat = (sem(s) for s in ("c_loaded", "stats_done", "mvs", "vareps", "rstd", "nmr", "chat"))
        cT_ps, cT_h, cT_l = sem("cT_ps"), sem("cT_h"), sem("cT_l")
        k_ps, k_h, k_l = sem("k_ps"), sem("k_h"), sem("k_l")
        v_ps, v_done = sem("v_ps"), sem("v_done")
        k_stacked = [sem(f"k_stacked{g}") for g in range(KC)]
        q_stacked = [sem(f"q_stacked{g}") for g in range(KC)]
        scored_t = [sem(f"scored_t{t}") for t in range(QT)]
        maxed, m_ps, m_h, m_l, m_out, m_in = (sem(s) for s in ("maxed", "m_ps", "m_h", "m_l", "m_out", "m_in"))
        st_ps, exped, pre_summed, p_summed, constant = (sem(s) for s in ("st_ps", "exped", "pre_summed", "p_summed", "constant"))
        pv_done, sum_ps, inverted, o_done = (sem(s) for s in ("pv_done", "sum_ps", "inverted", "o_done"))
        o_out = [sem(f"o_out{i}") for i in range(2)]
        STACK, QSTACK = 16 * HPG * TERMS, 16 * TERMS
        HALVES = ((0, SHALF[0]), (SHALF[0], SHALF[1]))
        FILL = [[("k", 0, 0)], [("k", 0, 1)], [("k", 1, 0)], [("k", 1, 1), ("m", 0)], [("k", 2, 0)], [("k", 2, 1)],
                [("v", 0)], [("v", 1), ("m", 1)], [("k", 3, 0)], [("k", 3, 1)], [("v", 2), ("c", 0)],
                [("v", 3), ("c", 1), ("m", 2)], [("v", 4), ("c", 2)], [("c", 3)], [("v", 5), ("c", 4)],
                [("c", 5), ("m", 3)]]
        ORDER = [f for step in FILL for f in step]
        LAG = 6
        block = ctx.enter_context(nc.Block())

        def bodies(eng, body):
            body(Batch(0), True, True, False)
            body(Batch(1), True, True, True)
            with eng.Fori(0, (B - 4) // 2) as i:
                body(Batch(2, i), True, True, True)
                body(Batch(3, i), True, True, True)
            body(Batch(B - 2), True, True, True)
            body(Batch(B - 1), True, False, True)
            body(Batch(B), False, False, True)

        def far(b):
            return not (isinstance(b.i, int) and b.c > B - 3)

        def exists(b, kind):
            at = 2 if not isinstance(b.i, int) else b.c
            return {"k": at < B - 1, "v": at < B - 1, "c": at < B - 2, "m": 0 <= at < B}[kind]

        OF = {"k": 1, "v": 1, "c": 2, "m": 0}

        def fill_at(b, h, kinds):
            return [(f, b) for f in FILL[h] if f[0] in kinds and exists(b, f[0])]

        def bank_free(b, fill):
            before = [(b.plus(-1), f) for f in ORDER if exists(b.plus(-1) if isinstance(b.i, int) else b, f[0])]
            before += [(b, f) for f in ORDER[:ORDER.index(fill)] if exists(b, f[0])]
            o, (kind, *where) = before[-1]
            o = o.plus(OF[kind])
            if kind == "c":
                return cT_l, o.n(ST, where[0] + 1)
            if kind == "k":
                return k_l, o.n(2 * KC, 2 * where[0] + where[1] + 1)
            if kind == "m":
                return m_l, o.n(KC, where[0] + 1)
            return v_done, o.n(ST, where[0] + 1)

        def late(b, h, att, prv):
            if h >= LAG:
                return [(b, h - LAG)] if att else []
            return [(b.plus(-1), h - LAG + NH)] if prv else []

        def late_pv(b, h, att, prv):
            heads = [h - LAG - 2, h - LAG - 1] if h % HPG == 0 else [h - LAG - 1] if h % HPG < 3 else []
            if heads and heads[0] >= 0:
                return [(b, l) for l in heads] if att else []
            return [(b.plus(-1), l + NH) for l in heads] if prv else []

        def late_group(b, h, att, prv):
            if h % HPG != 3:
                return []
            g = (h - LAG - HPG - 1) // HPG
            if g >= 0:
                return [(b, g)] if att else []
            return [(b.plus(-1), g + KC)] if prv else []

        @block.sync
        def _(sp):
            def load_c(b):
                wait(sp, cT_ps, b.n(ST, 0))
                sp.dma_start(c_in[:], ctx_in_dram[bass.ds(b.index(), 1)].rearrange("a (t p) n -> p (a t) n", p=SN)).then_inc(c_loaded, 16)

            def load_q(b, g):
                wait(sp, st_ps, b.n(3 * NH, 3 * HPG * (g + 1) - 3 * NH))
                for r, s in enumerate((0, 0, 1)):
                    src = qc[bass.ds(b.index(), 1), s, g * P:(g + 1) * P].rearrange("a (j d) t -> d (a j) t", d=HD)
                    sp.dma_start(qst[HD * r:HD * r + HD, g].bitcast(F32), src).then_inc(q_stacked[g], 16)

            def stack_k(b, g):
                sp.wait_ge(k_l, b.n(2 * KC, 2 * g + 2))
                wait(sp, st_ps, b.n(3 * NH, 3 * HPG * (g + 1) - 3 * NH))
                for j in range(HPG):
                    for r, s in enumerate((0, 1, 0)):
                        sp.dma_start(kst[HD * r:HD * r + HD, g, j].bitcast(F32),
                                     nat[s][HD * j:HD * j + HD, g].bitcast(F32)).then_inc(k_stacked[g], 16)

            def body(b, att, nxt, prv):
                a = b.plus(1)
                if far(b):
                    load_c(b.plus(2))
                for g in (2, 3, 0, 1):
                    o = b if g >= 2 else a
                    if (att and not first(b)) if g >= 2 else nxt:
                        load_q(o, g)
                        stack_k(o, g)

            def first(b):
                return isinstance(b.i, int) and b.c == 0

            load_c(Batch(1))
            for g in range(KC):
                load_q(Batch(0), g)
            for g in range(KC):
                stack_k(Batch(0), g)
            bodies(sp, body)

        @block.tensor
        def _(pe):
            def fill_(body_b, fill, chained=True):
                if chained:
                    pe.wait_ge(*bank_free(body_b, fill))
                kind, *where = fill
                b = body_b.plus(OF[kind])
                if kind == "m":
                    g, = where
                    pe.wait_ge(maxed, b.n(NH * QT, HPG * QT * (g + 1)))
                    for t in range(QT):
                        last = pe.transpose(pj_ps[0:HPG, t * QN:(t + 1) * QN], nmax[:, g % 2, :, t], ident[0:QN, 0:QN])
                    last.then_inc(m_ps, 1)
                if kind == "c":
                    t, = where
                    pe.wait_ge(chat, b.n(ST, t + 1))
                    for k in range(KC):
                        last = pe.transpose(pj_ps[:, k * SN:(k + 1) * SN], c_in[:, t, k * P:(k + 1) * P], ident[0:SN, 0:SN])
                    last.then_inc(cT_ps, 1)
                if kind == "k":
                    g, half = where
                    pe.wait_ge(cT_l, b.n(ST, ST if half else 4))
                    c0, cn = HALVES[half]
                    for k in range(KC):
                        last = product(pe, pj_ps[:, 0:cn], tuple(w[:, k, g * P:(g + 1) * P] for w in wkv),
                                       tuple(c[:, k, c0:c0 + cn] for c in cT), k == 0, k == KC - 1)
                    last.then_inc(k_ps, 1)
                if kind == "v":
                    t, = where
                    pe.wait_ge(cT_l, b.n(ST, t + 1))
                    for k in range(KC):
                        last = product(pe, pj_ps[0:SN, :], tuple(c[:, k, t * SN:(t + 1) * SN] for c in cT),
                                       tuple(w[:, k, H:2 * H] for w in wkv), k == 0, k == KC - 1)
                    last.then_inc(v_ps, 1)

            def score(b, h):
                g, j = h // HPG, h % HPG
                if j == 0:
                    pe.wait_ge(k_stacked[g], b.n(STACK, STACK))
                    pe.wait_ge(q_stacked[g], b.n(QSTACK, QSTACK))
                for t in range(QT):
                    wait(pe, maxed, b.n(NH * QT, h * QT + t - 1))
                    for c0, cn in HALVES:
                        last = pe.matmul(sc_ps[t][0:QN, SC0 + c0:SC0 + c0 + cn], qst[0:TERMS * HD, g, j, t * QN:(t + 1) * QN],
                                         kst[0:TERMS * HD, g, j, c0:c0 + cn], start=True, stop=True)
                    last.then_inc(scored_t[t], 1)

            def score_t(b, h, c):
                g, j = h // HPG, h % HPG
                if j == 0 and c == 0:
                    pe.wait_ge(m_in, b.n(16 * KC, 16 * (g + 1)))
                wait(pe, exped, b.n(3 * NH, 3 * h + c - 1))
                for m in range(2):
                    kt = 2 * c + m
                    last = pe.matmul(tr_ps[(3 * h + c) % 2][0:SN, m * N:(m + 1) * N], kst[:, g, j, kt * SN:(kt + 1) * SN],
                                     qst[:, g, j, :], start=True, stop=True)
                last.then_inc(st_ps, 1)

            def pv(b, h):
                g, j = h // HPG, h % HPG
                ch = h * HD
                pe.wait_ge(exped, b.n(3 * NH, 3 * h + 3))
                if h == 0:
                    pe.wait_ge(v_done, b.n(ST, ST))
                if j == 0:
                    wait(pe, o_done, b.n(KC, g))
                for kt in range(ST):
                    last = pe.matmul(or_ps[HD * j:HD * j + HD, 0:N], vt[:, b.par, kt, ch:ch + HD], prT[:, j, kt],
                                     start=kt == 0, stop=kt == ST - 1)
                last.then_inc(pv_done, 1)

            def sums(b, h):
                j = h % HPG
                pe.wait_ge(p_summed, b.n(NH, h + 1))
                pe.matmul(or_ps[HD * j:HD * j + HD, R0:R0 + N], ones[:], psum[:, j], start=True, stop=True).then_inc(sum_ps, 1)

            def body(b, att, nxt, prv):
                a = b.plus(1)
                for h in range(NH):
                    for c in range(ST // 2):
                        for f, o in fill_at(b, h, "kv") if c == 2 else ():
                            fill_(o, f)
                        for o, l in late(b, h, att, prv):
                            score_t(o, l, c)
                    for o, l in late_pv(b, h, att, prv):
                        pv(o, l)
                    for f, o in fill_at(b, h, "c"):
                        fill_(o, f)
                    if h < NH - 1 and att:
                        score(b, h + 1)
                    if h == NH - 1 and nxt:
                        score(a, 0)
                    for o, l in late_pv(b, h, att, prv):
                        sums(o, l)
                    for f, o in fill_at(b, h, "m"):
                        fill_(o, f)

            pe.wait_ge(constant, 2)
            for t in range(ST):
                wait(pe, cT_l, t)
                fill_(Batch(-2), ("c", t), False)
            for h in range(NH):
                for f, o in fill_at(Batch(-1), h, "kvc"):
                    fill_(o, f)
            score(Batch(0), 0)
            bodies(pe, body)

        @block.vector
        def _(dve):
            def stats(b, t):
                if t == 0:
                    wait(dve, c_loaded, b.n(16, 0))
                dve.bn_stats(st[:, t], c_in[:, t]).then_inc(stats_done, 1)

            def aggregate(b, half):
                at = range(3 * half, 3 * half + 3)
                dve.wait_ge(stats_done, b.n(ST, 3 * half + 3))
                dve.memset(turn[:], 0.0)
                for t in at:
                    last = dve.bn_aggr(mv[:, t], st[:, t])
                last.then_inc(mvs, 1)

            def neg_mean(b, half):
                dve.wait_ge(rstd, b.n(2, half + 1))
                at = slice(3 * half, 3 * half + 3)
                dve.scalar_tensor_tensor(out=nm[:, at], in0=mv[:, at, 0], scalar=-1.0, in1=rs[:, at], op0=ALU.mult, op1=ALU.mult).then_inc(nmr, 1)

            def low(b, fill):
                kind, *where = fill
                b = b.plus(OF[kind])
                if kind == "m":
                    g, = where
                    dve.wait_ge(m_h, b.n(KC, g + 1))
                    dve.tensor_tensor(mrow[1][:], pj_ps[0:HPG, 0:N], mrow[0][:].bitcast(F32), ALU.subtract).then_inc(m_l, 1)
                if kind == "c":
                    t, = where
                    dve.wait_ge(cT_h, b.n(ST, t + 1))
                    at = slice(t * SN, (t + 1) * SN)
                    dve.tensor_tensor(cT[1][:, :, at], pj_ps[:, 0:KC * SN].rearrange("p (k n) -> p k n", k=KC),
                                      cT[0][:, :, at].bitcast(F32), ALU.subtract).then_inc(cT_l, 1)
                if kind == "k":
                    g, half = where
                    c0, cn = HALVES[half]
                    dve.wait_ge(k_h, b.n(2 * KC, 2 * g + half + 1))
                    dve.scalar_tensor_tensor(out=nat[1][:, g, c0:c0 + cn], in0=pj_ps[:, 0:cn], scalar=bkv[:, g:g + 1],
                                             in1=nat[0][:, g, c0:c0 + cn].bitcast(F32), op0=ALU.add, op1=ALU.subtract).then_inc(k_l, 1)
                if kind == "v":
                    t, = where
                    dve.wait_ge(v_ps, b.n(ST, t + 1))
                    wait(dve, pv_done, b.n(NH, -NH))
                    dve.tensor_copy(vt[:, b.par, t], pj_ps[0:SN, :]).then_inc(v_done, 1)

            def row_max(b, h, t):
                g, j = h // HPG, h % HPG
                dve.wait_ge(scored_t[t], b.n(NH, h + 1))
                if j == 0:
                    wait(dve, m_ps, b.n(KC, g - 1))
                dve.tensor_reduce(nmax[:, g % 2, j, t:t + 1], sc_ps[t][0:QN, SC0:SC0 + S], AX_X, ALU.max, negate=True).then_inc(maxed, 1)

            def normalize(b, g):
                dve.wait_ge(sum_ps, b.n(NH, HPG * (g + 1)))
                wait(dve, o_done, b.n(KC, g))
                dve.reciprocal(rb[:], or_ps[:, R0:R0 + N]).then_inc(inverted, 1)
                dve.wait_ge(pv_done, b.n(NH, HPG * (g + 1)))
                wait(dve, o_out[g % 2], b.n(32, 16 * (g // 2)))
                dve.wait_ge(inverted, b.n(KC, g + 1))
                dve.tensor_tensor(ou[:, g % 2], or_ps[:, 0:N], rb[:], ALU.mult).then_inc(o_done, 1)

            def body(b, att, nxt, prv):
                a = b.plus(1)
                for h in range(NH):
                    for f, o in fill_at(b, h, "kvc"):
                        low(o, f)
                    for t in range(QT):
                        if h < NH - 1 and att:
                            row_max(b, h + 1, t)
                        if h == NH - 1 and nxt:
                            row_max(a, 0, t)
                        for f, o in fill_at(b, h, "m") if t == 0 else ():
                            low(o, f)
                    for o, g in late_group(b, h, att, prv):
                        normalize(o, g)
                    if far(b) and 2 <= h < 2 + ST:
                        stats(b.plus(2), h - 2)
                    if far(b) and h in (5, 8):
                        aggregate(b.plus(2), (h - 5) // 3)
                    if far(b) and h in (7, 10):
                        neg_mean(b.plus(2), (h - 7) // 3)

            def norm(b):
                for t in range(ST):
                    stats(b, t)
                for half in range(2):
                    aggregate(b, half)
                    neg_mean(b, half)

            dve.memset(kst[TERMS * HD:ROWS].bitcast(F32), 1.0).then_inc(constant, 1)
            dve.memset(ones[:], 1.0).then_inc(constant, 1)
            norm(Batch(0))
            for t in range(ST):
                low(Batch(-2), ("c", t))
            for h in range(NH):
                if h == 6:
                    norm(Batch(1))
                for f, o in fill_at(Batch(-1), h, "kvc"):
                    low(o, f)
            for t in range(QT):
                row_max(Batch(0), 0, t)
            bodies(dve, body)

        @block.scalar
        def _(act):
            def apply_ln(b, t):
                if t % 3 == 0:
                    act.wait_ge(nmr, b.n(2, t // 3 + 1))
                act.activation(c_in[:, t], c_in[:, t], ACT.Identity, bias=nm[:, t:t + 1], scale=rs[:, t:t + 1]).then_inc(chat, 1)

            def high(b, fill):
                kind, *where = fill
                b = b.plus(OF[kind])
                if kind == "m":
                    g, = where
                    act.wait_ge(m_ps, b.n(KC, g + 1))
                    wait(act, m_out, b.n(32 * KC, 32 * g))
                    act.copy(mrow[0][:], pj_ps[0:HPG, 0:N]).then_inc(m_h, 1)
                if kind == "c":
                    t, = where
                    act.wait_ge(cT_ps, b.n(ST, t + 1))
                    wait(act, v_ps, b.n(ST, t + 1 - ST))
                    wait(act, k_ps, b.n(2 * KC, 0 if t >= 4 else -1))
                    act.copy(cT[0][:, :, t * SN:(t + 1) * SN], pj_ps[:, 0:KC * SN].rearrange("p (k n) -> p k n", k=KC)).then_inc(cT_h, 1)
                if kind == "k":
                    g, half = where
                    c0, cn = HALVES[half]
                    act.wait_ge(k_ps, b.n(2 * KC, 2 * g + half + 1))
                    if half == 0:
                        wait(act, k_stacked[g], b.n(STACK, 0))
                    act.activation(nat[0][:, g, c0:c0 + cn], pj_ps[:, 0:cn], ACT.Identity, bias=bkv[:, g:g + 1]).then_inc(k_h, 1)

            def exps(b, h, c):
                act.wait_ge(st_ps, b.n(3 * NH, 3 * h + c + 1))
                if c == 0:
                    wait(act, p_summed, b.n(NH, h - HPG + 1))
                    wait(act, pv_done, b.n(NH, h - HPG + 1))
                act.activation(prT[:, h % HPG, 2 * c:2 * c + 2], tr_ps[(3 * h + c) % 2][0:SN, 0:2 * N].rearrange("p (k t) -> p k t", k=2),
                               ACT.Exp).then_inc(exped, 1)

            def maxima_out(b, g):
                act.wait_ge(m_l, b.n(KC, g + 1))
                wait(act, m_in, b.n(16 * KC, 16 * (g - 1)))
                for s in range(2):
                    act.dma_start(m_dram[g % 2, s], mrow[s][:].bitcast(F32)).then_inc(m_out, 16)

            def maxima_in(b, g):
                act.wait_ge(m_out, b.n(32 * KC, 32 * (g + 1)))
                wait(act, st_ps, b.n(3 * NH, 3 * HPG * (g + 1) - 3 * NH))
                act.dma_start(qst[TERMS * HD:ROWS, g].rearrange("p j t -> p (j t)").bitcast(F32),
                              m_dram[g % 2].rearrange("s j t -> s (j t)")).then_inc(m_in, 16)

            def body(b, att, nxt, prv):
                for h in range(NH):
                    if h == 0 and prv:
                        maxima_out(b.plus(-1), KC - 1)
                    if h == 1 and prv:
                        maxima_in(b.plus(-1), KC - 1)
                    if h % HPG == 0 and h > 0 and att:
                        maxima_out(b, h // HPG - 1)
                    if h % HPG == 1 and h > 1 and att:
                        maxima_in(b, h // HPG - 1)
                    for c in range(ST // 2):
                        for f, o in fill_at(b, h, "kv") if c == 2 else ():
                            high(o, f)
                        for o, l in late(b, h, att, prv):
                            exps(o, l, c)
                    for f, o in fill_at(b, h, "cm"):
                        high(o, f)
                    if far(b) and 8 <= h < 8 + ST:
                        apply_ln(b.plus(2), h - 8)

            for t in range(ST):
                apply_ln(Batch(0), t)
            for t in range(ST):
                high(Batch(-2), ("c", t))
            for h in range(NH):
                for t in range(ST) if h == 7 else ():
                    apply_ln(Batch(1), t)
                for f, o in fill_at(Batch(-1), h, "kvc"):
                    high(o, f)
            bodies(act, body)

        @block.gpsimd
        def _(pool):
            def inverse_std(b, half):
                at = slice(3 * half, 3 * half + 3)
                pool.wait_ge(mvs, b.n(2, half + 1))
                pool.tensor_tensor(ve[:, at], mv[:, at, 1], eps[0:SN, 0:3], ALU.add).then_inc(vareps, 1)
                pool.wait_ge(vareps, b.n(2, half + 1))
                pool.tensor_tensor(rs[:, at], ve[:, at], neg_half[0:SN, 0:3], ALU.pow).then_inc(rstd, 1)

            def store(b, g):
                pool.wait_ge(o_done, b.n(KC, g + 1))
                pool.dma_start(o_dram[bass.ds(b.index(), 1), g * P:(g + 1) * P].rearrange("a p t -> p (a t)"), ou[:, g % 2]).then_inc(o_out[g % 2], 16)

            def sum_p(b, h):
                j = h % HPG
                pool.wait_ge(exped, b.n(3 * NH, 3 * h + 3))
                wait(pool, sum_ps, b.n(NH, h - HPG + 1))
                wait(pool, p_summed, b.n(NH, h))
                pool.tensor_tensor(part[:], prT[:, j, 0:2], prT[:, j, 2:4], ALU.add).then_inc(pre_summed, 1)
                pool.wait_ge(pre_summed, b.n(2 * NH, 2 * h + 1))
                pool.tensor_tensor(part[:], part[:], prT[:, j, 4:6], ALU.add).then_inc(pre_summed, 1)
                pool.wait_ge(pre_summed, b.n(2 * NH, 2 * h + 2))
                pool.tensor_tensor(psum[:, j], part[:, 0], part[:, 1], ALU.add).then_inc(p_summed, 1)

            def body(b, att, nxt, prv):
                for h in range(NH):
                    for o, g in late_group(b, h - 1, att, prv):
                        store(o, g)
                    if far(b) and h in (6, 9):
                        inverse_std(b.plus(2), (h - 6) // 3)
                    for o, l in late(b, h, att, prv):
                        sum_p(o, l)

            for b in (Batch(0), Batch(1)):
                for half in range(2):
                    inverse_std(b, half)
            bodies(pool, body)
            for i in range(2):
                pool.wait_ge(o_out[i], 32 * B)


def mlp_phase(nc, x1, o_dram, b_vc_t, w_cproj, b_cproj, w_mlp1, b_mlp1_t, w_mlp2, b_mlp2, gates, out, mod_t, ident, neg_half, eps):
    MC = MLP // P
    PAIRS = MC // 2
    GR = 3
    W2_RING = 8
    with ExitStack() as ctx:
        sb, ps, sem = alloc(nc, ctx, "mlp")
        wcp = [sb(f"wcp_{s}", [P, KC, H], F32R) for s in "hl"]
        w1 = [sb(f"w1_{s}", [P, KC, MLP], F32R) for s in "hl"]
        w2 = [sb(f"w2_{s}", [P, MC, H], F32R) for s in "hl"]
        bv = sb("bv", [P, KC])
        b1 = sb("b1", [P, MC])
        bcp, b2 = sb("bcp", [QN, H]), sb("b2", [QN, H])
        rows = lambda v: v.rearrange("(a n) -> a n", a=1).broadcast_to([QN, H])
        o_in = sb("o_in", [P, KC, N])
        load_phase(nc, "mlp", [(w_cproj, wcp[0], wcp[1], 1.0), (w_mlp1, w1[0], w1[1], 1.0)],
                   [(bv[:], b_vc_t), (b1[:], b_mlp1_t), (bcp[:], rows(b_cproj)), (b2[:], rows(b_mlp2)),
                    (o_in[:], o_dram[0].rearrange("(g p) t -> p g t", p=P))])
        oT = [sb(f"oT_{s}", [P, KC, N], F32R) for s in "hl"]
        x_in = sb("x_in", [QN, QT, H])
        x2 = sb("x2", [QN, 2, QT, H])
        y = sb("y", [QN, QT, H])
        gate = sb("gate", [QN, H])
        xv = sb("xv", [P, KC, N])
        xT = [sb(f"xT_{s}", [P, KC, N], F32R) for s in "hl"]
        hv = sb("hv", [P, 2, 2, N])
        hT = [sb(f"hT_{s}", [P, GR, 2, N], F32R) for s in "hl"]
        stage = [sb(f"stage{s}", [P, H]) for s in range(W2_RING)]
        w2_views = split_views([(w_mlp2, w2[0], w2[1], 1.0)], stage)
        turn = sb("turn", [1, 1])
        st, mv = sb("st", [QN, QT, 6]), sb("mv", [QN, QT, 2])
        ve, rs, nm = sb("ve", [QN, QT]), sb("rs", [QN, QT]), sb("nm", [QN, QT])

        h_ps = [ps(f"h_ps{i}") for i in range(2)]
        a_ps = [ps(f"a_ps{i}") for i in range(2)]
        c_ps = [ps(f"c_ps{i}") for i in range(2)]
        t_ps = [ps(f"t_ps{i}") for i in range(2)]

        o_loaded, x_loaded, gate_loaded = sem("o_loaded"), sem("x_loaded"), sem("gate_loaded")
        oT_h, oT_l, cp_ps, cp_done, x2_done = (sem(s) for s in ("oT_h", "oT_l", "cp_ps", "cp_done", "x2_done"))
        stats_done, mvs, vareps, rstd, nmr, xhat = (sem(s) for s in ("stats_done", "mvs", "vareps", "rstd", "nmr", "xhat"))
        xT_ps, xT_v, xT_h, xT_l = sem("xT_ps"), sem("xT_v"), sem("xT_h"), sem("xT_l")
        h_mm, h_act, h_h, h_l, h_used = (sem(s) for s in ("h_mm", "h_act", "h_h", "h_l", "h_used"))
        y_done, gated, summed, out_done = (sem(s) for s in ("y_done", "gated", "summed", "out_done"))
        w2_in = [sem(f"w2_in{s}") for s in range(W2_RING)]
        w2_h, w2_l = sem("w2_h"), sem("w2_l")
        block = ctx.enter_context(nc.Block())

        def bodies(eng, body):
            body(Batch(0), True, True, False)
            body(Batch(1), True, True, True)
            with eng.Fori(0, (B - 4) // 2) as i:
                body(Batch(2, i), True, True, True)
                body(Batch(3, i), True, True, True)
            body(Batch(B - 2), True, True, True)
            body(Batch(B - 1), True, False, True)
            body(Batch(B), False, False, True)

        @block.sync
        def _(sp):
            def load(b):
                wait(sp, oT_l, b.n(KC, 0))
                sp.dma_start(o_in[:], o_dram[bass.ds(b.index(), 1)].rearrange("a (g p) t -> p (a g) t", p=P)).then_inc(o_loaded, 16)
                wait(sp, xT_ps, b.n(2, 0))
                sp.dma_start(x_in[:], x1[bass.ds(b.index(), 1)].rearrange("a (t p) n -> p (a t) n", p=QN)).then_inc(x_loaded, 16)

            def finish(b):
                wait(sp, gated, b.n(2, 0))
                sp.dma_start(gate[:], gates[1, bass.ds(b.index(), 1)].broadcast_to([QN, H])).then_inc(gate_loaded, 16)
                for t in range(QT):
                    sp.wait_ge(summed, b.n(2, t + 1))
                    sp.dma_start(out[bass.ds(b.index(), 1), t * QN:(t + 1) * QN].rearrange("a p n -> p (a n)"), y[:, t]).then_inc(out_done, 16)

            def body(b, att, nxt, prv):
                if prv:
                    finish(b.plus(-1))
                if nxt and not (isinstance(b.i, int) and b.c == B - 2):
                    load(b.plus(2))

            sp.dma_start(x_in[:], x1[0].rearrange("(t p) n -> p t n", p=QN)).then_inc(x_loaded, 16)
            for t, (src, st_, _, _, _) in enumerate(w2_views):
                wait(sp, w2_l, t - W2_RING + 1)
                sp.dma_start(st_, src).then_inc(w2_in[t % W2_RING], 16)
            load(Batch(1))
            bodies(sp, body)
            sp.wait_ge(out_done, 32 * B)

        @block.tensor
        def _(pe):
            def cproj(b, t):
                pe.wait_ge(oT_l, b.n(KC, KC))
                wait(pe, cp_done, b.n(2, t - 1))
                for k in range(KC):
                    last = product(pe, c_ps[t][0:QN, :], tuple(o[:, k, t * QN:(t + 1) * QN] for o in oT),
                                   tuple(w[:, k] for w in wcp), k == 0, k == KC - 1)
                last.then_inc(cp_ps, 1)

            def trans_x(b):
                pe.wait_ge(xhat, b.n(1, 1))
                wait(pe, xT_v, b.n(1, 0))
                for c in range(2):
                    for k in range(2):
                        for t in range(QT):
                            at = k * N + t * QN
                            last = pe.transpose(t_ps[c][:, at:at + QN], x_in[:, t, (2 * c + k) * P:(2 * c + k + 1) * P], ident[0:QN, 0:QN])
                    last.then_inc(xT_ps, 1)

            def hidden(b, p):
                if p == 0:
                    pe.wait_ge(xT_l, b.n(1, 1))
                wait(pe, h_act, b.n(PAIRS, p - 1))
                for m in range(2):
                    at = (2 * p + m) * P
                    for k in range(KC):
                        last = product(pe, h_ps[p % 2][:, m * N:(m + 1) * N], tuple(w[:, k, at:at + P] for w in w1),
                                       tuple(v[:, k] for v in xT), k == 0, k == KC - 1)
                last.then_inc(h_mm, 1)

            def output(b, p, u):
                pe.wait_ge(h_l, b.n(PAIRS, p + 1))
                if p == 0 and isinstance(b.i, int) and b.c == 0:
                    pe.wait_ge(w2_l, len(w2_views))
                if p == 0:
                    wait(pe, y_done, b.n(2, 0))
                for m in range(2):
                    for t in range(QT):
                        last = product(pe, a_ps[t][0:QN, :], tuple(v[:, u % GR, m, t * QN:(t + 1) * QN] for v in hT),
                                       tuple(w[:, 2 * p + m] for w in w2), p == 0 and m == 0, p == PAIRS - 1 and m == 1)
                last.then_inc(h_used, 1)

            def body(b, att, nxt, prv):
                a = b.plus(1)
                for p in range(PAIRS):
                    if att:
                        hidden(b, p)
                        if p >= 2:
                            output(b, p - 2, p - 2)
                    if nxt and p in (1, 2):
                        cproj(a, p - 1)
                    if nxt and p == 6:
                        trans_x(a)
                if att:
                    output(b, PAIRS - 2, PAIRS - 2)
                    output(b, PAIRS - 1, PAIRS - 1)

            for t in range(QT):
                cproj(Batch(0), t)
            trans_x(Batch(0))
            bodies(pe, body)

        @block.vector
        def _(dve):
            def low_o(b):
                for g in range(KC):
                    dve.wait_ge(oT_h, b.n(KC, g + 1))
                    dve.scalar_tensor_tensor(out=oT[1][:, g], in0=o_in[:, g], scalar=bv[:, g:g + 1],
                                             in1=oT[0][:, g].bitcast(F32), op0=ALU.add, op1=ALU.subtract).then_inc(oT_l, 1)

            def residual(b, t):
                dve.wait_ge(cp_ps, b.n(2, t + 1))
                wait(dve, summed, b.n(2, -2))
                dve.tensor_tensor(x2[:, b.par, t], c_ps[t][0:QN, :], bcp[:], ALU.add).then_inc(cp_done, 1)

            def stats(b):
                for t in range(QT):
                    dve.wait_ge(x2_done, b.n(2, t + 1))
                    last = dve.bn_stats(st[:, t], x2[:, b.par, t])
                last.then_inc(stats_done, 1)
                dve.wait_ge(stats_done, b.n(1, 1))
                dve.memset(turn[:], 0.0)
                for t in range(QT):
                    last = dve.bn_aggr(mv[:, t], st[:, t])
                last.then_inc(mvs, 1)

            def neg_mean(b):
                dve.wait_ge(rstd, b.n(1, 1))
                dve.scalar_tensor_tensor(out=nm[:], in0=mv[:, :, 0], scalar=-1.0, in1=rs[:], op0=ALU.mult, op1=ALU.mult).then_inc(nmr, 1)

            def modulate(b):
                wait(dve, xT_l, b.n(1, 0))
                for c in range(2):
                    dve.wait_ge(xT_ps, b.n(2, c + 1))
                    for k in range(2):
                        m = 2 * c + k
                        last = dve.tensor_scalar(xv[:, m], t_ps[c][:, k * N:(k + 1) * N], mod_t[:, KC + m, bass.ds(b.index(), 1)],
                                                 mod_t[:, m, bass.ds(b.index(), 1)], ALU.mult, ALU.add)
                last.then_inc(xT_v, 1)

            def split_h(b, p):
                dve.wait_ge(h_act, b.n(PAIRS, p + 1))
                wait(dve, h_used, b.n(PAIRS, p - GR + 1))
                dve.tensor_copy(hT[0][:, p % GR], hv[:, p % 2]).then_inc(h_h, 1)
                dve.wait_ge(h_h, b.n(PAIRS, p + 1))
                dve.tensor_tensor(hT[1][:, p % GR], hv[:, p % 2], hT[0][:, p % GR].bitcast(F32), ALU.subtract).then_inc(h_l, 1)

            def add_bias(b, t):
                dve.wait_ge(h_used, b.n(PAIRS, PAIRS))
                wait(dve, out_done, b.n(32, 0))
                dve.tensor_tensor(y[:, t], a_ps[t][0:QN, :], b2[:], ALU.add).then_inc(y_done, 1)

            def body(b, att, nxt, prv):
                a, z = b.plus(1), b.plus(-1)
                if prv:
                    add_bias(z, 0)
                    add_bias(z, 1)
                for p in range(PAIRS):
                    if att:
                        split_h(b, p)
                    if nxt and p == 0:
                        low_o(a)
                    if nxt and p in (2, 3):
                        residual(a, p - 2)
                    if nxt and p == 4:
                        stats(a)
                    if nxt and p == 5:
                        neg_mean(a)
                    if nxt and p == 6:
                        modulate(a)

            def low_w2(first, last):
                for t in range(first, last):
                    _, st_, hi, lo, _ = w2_views[t]
                    dve.wait_ge(w2_h, t + 1)
                    dve.tensor_tensor(lo, st_, hi.bitcast(F32), ALU.subtract).then_inc(w2_l, 1)

            a = Batch(0)
            low_o(a)
            low_w2(0, 3)
            residual(a, 0)
            residual(a, 1)
            low_w2(3, 6)
            stats(a)
            low_w2(6, 8)
            neg_mean(a)
            low_w2(8, 12)
            modulate(a)
            low_w2(12, 16)
            bodies(dve, body)

        @block.scalar
        def _(act):
            def high_o(b):
                wait(act, o_loaded, b.n(16, 0))
                wait(act, cp_ps, b.n(2, 0))
                for g in range(KC):
                    act.activation(oT[0][:, g], o_in[:, g], ACT.Identity, bias=bv[:, g:g + 1]).then_inc(oT_h, 1)

            def apply_ln(b):
                act.wait_ge(nmr, b.n(1, 1))
                for t in range(QT):
                    last = act.activation(x_in[:, t], x2[:, b.par, t], ACT.Identity, bias=nm[:, t:t + 1], scale=rs[:, t:t + 1])
                last.then_inc(xhat, 1)

            def high_x(b):
                act.wait_ge(xT_v, b.n(1, 1))
                wait(act, h_mm, b.n(PAIRS, 0))
                act.copy(xT[0][:], xv[:]).then_inc(xT_h, 1)

            def gelu(b, p):
                act.wait_ge(h_mm, b.n(PAIRS, p + 1))
                wait(act, h_l, b.n(PAIRS, p - 1))
                for m in range(2):
                    c = 2 * p + m
                    last = act.activation(hv[:, p % 2, m], h_ps[p % 2][:, m * N:(m + 1) * N], ACT.Gelu_apprx_tanh, bias=b1[:, c:c + 1])
                last.then_inc(h_act, 1)

            def body(b, att, nxt, prv):
                a = b.plus(1)
                for p in range(PAIRS):
                    if att:
                        gelu(b, p)
                    if nxt and p == 0:
                        high_o(a)
                    if nxt and p == 5:
                        apply_ln(a)
                if nxt:
                    high_x(a)

            def high_w2(first, last):
                for t in range(first, last):
                    _, st_, hi, _, _ = w2_views[t]
                    act.wait_ge(w2_in[t % W2_RING], 16 * (t // W2_RING + 1))
                    act.copy(hi, st_).then_inc(w2_h, 1)

            a = Batch(0)
            high_o(a)
            high_w2(0, 8)
            apply_ln(a)
            high_w2(8, 12)
            high_x(a)
            high_w2(12, 16)
            bodies(act, body)

        @block.gpsimd
        def _(pool):
            def add_x1(b, t):
                pool.wait_ge(cp_done, b.n(2, t + 1))
                if t == 0:
                    pool.wait_ge(x_loaded, b.n(16, 16))
                pool.tensor_tensor(x2[:, b.par, t], x2[:, b.par, t], x_in[:, t], ALU.add).then_inc(x2_done, 1)

            def inverse_std(b):
                pool.wait_ge(mvs, b.n(1, 1))
                pool.tensor_tensor(ve[:], mv[:, :, 1], eps[0:QN, 0:QT], ALU.add).then_inc(vareps, 1)
                pool.wait_ge(vareps, b.n(1, 1))
                pool.tensor_tensor(rs[:], ve[:], neg_half[0:QN, 0:QT], ALU.pow).then_inc(rstd, 1)

            def low_x(b):
                pool.wait_ge(xT_h, b.n(1, 1))
                pool.tensor_tensor(xT[1][:], xv[:], xT[0][:].bitcast(F32), ALU.subtract).then_inc(xT_l, 1)

            def gated_sum(b, t):
                if t == 0:
                    pool.wait_ge(gate_loaded, b.n(16, 16))
                pool.wait_ge(y_done, b.n(2, t + 1))
                pool.tensor_tensor(y[:, t], y[:, t], gate[:], ALU.mult).then_inc(gated, 1)
                pool.wait_ge(gated, b.n(2, t + 1))
                pool.tensor_tensor(y[:, t], y[:, t], x2[:, b.par, t], ALU.add).then_inc(summed, 1)

            def front(b):
                for t in range(QT):
                    add_x1(b, t)
                inverse_std(b)
                low_x(b)

            def body(b, att, nxt, prv):
                if prv:
                    for t in range(QT):
                        gated_sum(b.plus(-1), t)
                if nxt:
                    front(b.plus(1))

            front(Batch(0))
            bodies(pool, body)


def build(nc, x, context, cond_t, w_mod, b_mod, w_qkv, b_qkv_t, w_proj, b_proj, w_qc, b_qc_t, w_kvc, b_kvc_t,
          w_cproj, b_cproj, w_mlp1, b_mlp1_t, w_mlp2, b_mlp2, out):
    x1 = nc.dram_tensor("x1", (B, N, H), F32, kind="Internal").ap()
    qc = nc.dram_tensor("qc", (B, 2, H, N), F32, kind="Internal").ap()
    o_cross = nc.dram_tensor("o_cross", (B, H, N), F32, kind="Internal").ap()
    maxima = nc.dram_tensor("maxima", (2, 2, HPG, N), F32, kind="Internal").ap()
    gates = nc.dram_tensor("gates", (2, B, H), F32, kind="Internal").ap()
    with ExitStack() as ctx:
        sb, ps, sem = alloc(nc, ctx, "shared")
        ident = sb("ident", [P, P])
        select = sb("select", [HPG, P])
        neg_half, eps = sb("neg_half", [P, 8]), sb("eps", [P, 8])
        mod_t = sb("mod_t", [P, 4 * KC, B])
        constants_phase(nc, ident, select, neg_half, eps)
        self_phase(nc, x, cond_t, w_mod, b_mod, w_qkv, b_qkv_t, w_proj, b_proj, w_qc, b_qc_t, gates, x1, qc, mod_t, ident, select, neg_half, eps)
        cross_phase(nc, context, w_kvc, b_kvc_t, qc, maxima, o_cross, ident, neg_half, eps)
        mlp_phase(nc, x1, o_cross, b_kvc_t[:, KC:2 * KC], w_cproj, b_cproj, w_mlp1, b_mlp1_t, w_mlp2, b_mlp2, gates, out,
                  mod_t[:, 2 * KC:4 * KC], ident, neg_half, eps)


def kernel(x, cond_1024, ctx_1024, **weights):
    import numpy as np
    import concourse.bacc as bacc
    from concourse.bass_utils import run_bass_kernel_spmd

    w = {name.replace("L0_xcond_", ""): np.asarray(a) for name, a in weights.items()}

    def columns(v):
        return v.reshape(-1, P).T

    arrays = {
        "x": x, "context": ctx_1024, "cond_t": np.asarray(cond_1024).T.reshape(KC, P, B).transpose(1, 0, 2),
        "w_mod": w["W_mod"], "b_mod": w["b_mod"], "w_qkv": w["W_qkv"], "b_qkv_t": columns(w["b_qkv"]),
        "w_proj": w["W_proj"], "b_proj": w["b_proj"], "w_qc": w["W_qc"], "b_qc_t": columns(w["b_qc"]),
        "w_kvc": w["W_kvc"], "b_kvc_t": columns(w["b_kvc"]), "w_cproj": w["W_cproj"], "b_cproj": w["b_cproj"],
        "w_mlp1": w["W_mlp1"], "b_mlp1_t": columns(w["b_mlp1"]), "w_mlp2": w["W_mlp2"], "b_mlp2": w["b_mlp2"],
    }
    arrays = {f"in_{name}": np.ascontiguousarray(a) for name, a in arrays.items()}
    nc = bacc.Bacc("TRN2", target_bir_lowering=False, num_devices=1, dynamic_dma_scratch_size=4096)
    aps = {name[3:]: nc.dram_tensor(name, a.shape, F32, kind="ExternalInput").ap() for name, a in arrays.items()}
    out = nc.dram_tensor("out", (B, N, H), F32, kind="ExternalOutput").ap()
    build(nc, out=out, **aps)
    r = run_bass_kernel_spmd(nc, [arrays], core_ids=[0])
    return r.results[0]["out"]
```
